# Optimizing a Trainium2 kernel written in Bass

```python
import numpy as np
import jax
import jax.numpy as jnp

def _softmax(x, axis=-1):
    return jax.nn.softmax(x, axis=axis)

def _gelu(x):
    return jax.nn.gelu(x, approximate=True)

def _silu(x):
    return jax.nn.silu(x)

def _sigmoid(x):
    return jax.nn.sigmoid(x)

def _layernorm(x, axis=-1, eps=1e-05):
    m = jnp.mean(x, axis=axis, keepdims=True)
    v = jnp.var(x, axis=axis, keepdims=True)
    return (x - m) / jnp.sqrt(v + eps)

def _scatter_add(tgt, idx, src, axis=0):
    return tgt.at[idx].add(src)

def _segment_sum(src, seg, n):
    return jax.ops.segment_sum(src, seg, n)
kernel_name = 'mk_seq_postln_d2_jaxref_r8_d6425c'

def setup_inputs(seed: int=0):
    np.random.seed(seed)
    _w = jnp.asarray

    def _L0_attn_setup():
        import jax, jax.numpy as jnp
        import numpy as np
        N_HEADS = 16

        def _rotate_half(t):
            shp = t.shape
            t2 = t.reshape(*shp[:-1], shp[-1] // 2, 2)
            return jnp.stack((-t2[..., 1], t2[..., 0]), axis=-1).reshape(shp)
        key = jax.random.key(seed)
        k1, k2, k3 = jax.random.split(key, 3)
        B, N, D = (2, 256, 128)
        x = jax.random.normal(k1, (B, N, D), dtype=jnp.float32)
        w_qkv = jax.random.normal(k2, (D, 3 * D), dtype=jnp.float32) * D ** (-0.5)
        w_proj = jax.random.normal(k3, (D, D), dtype=jnp.float32) * D ** (-0.5)
        return {'x': x, 'w_qkv': w_qkv, 'w_proj': w_proj}
    _L0_attn_in = _L0_attn_setup()

    def _L0_ffn_setup():
        import jax, jax.numpy as jnp
        import numpy as np
        D_IN, D_HID = (128, 512)

        def _ternary(key, shape):
            return jax.random.randint(key, shape, -1, 2).astype(jnp.float32)

        def _tlin(x, w, s):
            return jnp.einsum('bsi,oi->bso', x, w) * s
        key = jax.random.key(seed)
        ks = jax.random.split(key, 12)
        inv = lambda fan: 1.0 / np.sqrt(fan).astype(np.float32)
        return {'x': jax.random.normal(ks[0], (4, 256, D_IN), dtype=jnp.float32), 'w1_w': _ternary(ks[1], (D_HID, D_IN)), 'w1_s': jax.random.uniform(ks[2], (D_HID,), dtype=jnp.float32) * inv(D_IN), 'w2_w': _ternary(ks[3], (D_HID, D_IN)), 'w2_s': jax.random.uniform(ks[4], (D_HID,), dtype=jnp.float32) * inv(D_IN), 'h1_w': _ternary(ks[5], (D_HID, D_HID)), 'h1_s': jax.random.uniform(ks[6], (D_HID,), dtype=jnp.float32) * inv(D_HID), 'h2_w': _ternary(ks[7], (D_HID, D_HID)), 'h2_s': jax.random.uniform(ks[8], (D_HID,), dtype=jnp.float32) * inv(D_HID), 'w3_w': _ternary(ks[9], (D_IN, D_HID)), 'w3_s': jax.random.uniform(ks[10], (D_IN,), dtype=jnp.float32) * inv(D_HID)}
    _L0_ffn_in = _L0_ffn_setup()

    def _L1_attn_setup():
        import jax, jax.numpy as jnp
        import numpy as np
        EMBED_DIM = 128
        NUM_HEADS = 16
        HEAD_DIM = EMBED_DIM // NUM_HEADS
        BATCH = 2
        SEQ = 256
        key = jax.random.key(seed)
        k1, k2, k3, k4, k5 = jax.random.split(key, 5)
        scale_in = 1.0 / np.sqrt(EMBED_DIM)
        return {'x': jax.random.normal(k1, (BATCH, SEQ, EMBED_DIM), dtype=jnp.float32), 'head_mask': jnp.ones((NUM_HEADS,), dtype=jnp.float32), 'qkv_w': jax.random.normal(k2, (3 * EMBED_DIM, EMBED_DIM), dtype=jnp.float32) * scale_in, 'qkv_b': jax.random.normal(k3, (3 * EMBED_DIM,), dtype=jnp.float32) * 0.02, 'fc_w': jax.random.normal(k4, (EMBED_DIM, EMBED_DIM), dtype=jnp.float32) * scale_in, 'fc_b': jax.random.normal(k5, (EMBED_DIM,), dtype=jnp.float32) * 0.02}
    _L1_attn_in = _L1_attn_setup()

    def _L1_ffn_setup():
        import jax, jax.numpy as jnp
        import numpy as np
        DIM = 128
        DEPTH = 2
        HEADS = 8
        DIM_HEAD = 64
        WINDOW = 64
        INNER = HEADS * DIM_HEAD
        HID = int(DIM * 4 * 2 / 3)
        B, N = (2, 1024)
        QK_SCALE = 8.0

        def shift_token(t):
            t1, t2 = jnp.split(t, 2, axis=-1)
            t2 = jnp.pad(t2, ((0, 0), (1, 0), (0, 0)))[:, :-1]
            return jnp.concatenate([t1, t2], axis=-1)

        def l2norm(t):
            return t / jnp.clip(jnp.linalg.norm(t, axis=-1, keepdims=True), 1e-12)

        def rotate_half(x):
            x1, x2 = jnp.split(x, 2, axis=-1)
            return jnp.concatenate([-x2, x1], axis=-1)

        def rotary_xpos(q, k):
            n = q.shape[-2]
            half_idx = jnp.arange(0, DIM_HEAD, 2, dtype=jnp.float32)
            inv_freq = 1.0 / 10000.0 ** (half_idx / DIM_HEAD)
            t = jnp.arange(n, dtype=jnp.float32)
            freqs = t[:, None] * inv_freq[None, :]
            freqs = jnp.concatenate([freqs, freqs], axis=-1)
            base = (half_idx + 0.4 * DIM_HEAD) / (1.4 * DIM_HEAD)
            power = (t - n // 2) / float(WINDOW // 2)
            scale = base[None, :] ** power[:, None]
            scale = jnp.concatenate([scale, scale], axis=-1)
            cos, sin = (jnp.cos(freqs), jnp.sin(freqs))
            q = q * cos * scale + rotate_half(q) * sin * scale
            k = k * cos / scale + rotate_half(k) * sin / scale
            return (q, k)

        def local_attention(q, k, v):
            b, h, n, d = q.shape
            w = n // WINDOW
            bq = q.reshape(b, h, w, WINDOW, d) * QK_SCALE
            bk = k.reshape(b, h, w, WINDOW, d)
            bv = v.reshape(b, h, w, WINDOW, d)

            def look_around(t):
                p = jnp.pad(t, ((0, 0), (0, 0), (1, 0), (0, 0), (0, 0)))
                return jnp.concatenate([p[:, :, :w], p[:, :, 1:]], axis=3)
            bk, bv = (look_around(bk), look_around(bv))
            bt = jnp.arange(n).reshape(w, WINDOW)
            btp = jnp.pad(bt, ((1, 0), (0, 0)), constant_values=-1)
            btk = jnp.concatenate([btp[:w], btp[1:]], axis=1)
            sim = jnp.einsum('bhwid,bhwjd->bhwij', bq, bk)
            i = bt[:, :, None]
            j = btk[:, None, :]
            mask = (i < j) | (i > j + WINDOW) | (j == -1)
            sim = jnp.where(mask, -jnp.finfo(sim.dtype).max, sim)
            attn = jax.nn.softmax(sim, axis=-1)
            out = jnp.einsum('bhwij,bhwjd->bhwid', attn, bv)
            return out.reshape(b, h, n, d)

        def _layer(x, wqkv, qs, ksc, wo, lg, lb, w1, b1, w2, b2):
            b, n, _ = x.shape
            h = shift_token(x)
            qkv = h @ wqkv
            q, k, v = jnp.split(qkv, 3, axis=-1)
            to_heads = lambda t: t.reshape(b, n, HEADS, DIM_HEAD).transpose(0, 2, 1, 3)
            q, k, v = (to_heads(q), to_heads(k), to_heads(v))
            q = l2norm(q) * qs
            k = l2norm(k) * ksc
            q, k = rotary_xpos(q, k)
            o = local_attention(q, k, v)
            o = o.transpose(0, 2, 1, 3).reshape(b, n, INNER)
            x = x + o @ wo
            h = shift_token(x)
            mu = h.mean(-1, keepdims=True)
            var = h.var(-1, keepdims=True)
            h = (h - mu) / jnp.sqrt(var + 1e-05) * lg + lb
            h = h @ w1 + b1
            a, g = jnp.split(h, 2, axis=-1)
            h = a * jax.nn.gelu(g, approximate=False)
            x = x + h @ w2 + b2
            return x
        key = jax.random.key(seed)
        ks = jax.random.split(key, 6)
        return {'x': jax.random.normal(ks[0], (B, N, DIM), jnp.float32), 'wqkv': jax.random.normal(ks[1], (DEPTH, DIM, 3 * INNER), jnp.float32) * 0.02, 'q_scale': jnp.ones((DEPTH, DIM_HEAD), jnp.float32), 'k_scale': jnp.ones((DEPTH, DIM_HEAD), jnp.float32), 'wo': jax.random.normal(ks[2], (DEPTH, INNER, DIM), jnp.float32) * 0.02, 'ln_g': jnp.ones((DEPTH, DIM), jnp.float32), 'ln_b': jnp.zeros((DEPTH, DIM), jnp.float32), 'w1': jax.random.normal(ks[3], (DEPTH, DIM, 2 * HID), jnp.float32) * 0.02, 'b1': jnp.zeros((DEPTH, 2 * HID), jnp.float32), 'w2': jax.random.normal(ks[4], (DEPTH, HID, DIM), jnp.float32) * 0.02, 'b2': jnp.zeros((DEPTH, DIM), jnp.float32)}
    _L1_ffn_in = _L1_ffn_setup()
    _d = {'L0_attn_x': _L0_attn_in['x'], 'L0_attn_w_qkv': _L0_attn_in['w_qkv'], 'L0_attn_w_proj': _L0_attn_in['w_proj'], 'L0_ffn_w1_w': _L0_ffn_in['w1_w'], 'L0_ffn_w1_s': _L0_ffn_in['w1_s'], 'L0_ffn_w2_w': _L0_ffn_in['w2_w'], 'L0_ffn_w2_s': _L0_ffn_in['w2_s'], 'L0_ffn_h1_w': _L0_ffn_in['h1_w'], 'L0_ffn_h1_s': _L0_ffn_in['h1_s'], 'L0_ffn_h2_w': _L0_ffn_in['h2_w'], 'L0_ffn_h2_s': _L0_ffn_in['h2_s'], 'L0_ffn_w3_w': _L0_ffn_in['w3_w'], 'L0_ffn_w3_s': _L0_ffn_in['w3_s'], 'L1_attn_head_mask': _L1_attn_in['head_mask'], 'L1_attn_qkv_w': _L1_attn_in['qkv_w'], 'L1_attn_qkv_b': _L1_attn_in['qkv_b'], 'L1_attn_fc_w': _L1_attn_in['fc_w'], 'L1_attn_fc_b': _L1_attn_in['fc_b'], 'L1_ffn_wqkv': _L1_ffn_in['wqkv'], 'L1_ffn_q_scale': _L1_ffn_in['q_scale'], 'L1_ffn_k_scale': _L1_ffn_in['k_scale'], 'L1_ffn_wo': _L1_ffn_in['wo'], 'L1_ffn_ln_g': _L1_ffn_in['ln_g'], 'L1_ffn_ln_b': _L1_ffn_in['ln_b'], 'L1_ffn_w1': _L1_ffn_in['w1'], 'L1_ffn_b1': _L1_ffn_in['b1'], 'L1_ffn_w2': _L1_ffn_in['w2'], 'L1_ffn_b2': _L1_ffn_in['b2']}
    _x0 = _d['L0_attn_x']
    _d['L0_attn_x'] = jax.random.normal(jax.random.fold_in(jax.random.key(seed), 1), (32, 256, 128), dtype=_x0.dtype)
    del _x0
    return _d

def reference(L0_attn_x, L0_attn_w_qkv, L0_attn_w_proj, L0_ffn_w1_w, L0_ffn_w1_s, L0_ffn_w2_w, L0_ffn_w2_s, L0_ffn_h1_w, L0_ffn_h1_s, L0_ffn_h2_w, L0_ffn_h2_s, L0_ffn_w3_w, L0_ffn_w3_s, L1_attn_head_mask, L1_attn_qkv_w, L1_attn_qkv_b, L1_attn_fc_w, L1_attn_fc_b, L1_ffn_wqkv, L1_ffn_q_scale, L1_ffn_k_scale, L1_ffn_wo, L1_ffn_ln_g, L1_ffn_ln_b, L1_ffn_w1, L1_ffn_b1, L1_ffn_w2, L1_ffn_b2):

    def _L0_attn_ref(x, w_qkv, w_proj):
        import jax, jax.numpy as jnp
        import numpy as np
        N_HEADS = 16

        def _rotate_half(t):
            shp = t.shape
            t2 = t.reshape(*shp[:-1], shp[-1] // 2, 2)
            return jnp.stack((-t2[..., 1], t2[..., 0]), axis=-1).reshape(shp)
        B, N, D = x.shape
        H = N_HEADS
        hd = D // H
        qkv = x @ w_qkv
        qkv = qkv.reshape(B, N, 3, H, hd).transpose(2, 0, 3, 1, 4)
        q, k, v = (qkv[0], qkv[1], qkv[2])
        inv_freq = 1.0 / 10000.0 ** (jnp.arange(0, hd, 2, dtype=jnp.float32) / hd)
        freqs = jnp.arange(N, dtype=jnp.float32)[:, None] * inv_freq[None, :]
        sin = jnp.repeat(jnp.sin(freqs), 2, axis=-1)[None, None]
        cos = jnp.repeat(jnp.cos(freqs), 2, axis=-1)[None, None]
        q = q * cos + _rotate_half(q) * sin
        k = k * cos + _rotate_half(k) * sin
        scale = hd ** (-0.5)
        attn = jax.nn.softmax(jnp.einsum('bhqd,bhkd->bhqk', q, k) * scale, axis=-1)
        out = jnp.einsum('bhqk,bhkd->bhqd', attn, v)
        out = out.transpose(0, 2, 1, 3).reshape(B, N, D)
        return out @ w_proj

    def _L0_ffn_ref(x, w1_w, w1_s, w2_w, w2_s, h1_w, h1_s, h2_w, h2_s, w3_w, w3_s):
        import jax, jax.numpy as jnp
        import numpy as np
        D_IN, D_HID = (128, 512)

        def _ternary(key, shape):
            return jax.random.randint(key, shape, -1, 2).astype(jnp.float32)

        def _tlin(x, w, s):
            return jnp.einsum('bsi,oi->bso', x, w) * s
        h = jax.nn.silu(_tlin(x, w1_w, w1_s)) * _tlin(x, w2_w, w2_s)
        h = jax.nn.gelu(_tlin(h, h1_w, h1_s), approximate=False)
        h = jax.nn.gelu(_tlin(h, h2_w, h2_s), approximate=False)
        return _tlin(h, w3_w, w3_s)

    def _L1_attn_ref(x, head_mask, qkv_w, qkv_b, fc_w, fc_b):
        import jax, jax.numpy as jnp
        import numpy as np
        EMBED_DIM = 128
        NUM_HEADS = 16
        HEAD_DIM = EMBED_DIM // NUM_HEADS
        BATCH = 2
        SEQ = 256
        N, S, D = x.shape
        H, hd = (NUM_HEADS, HEAD_DIM)
        qkv = jnp.einsum('nsd,ed->nse', x, qkv_w) + qkv_b
        qkv = qkv.reshape(N, S, H, 3, hd).transpose(3, 0, 2, 1, 4)
        q, k, v = (qkv[0], qkv[1], qkv[2])
        hm = head_mask.reshape(1, H, 1, 1)
        q = q * hm
        k = k * hm
        v = v * hm
        energy = jnp.einsum('nhqd,nhkd->nhqk', q, k)
        attention = jax.nn.softmax(energy / jnp.sqrt(jnp.float32(hd)), axis=-1)
        out = jnp.einsum('nhqk,nhkd->nhqd', attention, v)
        out = out.transpose(0, 2, 1, 3).reshape(N, S, H * hd)
        out = jnp.einsum('nsd,ed->nse', out, fc_w) + fc_b
        return out

    def _L1_ffn_ref(x, wqkv, q_scale, k_scale, wo, ln_g, ln_b, w1, b1, w2, b2):
        import jax, jax.numpy as jnp
        import numpy as np
        DIM = 128
        DEPTH = 2
        HEADS = 8
        DIM_HEAD = 64
        WINDOW = 64
        INNER = HEADS * DIM_HEAD
        HID = int(DIM * 4 * 2 / 3)
        B, N = (2, 1024)
        QK_SCALE = 8.0

        def shift_token(t):
            t1, t2 = jnp.split(t, 2, axis=-1)
            t2 = jnp.pad(t2, ((0, 0), (1, 0), (0, 0)))[:, :-1]
            return jnp.concatenate([t1, t2], axis=-1)

        def l2norm(t):
            return t / jnp.clip(jnp.linalg.norm(t, axis=-1, keepdims=True), 1e-12)

        def rotate_half(x):
            x1, x2 = jnp.split(x, 2, axis=-1)
            return jnp.concatenate([-x2, x1], axis=-1)

        def rotary_xpos(q, k):
            n = q.shape[-2]
            half_idx = jnp.arange(0, DIM_HEAD, 2, dtype=jnp.float32)
            inv_freq = 1.0 / 10000.0 ** (half_idx / DIM_HEAD)
            t = jnp.arange(n, dtype=jnp.float32)
            freqs = t[:, None] * inv_freq[None, :]
            freqs = jnp.concatenate([freqs, freqs], axis=-1)
            base = (half_idx + 0.4 * DIM_HEAD) / (1.4 * DIM_HEAD)
            power = (t - n // 2) / float(WINDOW // 2)
            scale = base[None, :] ** power[:, None]
            scale = jnp.concatenate([scale, scale], axis=-1)
            cos, sin = (jnp.cos(freqs), jnp.sin(freqs))
            q = q * cos * scale + rotate_half(q) * sin * scale
            k = k * cos / scale + rotate_half(k) * sin / scale
            return (q, k)

        def local_attention(q, k, v):
            b, h, n, d = q.shape
            w = n // WINDOW
            bq = q.reshape(b, h, w, WINDOW, d) * QK_SCALE
            bk = k.reshape(b, h, w, WINDOW, d)
            bv = v.reshape(b, h, w, WINDOW, d)

            def look_around(t):
                p = jnp.pad(t, ((0, 0), (0, 0), (1, 0), (0, 0), (0, 0)))
                return jnp.concatenate([p[:, :, :w], p[:, :, 1:]], axis=3)
            bk, bv = (look_around(bk), look_around(bv))
            bt = jnp.arange(n).reshape(w, WINDOW)
            btp = jnp.pad(bt, ((1, 0), (0, 0)), constant_values=-1)
            btk = jnp.concatenate([btp[:w], btp[1:]], axis=1)
            sim = jnp.einsum('bhwid,bhwjd->bhwij', bq, bk)
            i = bt[:, :, None]
            j = btk[:, None, :]
            mask = (i < j) | (i > j + WINDOW) | (j == -1)
            sim = jnp.where(mask, -jnp.finfo(sim.dtype).max, sim)
            attn = jax.nn.softmax(sim, axis=-1)
            out = jnp.einsum('bhwij,bhwjd->bhwid', attn, bv)
            return out.reshape(b, h, n, d)

        def _layer(x, wqkv, qs, ksc, wo, lg, lb, w1, b1, w2, b2):
            b, n, _ = x.shape
            h = shift_token(x)
            qkv = h @ wqkv
            q, k, v = jnp.split(qkv, 3, axis=-1)
            to_heads = lambda t: t.reshape(b, n, HEADS, DIM_HEAD).transpose(0, 2, 1, 3)
            q, k, v = (to_heads(q), to_heads(k), to_heads(v))
            q = l2norm(q) * qs
            k = l2norm(k) * ksc
            q, k = rotary_xpos(q, k)
            o = local_attention(q, k, v)
            o = o.transpose(0, 2, 1, 3).reshape(b, n, INNER)
            x = x + o @ wo
            h = shift_token(x)
            mu = h.mean(-1, keepdims=True)
            var = h.var(-1, keepdims=True)
            h = (h - mu) / jnp.sqrt(var + 1e-05) * lg + lb
            h = h @ w1 + b1
            a, g = jnp.split(h, 2, axis=-1)
            h = a * jax.nn.gelu(g, approximate=False)
            x = x + h @ w2 + b2
            return x
        for l in range(DEPTH):
            x = _layer(x, wqkv[l], q_scale[l], k_scale[l], wo[l], ln_g[l], ln_b[l], w1[l], b1[l], w2[l], b2[l])
        return x
    x = L0_attn_x
    x = _layernorm(x + _L0_attn_ref(x, L0_attn_w_qkv, L0_attn_w_proj), axis=-1)
    x = _layernorm(x + _L0_ffn_ref(x, L0_ffn_w1_w, L0_ffn_w1_s, L0_ffn_w2_w, L0_ffn_w2_s, L0_ffn_h1_w, L0_ffn_h1_s, L0_ffn_h2_w, L0_ffn_h2_s, L0_ffn_w3_w, L0_ffn_w3_s), axis=-1)
    x = _layernorm(x + _L1_attn_ref(x, L1_attn_head_mask, L1_attn_qkv_w, L1_attn_qkv_b, L1_attn_fc_w, L1_attn_fc_b), axis=-1)
    x = _layernorm(x + _L1_ffn_ref(x, L1_ffn_wqkv, L1_ffn_q_scale, L1_ffn_k_scale, L1_ffn_wo, L1_ffn_ln_g, L1_ffn_ln_b, L1_ffn_w1, L1_ffn_b1, L1_ffn_w2, L1_ffn_b2), axis=-1)
    return x

_drawn_inputs = setup_inputs


def setup_inputs(seed=0):
    import zlib

    import numpy as np

    out = dict(_drawn_inputs(seed))
    spreads = {'L1_ffn_q_scale': (1.0, 0.6),
     'L1_ffn_k_scale': (1.0, 0.6),
     'L1_ffn_ln_g': (1.0, 0.6),
     'L1_ffn_ln_b': (0.0, 0.8),
     'L1_ffn_b1': (0.0, 0.8),
     'L1_ffn_b2': (0.0, 0.599)}
    factors = {'L0_ffn_w1_w': 8.0,
     'L0_ffn_w1_s': 8.0,
     'L0_ffn_w2_w': 8.0,
     'L0_ffn_w2_s': 8.0,
     'L0_ffn_h1_w': 8.0,
     'L0_ffn_h1_s': 8.0,
     'L0_ffn_h2_w': 8.0,
     'L0_ffn_h2_s': 8.0,
     'L0_ffn_w3_w': 8.0,
     'L0_ffn_w3_s': 8.0,
     'L1_attn_qkv_b': 3.25,
     'L1_attn_fc_b': 2.815,
     'L1_ffn_wqkv': 3.052,
     'L1_ffn_wo': 3.07,
     'L1_ffn_w1': 6.621,
     'L1_ffn_w2': 6.485}
    for name, (base, spread) in spreads.items():
        noise = np.random.default_rng([zlib.crc32(name.encode()), seed]).standard_normal(out[name].shape)
        drawn = base * np.exp(spread * noise) if base else spread * noise
        out[name] = jnp.asarray(drawn.astype(out[name].dtype))
    for name, factor in factors.items():
        out[name] = (out[name] * factor).astype(out[name].dtype)
    return out
```

```python
import concourse.bass as bass
from concourse import mybir
from contextlib import ExitStack
import numpy as np

F32 = mybir.dt.float32
BF16 = mybir.dt.bfloat16
ALU = mybir.AluOpType
ACT = mybir.ActivationFunctionType
AX = mybir.AxisListType

P = 128
BATCH, SEQ, D = 32, 256, 128
TOKENS = BATCH * SEQ
LN_EPS = 1e-5


def phase_semaphores(nc, ctx):
    sems = []

    def clear():
        nc.clear_and_free_semaphores(sems)
        nc.all_engine_barrier()

    ctx.callback(clear)
    return sems


class Slot:

    def __init__(self, i, step, offset):
        self.i, self.step, self.offset = i, step, offset
        self.known = i is None
        self.n = offset if i is None else i * step + offset

    def fills(self, ahead, ring):
        times = (self.offset + ahead) // ring + 1
        return times if self.known else self.i * (self.step // ring) + times


def at_least(engine, sem, value):
    if isinstance(value, int) and value <= 0:
        return
    engine.wait_ge(sem, value)


HEADS, HD = 16, 8
UNITS = HEADS // 2
Q_PARTS = [0, 0, 0, 1, 1, 2]
K_PARTS = [0, 1, 2, 0, 1, 0]
STACKED = HD * len(Q_PARTS)
MAX_ROW = 96
ROWS_MAX, ROWS_PROB = MAX_ROW, MAX_ROW + 3
AHEAD = 3
RING = 4
STACK_DMAS = len(Q_PARTS) + len(K_PARTS)


def attention(nc, name, xT, out, consts, w, rotary, last):
    with ExitStack() as ctx:
        def sb(n, shape, dt=F32):
            return ctx.enter_context(nc.sbuf_tensor(f"{name}_{n}", shape, dt))

        def ps(n, shape, dt=F32):
            return ctx.enter_context(nc.psum_tensor(f"{name}_{n}", shape, dt))

        sems = phase_semaphores(nc, ctx)

        def sem(n):
            sems.append(nc.alloc_semaphore(f"{name}_{n}"))
            return sems[-1]

        ident, ident_bf = consts["ident"], consts["ident_bf"]

        wq, wk, wv, wo = (sb(n, [P, D]) for n in ("wq", "wk", "wv", "wo"))
        if rotary:
            wq_rot, wk_rot = sb("wq_rot", [P, D]), sb("wk_rot", [P, D])
            cos_sin = sb("cos_sin", [P, 2, SEQ])
        else:
            bias_mask = sb("bias_mask", [P, 3])
            v_bias, v_mask = sb("v_bias", [P, D]), sb("v_mask", [P, D])
            wo_bias, ones_row = sb("wo_bias", [1, D]), sb("ones_row", [1, P])

        x_proj = [sb(f"x_proj{i}", [P, SEQ]) for i in range(2)]
        x_res = [sb(f"x_res{i}", [P, SEQ]) for i in range(2)]
        qk_terms = sb("qk_terms", [P, 2, 2, SEQ])
        qk = sb("qk", [P, 2, SEQ])
        qk_rest = sb("qk_rest", [P, 2, SEQ])
        qk_part = sb("qk_part", [P, 3, 2, SEQ], BF16)
        q_stack = [sb(f"q_stack{i}", [P, HEADS, SEQ], BF16) for i in range(RING)]
        k_stack = [sb(f"k_stack{i}", [P, HEADS, SEQ], BF16) for i in range(RING)]
        v_ones = [sb(f"v_ones{i}", [P, 2, HEADS, 32]) for i in range(RING)]
        row_max = [sb(f"row_max{i}", [P, 2, HEADS]) for i in range(2)]
        max_rest = sb("max_rest", [P, 2, HEADS // 2])
        max_part = [sb(f"max_part{i}", [P, 2, 3, HEADS // 2], BF16) for i in range(2)]
        max_rows = [sb(f"max_rows{i}", [24, SEQ], BF16) for i in range(2)]
        prob = [sb(f"prob{i}", [P, 2, 2, SEQ]) for i in range(4)]
        pv_t = sb("pv_t", [P, 2, 8, 32])
        denom = sb("denom", [P, 2, 8, 1])
        heads_t = sb("heads_t", [P, 8, 32])
        o_sb = sb("o_sb", [P, SEQ])
        y_sb = sb("y_sb", [P, 2, D])
        stats, mean_var = sb("stats", [P, 2, 6]), sb("mean_var", [P, 2, 2])
        var_eps, rstd = sb("var_eps", [P, 2]), sb("rstd", [P, 2])
        z_sb = sb("z_sb", [P, 2, D])

        scores_q = [ps(f"scores_q{i}", [P, 2, SEQ]) for i in range(2)]
        scores_k = [ps(f"scores_k{i}", [P, 2, 2, SEQ]) for i in range(2)]
        pv = ps("pv", [P, 2, SEQ])
        misc = ps("misc", [P, 2 * SEQ])
        misc_bf = misc[:, :].bitcast(BF16)

        w_in, consts_made, stacks_clear, weights_made = (
            sem("w_in"), sem("consts_made"), sem("stacks_clear"), sem("weights_made"))
        x_proj_in = [sem(f"x_proj_in{i}") for i in range(2)]
        x_res_in = [sem(f"x_res_in{i}") for i in range(2)]
        stack_in = [sem(f"stack_in{i}") for i in range(RING)]
        max_in = [sem(f"max_in{i}") for i in range(2)]
        stored = [sem(f"stored{i}") for i in range(2)]
        qk_done, v_done, sq_done, sk_done, pv_done, maxt_done, y_done, zt_done = (
            sem(n) for n in ("qk_done", "v_done", "sq_done", "sk_done", "pv_done", "maxt_done", "y_done", "zt_done"))
        qk_taken, max_found, pv_turned, inverted, scaled, o_ready, bn_done, mv_done, z_ready = (
            sem(n) for n in ("qk_taken", "max_found", "pv_turned", "inverted", "scaled", "o_ready", "bn_done", "mv_done", "z_ready"))
        ln_step = sem("ln_step")
        exp_done, part1, part2, v_ready, maxt_taken, y_taken, x_written = (
            sem(n) for n in ("exp_done", "part1", "part2", "v_ready", "maxt_taken", "y_taken", "x_written"))
        added, rest_done, part3, max_step, max_split, eps_added, rstd_done = (
            sem(n) for n in ("added", "rest_done", "part3", "max_step", "max_split", "eps_added", "rstd_done"))

        def active(s):
            if not s.known:
                return True, True, True, True
            return tuple(0 <= s.n + ahead < BATCH for ahead in (AHEAD, 1, 0, -1))

        def slots(engine, body):
            for n in range(-AHEAD, RING + 1):
                body(Slot(None, RING, n))
            with engine.Fori(0, (BATCH - 2 * RING) // RING) as i:
                for offset in range(RING + 1, 2 * RING + 1):
                    body(Slot(i, RING, offset))
            for n in range(BATCH - RING + 1, BATCH + 1):
                body(Slot(None, RING, n))

        n_weights = 5 if rotary else 10
        block = ctx.enter_context(nc.Block())

        @block.sync
        def _(sp):
            for dst, src in ((wq, w["wq"]), (wk, w["wk"]), (wv, w["wv"]), (wo, w["wo"])):
                sp.dma_start(dst[:, :], src).then_inc(w_in, 16)
            if rotary:
                sp.dma_start(cos_sin[:, :, :], w["cos_sin"]).then_inc(w_in, 16)
            else:
                for c, b in enumerate(("bq", "bk", "mask")):
                    sp.dma_start(bias_mask[:, c:c + 1], w[b]).then_inc(w_in, 16)
                sp.dma_start(v_bias[:, :], w["bv"].to_broadcast([P, D])).then_inc(w_in, 16)
                sp.dma_start(v_mask[:, :], w["mask_v"].to_broadcast([P, D])).then_inc(w_in, 16)
                sp.dma_start(wo_bias[:, :], w["bo"]).then_inc(w_in, 16)
            sp.wait_ge(stacks_clear, 1)

            def slot(s):
                n, j = s.n, s.offset % RING
                a, b1, b3, c = active(s)
                def value(v):
                    return v if s.known else sp.snap(v)

                x_ahead, x_now, x_before = value(n * SEQ + AHEAD * SEQ), value(n * SEQ), value(n * SEQ - SEQ)
                v_read, y_read, z_made = value(n + AHEAD - 1), value(n - 1), value(2 * n)
                max_taken_n, max_taken_next = value(2 * n + 2), value(2 * n + 3)
                parts_made = value(n + AHEAD + 1)
                if a:
                    at_least(sp, v_done, v_read)
                    sp.dma_start(x_proj[(j + AHEAD) % 2][:, :],
                                 xT[:, bass.ds(x_ahead, SEQ)]).then_inc(x_proj_in[(j + AHEAD) % 2], 16)
                if b3:
                    at_least(sp, y_done, y_read)
                    sp.dma_start(x_res[j % 2][:, :], xT[:, bass.ds(x_now, SEQ)]).then_inc(x_res_in[j % 2], 16)
                    sp.wait_ge(maxt_taken, max_taken_n)
                    sp.dma_start(q_stack[j][MAX_ROW:MAX_ROW + 3, 8:16, :], max_rows[1][:, :]).then_inc(max_in[1], 16)
                if a:
                    sp.wait_ge(part1, parts_made)
                    stack_part(j, 0)
                if b1:
                    sp.wait_ge(maxt_taken, max_taken_next)
                    sp.dma_start(q_stack[(j + 1) % RING][MAX_ROW:MAX_ROW + 3, 0:8, :],
                                 max_rows[0][:, :]).then_inc(max_in[0], 16)
                if a:
                    sp.wait_ge(part2, parts_made)
                    stack_part(j, 1)
                    sp.wait_ge(part3, parts_made)
                    stack_part(j, 2)
                if c and last:
                    sp.wait_ge(z_ready, z_made)
                    sp.dma_start(out[bass.ds(x_before, SEQ), :].rearrange("(t p) d -> p t d", p=P),
                                 z_sb[:, :, :]).then_inc(stored[0], 16)

            def stack_part(j, part):
                ja = (j + AHEAD) % RING
                for which, stack, order in ((0, q_stack[ja], Q_PARTS), (1, k_stack[ja], K_PARTS)):
                    for row, p in enumerate(order):
                        if p == part:
                            sp.dma_start(stack[HD * row:HD * (row + 1), :, :],
                                         qk_part[:, part, which, :]).then_inc(stack_in[ja], 16)

            slots(sp, slot)
            if last:
                sp.wait_ge(stored[0], 16 * BATCH)

        @block.tensor
        def _(pe):
            pe.wait_ge(weights_made, 1)
            pe.wait_ge(stacks_clear, 1)

            def misc_free(s, a, b1, b3, c, use):
                n = s.n
                order = [("maxt1", b3, maxt_taken, 2 * n + 2), ("q", a, qk_taken, 2 * (n + AHEAD) + 1),
                         ("k", a, qk_taken, 2 * (n + AHEAD) + 2), ("y", c, y_taken, n),
                         ("v", a, v_ready, n + AHEAD + 1), ("maxt0", b1, maxt_taken, 2 * (n + 1) + 1)]
                if not last:
                    order.append(("zt", c, x_written, n))
                k = [o[0] for o in order].index(use)
                for o in reversed(order[:k]):
                    if o[1]:
                        return at_least(pe, o[2], o[3])
                at_least(pe, maxt_taken, 2 * n + 1 if b3 else 0)
                a0, _, b30, c0 = active(Slot(s.i, RING, s.offset - 1))
                if a0:
                    at_least(pe, v_ready, n + AHEAD)
                if c0:
                    at_least(pe, y_taken, n - 1)
                    if not last:
                        at_least(pe, x_written, n - 1)
                elif b30:
                    at_least(pe, maxt_taken, 2 * n)

            def weigh_v(n, j, g):
                pe.wait_ge(exp_done, UNITS * n + 2 * g + 2)
                if g == 0:
                    at_least(pe, v_ready, n + 1)
                if g % 2 == 0:
                    at_least(pe, pv_turned, 2 * n + g // 2)
                for kt in range(2):
                    for r in range(4):
                        h = 4 * g + r
                        mm = nc.tensor.matmul(pv[32 * r:32 * r + 32, g % 2, :], v_ones[j][:, kt, h, :],
                                              prob[(2 * g + r // 2) % 4][:, r % 2, kt, :],
                                              start=(kt == 0), stop=(kt == 1))
                mm.then_inc(pv_done, 1)

            def project(x, first, rot):
                mm = nc.tensor.matmul(misc[:, 0:SEQ], first[:, :], x, start=True, stop=True)
                if rot is not None:
                    mm = nc.tensor.matmul(misc[:, SEQ:2 * SEQ], rot[:, :], x, start=True, stop=True)
                mm.then_inc(qk_done, 1)

            def slot(s):
                n, j = s.n, s.offset % RING
                a, b1, b3, c = active(s)
                ja, jb = (j + AHEAD) % RING, (j + 1) % RING
                for u in range(UNITS):
                    if b1:
                        if u == 0:
                            at_least(pe, stack_in[jb], 16 * STACK_DMAS * s.fills(1, RING))
                        for qt in range(2):
                            at_least(pe, max_found, 2 * UNITS * (n + 1) + 2 * u + qt - 1)
                            for e in range(2):
                                h = 2 * u + e
                                mm = nc.tensor.matmul(scores_q[qt][:, e, :],
                                                      q_stack[jb][0:ROWS_MAX, h, P * qt:P * qt + P],
                                                      k_stack[jb][0:ROWS_MAX, h, :], start=True, stop=True)
                            mm.then_inc(sq_done, 1)
                    if b3:
                        if u % 4 == 0:
                            pe.wait_ge(max_in[u // 4], 16 * (n + 1))
                        at_least(pe, exp_done, UNITS * n + u - 1)
                        for e in range(2):
                            for kt in range(2):
                                h = 2 * u + e
                                mm = nc.tensor.matmul(scores_k[u % 2][:, e, kt, :],
                                                      k_stack[j][0:ROWS_PROB, h, P * kt:P * kt + P],
                                                      q_stack[j][0:ROWS_PROB, h, :], start=True, stop=True)
                        mm.then_inc(sk_done, 1)
                    if u == 0 and c:
                        weigh_v(n - 1, (j - 1) % RING, 3)
                    if u in (2, 4, 6) and b3:
                        weigh_v(n, j, u // 2 - 1)
                    if u == 0 and b3:
                        turn_max(s, a, b1, b3, c, 1, n)
                    if u == 1 and a:
                        pe.wait_ge(x_proj_in[ja % 2], 16 * s.fills(AHEAD, 2))
                        misc_free(s, a, b1, b3, c, "q")
                        project(x_proj[ja % 2][:, :], wq, wq_rot if rotary else None)
                    if u == 2 and a:
                        misc_free(s, a, b1, b3, c, "k")
                        project(x_proj[ja % 2][:, :], wk, wk_rot if rotary else None)
                    if u == 3 and c:
                        misc_free(s, a, b1, b3, c, "y")
                        pe.wait_ge(o_ready, n)
                        jr = (j - 1) % 2
                        pe.wait_ge(x_res_in[jr], 16 * s.fills(-1, 2))
                        for t in range(2):
                            ts, y = slice(P * t, P * t + P), misc[:, D * t:D * t + D]
                            nc.tensor.matmul(y, o_sb[:, ts], wo[:, :], start=True, stop=False)
                            if not rotary:
                                nc.tensor.matmul(y, ones_row[:, :], wo_bias[:, :], start=False, stop=False)
                            mm = nc.tensor.matmul(y, x_res[jr][:, ts], ident[:, :], start=False, stop=True)
                        mm.then_inc(y_done, 1)
                    if u == 4 and a:
                        misc_free(s, a, b1, b3, c, "v")
                        for kt in range(2):
                            mm = nc.tensor.matmul(misc[:, D * kt:D * kt + D], x_proj[ja % 2][:, P * kt:P * kt + P],
                                                  wv[:, :], start=True, stop=True)
                        mm.then_inc(v_done, 1)
                    if u == 5 and b1:
                        turn_max(s, a, b1, b3, c, 0, n + 1)
                    if u == 7 and c and not last:
                        misc_free(s, a, b1, b3, c, "zt")
                        pe.wait_ge(z_ready, 2 * n)
                        for t in range(2):
                            mm = nc.tensor.transpose(misc[:, P * t:P * t + P], z_sb[:, t, :], ident[:, :])
                        mm.then_inc(zt_done, 1)

            def turn_max(s, a, b1, b3, c, half, batch):
                misc_free(s, a, b1, b3, c, f"maxt{half}")
                pe.wait_ge(max_split, 2 * batch + half + 1)
                for qt in range(2):
                    mm = nc.tensor.transpose(misc_bf[0:24, P * qt:P * qt + P],
                                             max_part[half][:, qt, :, :].rearrange("p a h -> p (a h)"), ident_bf[:, :])
                mm.then_inc(maxt_done, 1)

            slots(pe, slot)

        @block.vector
        def _(dve):
            def made(ins, value):
                ins.then_inc(consts_made, 1)
                dve.wait_ge(consts_made, value)

            dve.wait_ge(w_in, 16 * n_weights)
            if rotary:
                for w_plain, w_rot in ((wq, wq_rot), (wk, wk_rot)):
                    plain = w_plain[:, :].rearrange("p (i e h) -> p i e h", e=2, h=HEADS)
                    rot = w_rot[:, :].rearrange("p (i e h) -> p i e h", e=2, h=HEADS)
                    nc.vector.tensor_scalar(rot[:, :, 0, :], plain[:, :, 1, :], -1.0, None, ALU.mult).then_inc(consts_made, 1)
                    nc.vector.tensor_copy(rot[:, :, 1, :], plain[:, :, 0, :]).then_inc(consts_made, 1)
            else:
                nc.vector.tensor_tensor(wv[:, :], wv[:, :], v_mask[:, :], ALU.mult).then_inc(consts_made, 1)
                nc.vector.tensor_tensor(v_bias[:, :], v_bias[:, :], v_mask[:, :], ALU.mult).then_inc(consts_made, 1)
                nc.vector.memset(ones_row[:, :], 1.0).then_inc(consts_made, 1)
            for v in v_ones:
                nc.vector.memset(v[:, :, :, :], 0.0).then_inc(consts_made, 1)
            n0 = (4 if rotary else 3) + RING
            dve.wait_ge(consts_made, n0)
            for v in v_ones:
                nc.vector.memset(v[:, :, :, HD:HD + 1], 1.0).then_inc(consts_made, 1)
            dve.wait_ge(consts_made, n0 + RING)
            nc.vector.memset(heads_t[:, :, :], 0.0).then_inc(weights_made, 1)
            for s in (*q_stack, *k_stack):
                for q in range(32, MAX_ROW, 32):
                    nc.vector.memset(s[q:q + 32, :, :], 0.0).then_inc(consts_made, 1)
            for s in k_stack:
                nc.vector.memset(s[MAX_ROW:MAX_ROW + 3, :, :], -1.0).then_inc(consts_made, 1)
            dve.wait_ge(consts_made, n0 + RING + 5 * RING)
            nc.vector.memset(stats[:, :, :], 0.0).then_inc(stacks_clear, 1)

            def normalise_heads(m, half):
                at_least(dve, scaled, 2 * m + half)
                dve.wait_ge(pv_done, 4 * m + 2 * half + 2)
                nc.vector.transpose(pv_t[:, :, :, :].rearrange("p g c x -> p (g c x)"),
                                    pv[:, :, :].rearrange("p g q -> p (g q)")).then_inc(pv_turned, 1)
                dve.wait_ge(pv_turned, 2 * m + half + 1)
                nc.vector.reciprocal(denom[:, :, :, :], pv_t[:, :, :, HD:HD + 1]).then_inc(inverted, 1)
                dve.wait_ge(inverted, 2 * m + half + 1)
                dst = heads_t[:, :, :].rearrange("p c (g d) -> p g c d", d=HD)
                nc.vector.tensor_tensor(dst[:, 2 * half:2 * half + 2, :, :], pv_t[:, :, :, 0:HD],
                                        denom[:, :, :, :].to_broadcast([P, 2, 8, HD]), ALU.mult).then_inc(scaled, 1)
                if half == 1:
                    dve.wait_ge(scaled, 2 * m + 2)
                    at_least(dve, y_done, m)
                    nc.vector.transpose(o_sb[:, :], heads_t[:, :, :].rearrange("p c x -> p (c x)")).then_inc(o_ready, 1)

            def take_qk(n, which):
                dve.wait_ge(qk_done, 2 * (n + AHEAD) + 1 + which)
                if rotary:
                    at_least(dve, added, n + AHEAD)
                    nc.vector.tensor_tensor(qk_terms[:, which, :, :], misc[:, :].rearrange("p (e t) -> p e t", e=2),
                                            cos_sin[:, :, :], ALU.mult).then_inc(qk_taken, 1)
                else:
                    at_least(dve, part1, n + AHEAD)
                    at_least(dve, rest_done, n + AHEAD)
                    nc.vector.tensor_scalar(qk[:, which, :], misc[:, 0:SEQ], bias_mask[:, which:which + 1],
                                            bias_mask[:, 2:3], ALU.add, ALU.mult).then_inc(qk_taken, 1)

            def slot(s):
                n, j = s.n, s.offset % RING
                a, b1, b3, c = active(s)
                jb = (j + 1) % RING
                for u in range(UNITS):
                    if b1:
                        for qt in range(2):
                            if u == 0 and qt == 0:
                                at_least(dve, max_split, 2 * n)
                            dve.wait_ge(sq_done, 2 * UNITS * (n + 1) + 2 * u + qt + 1)
                            nc.vector.tensor_reduce(row_max[jb % 2][:, qt, 2 * u:2 * u + 2], scores_q[qt][:, :, :],
                                                    AX.X, ALU.max).then_inc(max_found, 1)
                    if u == 1 and a:
                        take_qk(n, 0)
                    if u == 1 and c:
                        normalise_heads(n - 1, 1)
                    if u == 2 and a:
                        take_qk(n, 1)
                    if u == 4 and c:
                        dve.wait_ge(y_taken, n)
                        for t in range(2):
                            nc.vector.bn_stats(stats[:, t, :], y_sb[:, t, :]).then_inc(bn_done, 1)
                        dve.wait_ge(bn_done, 2 * n)
                        at_least(dve, rstd_done, n - 1)
                        dve.sem_inc(ln_step, 1)
                        for t in range(2):
                            nc.vector.bn_aggr(mean_var[:, t, :], stats[:, t, :]).then_inc(mv_done, 1)
                    if u == 4 and a and not rotary:
                        ja = (j + AHEAD) % RING
                        dve.wait_ge(v_done, n + AHEAD + 1)
                        at_least(dve, pv_done, 4 * n)
                        nc.vector.tensor_tensor(v_ones[ja][:, :, :, 0:HD],
                                                misc[:, 0:2 * D].rearrange("p (k h d) -> p k h d", k=2, d=HD),
                                                v_bias[:, :].rearrange("p (k h d) -> p k h d", k=1, d=HD)
                                                .to_broadcast([P, 2, HEADS, HD]), ALU.add).then_inc(v_ready, 1)
                    if u == 5 and b3:
                        normalise_heads(n, 0)
                    if u == 6 and c:
                        dve.wait_ge(rstd_done, n)
                        if last:
                            at_least(dve, stored[0], 16 * (n - 1))
                        else:
                            at_least(dve, zt_done, n - 1)
                        for t in range(2):
                            nc.vector.tensor_scalar(z_sb[:, t, :], y_sb[:, t, :], mean_var[:, t, 0:1],
                                                    rstd[:, t:t + 1], ALU.subtract, ALU.mult).then_inc(z_ready, 1)

            slots(dve, slot)

        @block.scalar
        def _(act):
            act.wait_ge(weights_made, 1)

            def slot(s):
                n, j = s.n, s.offset % RING
                a, b1, b3, c = active(s)
                for u in range(UNITS):
                    if b3:
                        act.wait_ge(sk_done, UNITS * n + u + 1)
                        at_least(act, pv_done, 4 * n + u // 2 - 1)
                        nc.scalar.activation(prob[u % 4][:, :, :, :], scores_k[u % 2][:, :, :, :], ACT.Exp,
                                             scale=float(HD) ** -0.5).then_inc(exp_done, 1)
                    if u == 0 and b3:
                        take_max(n, 1)
                    if u == 3 and c:
                        act.wait_ge(y_done, n)
                        at_least(act, z_ready, 2 * (n - 1))
                        nc.scalar.copy(y_sb[:, :, :], misc[:, 0:2 * D].rearrange("p (t d) -> p t d", t=2)).then_inc(y_taken, 1)
                    if u == 3 and a:
                        act.wait_ge(added if rotary else qk_taken, (n + AHEAD + 1) * (1 if rotary else 2))
                        if not s.known or n + AHEAD > 0:
                            act.wait_ge(stack_in[(j + AHEAD - 1) % RING], 16 * STACK_DMAS * s.fills(AHEAD - 1, RING))
                        nc.scalar.copy(qk_part[:, 0, :, :], qk[:, :, :]).then_inc(part1, 1)
                    if u == 4 and a and rotary:
                        ja = (j + AHEAD) % RING
                        act.wait_ge(v_done, n + AHEAD + 1)
                        at_least(act, pv_done, 4 * n)
                        nc.scalar.copy(v_ones[ja][:, :, :, 0:HD],
                                       misc[:, 0:2 * D].rearrange("p (k h d) -> p k h d", k=2, d=HD)).then_inc(v_ready, 1)
                    if u == 5 and a:
                        act.wait_ge(rest_done, n + AHEAD + 1)
                        nc.scalar.copy(qk_part[:, 1, :, :], qk_rest[:, :, :]).then_inc(part2, 1)
                    if u == 6 and b1:
                        take_max(n + 1, 0)
                    if u == 7 and c and not last:
                        act.wait_ge(zt_done, n)
                        nc.scalar.copy(xT[:, bass.ds((n - 1) * SEQ, SEQ)], misc[:, 0:SEQ]).then_inc(x_written, 1)

            def take_max(batch, half):
                act.wait_ge(maxt_done, 2 * batch + half + 1)
                at_least(act, max_in[half], 16 * batch)
                nc.scalar.copy(max_rows[half][:, :], misc_bf[0:24, 0:SEQ]).then_inc(maxt_taken, 1)

            slots(act, slot)

        @block.gpsimd
        def _(pool):
            pool.wait_ge(weights_made, 1)
            zeros = consts["zeros"][:, 0:HEADS].rearrange("p (a b) -> p a b", a=2)

            def split_max(batch, j, half):
                hs = slice(8 * half, 8 * half + 8)
                m, part = row_max[j % 2], max_part[half]
                pool.wait_ge(max_found, 2 * UNITS * batch + 8 * half + 8)
                at_least(pool, maxt_done, 2 * (batch - 1) + half + 1)
                steps = 3 * (2 * batch + half)
                nc.gpsimd.tensor_tensor(part[:, :, 0, :], m[:, :, hs], zeros, ALU.add).then_inc(max_step, 1)
                pool.wait_ge(max_step, steps + 1)
                nc.gpsimd.tensor_tensor(max_rest[:, :, :], m[:, :, hs], part[:, :, 0, :], ALU.subtract).then_inc(max_step, 1)
                pool.wait_ge(max_step, steps + 2)
                nc.gpsimd.tensor_tensor(part[:, :, 1, :], max_rest[:, :, :], zeros, ALU.add).then_inc(max_step, 1)
                pool.wait_ge(max_step, steps + 3)
                nc.gpsimd.tensor_tensor(part[:, :, 2, :], max_rest[:, :, :], part[:, :, 1, :],
                                        ALU.subtract).then_inc(max_split, 1)

            def slot(s):
                n, j = s.n, s.offset % RING
                a, b1, b3, c = active(s)
                if b3:
                    split_max(n, j, 1)
                if a:
                    if rotary:
                        pool.wait_ge(qk_taken, 2 * (n + AHEAD) + 2)
                        at_least(pool, part1, n + AHEAD)
                        nc.gpsimd.tensor_tensor(qk[:, :, :], qk_terms[:, :, 0, :], qk_terms[:, :, 1, :],
                                                ALU.add).then_inc(added, 1)
                        pool.wait_ge(added, n + AHEAD + 1)
                    pool.wait_ge(part1, n + AHEAD + 1)
                    at_least(pool, part2, n + AHEAD)
                    nc.gpsimd.tensor_tensor(qk_rest[:, :, :], qk[:, :, :], qk_part[:, 0, :, :],
                                            ALU.subtract).then_inc(rest_done, 1)
                if b1:
                    split_max(n + 1, j + 1, 0)
                if c:
                    pool.wait_ge(mv_done, 2 * n)
                    at_least(pool, z_ready, 2 * (n - 1))
                    nc.gpsimd.tensor_tensor(var_eps[:, :], mean_var[:, :, 1], consts["eps"][:, 0:2], ALU.add).then_inc(eps_added, 1)
                    pool.wait_ge(eps_added, n)
                    nc.gpsimd.tensor_tensor(rstd[:, :], var_eps[:, :], consts["minus_half"][:, 0:2], ALU.pow).then_inc(rstd_done, 1)
                if a:
                    pool.wait_ge(part2, n + AHEAD + 1)
                    nc.gpsimd.tensor_tensor(qk_part[:, 2, :, :], qk_rest[:, :, :], qk_part[:, 1, :, :],
                                            ALU.subtract).then_inc(part3, 1)

            slots(pool, slot)



CHUNK = 512
CHUNKS = TOKENS // CHUNK
CT = CHUNK // P
HID = 512
HB = HID // P


class Normaliser:

    def __init__(self, name, sb, sem, consts, tiles):
        self.tiles, self.consts = tiles, consts
        self.stats, self.mean_var = sb("stats", [P, tiles, 6]), sb("mean_var", [P, tiles, 2])
        self.var_eps, self.rstd = sb("var_eps", [P, tiles]), sb("rstd", [P, tiles])
        self.z = sb("z", [P, tiles, D])
        self.bn_done, self.mv_done, self.ln_step, self.eps_added, self.rstd_done, self.z_ready = (
            sem(n) for n in ("bn_done", "mv_done", "ln_step", "eps_added", "rstd_done", "z_ready"))


def ffn(nc, name, xT, out, consts, w, last):
    with ExitStack() as ctx:
        def sb(n, shape, dt=F32):
            return ctx.enter_context(nc.sbuf_tensor(f"{name}_{n}", shape, dt))

        def ps(n, shape, dt=F32):
            return ctx.enter_context(nc.psum_tensor(f"{name}_{n}", shape, dt))

        sems = phase_semaphores(nc, ctx)

        def sem(n):
            sems.append(nc.alloc_semaphore(f"{name}_{n}"))
            return sems[-1]

        ident = consts["ident"]
        w1, w2 = sb("w1", [P, HID]), sb("w2", [P, HID])
        h1, h2 = sb("h1", [P, HB, HID]), sb("h2", [P, HB, HID])
        w3, s3 = sb("w3", [P, HB, D]), sb("s3", [P, D])
        scales = sb("scales", [P, 4, HB])
        s1_half, s12_half = sb("s1_half", [P, HB]), sb("s12_half", [P, HB])

        x_up = sb("x_up", [P, CHUNK])
        x_res = sb("x_res", [P, CHUNK])
        tanh = [sb(f"tanh{i}", [P, CHUNK]) for i in range(2)]
        gated = [sb(f"gated{i}", [P, CHUNK]) for i in range(2)]
        hid0, hid1, hid2 = (sb(f"hid{i}", [P, HB, CHUNK]) for i in range(3))
        y_sb = sb("y_sb", [P, CT, D])
        ln = Normaliser(name, sb, sem, consts, CT)

        ps1 = [ps(f"ps1_{i}", [P, CHUNK]) for i in range(2)]
        ps2 = [ps(f"ps2_{i}", [P, CHUNK]) for i in range(2)]
        psh = [ps(f"psh_{i}", [P, CHUNK]) for i in range(2)]
        psy, psz = ps("psy", [P, CT, D]), ps("psz", [P, CHUNK])

        w_in, x_up_in, x_res_in, stored = (sem(n) for n in ("w_in", "x_up_in", "x_res_in", "stored"))
        up_done, hid_done, y_done, zt_done = (sem(n) for n in ("up_done", "hid_done", "y_done", "zt_done"))
        scales_made, gate_done, hid0_ready = (sem(n) for n in ("scales_made", "gate_done", "hid0_ready"))
        tanh_done, gelu_done, y_taken, x_written = (sem(n) for n in ("tanh_done", "gelu_done", "y_taken", "x_written"))

        def active(s):
            if not s.known:
                return True, True, True
            return tuple(0 <= s.n + ahead < CHUNKS for ahead in (1, 0, -1))

        def slots(engine, body):
            for n in (-1, 0, 1):
                body(Slot(None, 1, n))
            with engine.Fori(0, CHUNKS - 3) as i:
                body(Slot(i, 1, 2))
            for n in (CHUNKS - 1, CHUNKS):
                body(Slot(None, 1, n))

        block = ctx.enter_context(nc.Block())

        @block.sync
        def _(sp):
            loads = [(w1[:, :], w["w1"]), (w2[:, :], w["w2"]), (w3[:, :, :], w["w3"].rearrange("(b p) n -> p b n", p=P)),
                     (h1[:, :, :], w["h1"].rearrange("(b p) n -> p b n", p=P)),
                     (h2[:, :, :], w["h2"].rearrange("(b p) n -> p b n", p=P)),
                     (scales[:, :, :], w["scales"]), (s3[:, :], w["s3"].to_broadcast([P, D]))]
            for dst, src in loads:
                sp.dma_start(dst, src).then_inc(w_in, 16)

            def slot(s):
                n = s.n
                up, mid, end = active(s)

                def value(v):
                    return v if s.known else sp.snap(v)

                at_up, at_res, at_out = value(n * CHUNK + CHUNK), value(n * CHUNK - CHUNK), value(n * CHUNK - CHUNK)
                up_read, y_read, z_made = value(2 * HB * n + 2 * HB), value(n - 1), value(CT * n)
                if up:
                    at_least(sp, up_done, up_read)
                    sp.dma_start(x_up[:, :], xT[:, bass.ds(at_up, CHUNK)]).then_inc(x_up_in, 16)
                if end:
                    at_least(sp, y_done, y_read)
                    sp.dma_start(x_res[:, :], xT[:, bass.ds(at_res, CHUNK)]).then_inc(x_res_in, 16)
                    if last:
                        sp.wait_ge(ln.z_ready, z_made)
                        sp.dma_start(out[bass.ds(at_out, CHUNK), :].rearrange("(t p) d -> p t d", p=P),
                                     ln.z[:, :, :]).then_inc(stored, 16)

            slots(sp, slot)
            if last:
                sp.wait_ge(stored, 16 * CHUNKS)

        @block.tensor
        def _(pe):
            pe.wait_ge(w_in, 16 * 7)
            pe.wait_ge(scales_made, 3 + HB)

            def layer(n, weights, source, first):
                for m in range(HB):
                    at_least(pe, gelu_done, first + m - 1)
                    for k in range(HB):
                        mm = nc.tensor.matmul(psh[m % 2][:, :], weights[:, k, P * m:P * m + P], source[:, k, :],
                                              start=(k == 0), stop=(k == HB - 1))
                    mm.then_inc(hid_done, 1)

            def slot(s):
                n = s.n
                up, mid, end = active(s)
                if mid:
                    pe.wait_ge(hid0_ready, HB * (n + 1))
                    layer(n, h1, hid0, 2 * HB * n)
                if end:
                    pe.wait_ge(gelu_done, 2 * HB * n)
                    at_least(pe, y_taken, n - 1)
                    pe.wait_ge(x_res_in, 16 * n)
                    for t in range(CT):
                        for k in range(HB):
                            nc.tensor.matmul(psy[:, t, :], hid2[:, k, P * t:P * t + P], w3[:, k, :],
                                             start=(k == 0), stop=False)
                        mm = nc.tensor.matmul(psy[:, t, :], x_res[:, P * t:P * t + P], ident[:, :], start=False, stop=True)
                    mm.then_inc(y_done, 1)
                if up:
                    pe.wait_ge(x_up_in, 16 * (n + 2))
                    for m in range(HB):
                        at_least(pe, hid0_ready, HB * (n + 1) + m - 1)
                        for bank, weights in ((ps1[m % 2], w1), (ps2[m % 2], w2)):
                            nc.tensor.matmul(bank[:, :], weights[:, P * m:P * m + P], x_up[:, :],
                                             start=True, stop=True).then_inc(up_done, 1)
                if end and not last:
                    pe.wait_ge(ln.z_ready, CT * n)
                    at_least(pe, x_written, n - 1)
                    for t in range(CT):
                        mm = nc.tensor.transpose(psz[:, P * t:P * t + P], ln.z[:, t, :], ident[:, :])
                    mm.then_inc(zt_done, 1)
                if mid:
                    pe.wait_ge(gelu_done, 2 * HB * n + HB)
                    layer(n, h2, hid1, 2 * HB * n + HB)

            slots(pe, slot)

        @block.scalar
        def _(act):
            act.wait_ge(w_in, 16 * 7)
            act.wait_ge(scales_made, 3 + HB)

            def gelus(n, which, target):
                for m in range(HB):
                    act.wait_ge(hid_done, 2 * HB * n + HB * which + m + 1)
                    if m == 0 and which == 1:
                        at_least(act, y_done, n)
                    if m == 0 and which == 0:
                        at_least(act, hid_done, 2 * HB * n)
                    nc.scalar.activation(target[:, m, :], psh[m % 2][:, :], ACT.Gelu,
                                         scale=scales[:, 2 + which, m:m + 1]).then_inc(gelu_done, 1)

            def slot(s):
                n = s.n
                up, mid, end = active(s)
                if mid:
                    gelus(n, 0, hid1)
                if end:
                    act.wait_ge(y_done, n)
                    at_least(act, ln.z_ready, CT * (n - 1))
                    nc.scalar.copy(y_sb[:, :, :], psy[:, :, :]).then_inc(y_taken, 1)
                if up:
                    for m in range(HB):
                        act.wait_ge(up_done, 2 * HB * (n + 1) + 2 * m + 1)
                        at_least(act, gate_done, HB * (n + 1) + m - 1)
                        nc.scalar.activation(tanh[m % 2][:, :], ps1[m % 2][:, :], ACT.Tanh,
                                             scale=s1_half[:, m:m + 1]).then_inc(tanh_done, 1)
                if end and not last:
                    act.wait_ge(zt_done, n)
                    nc.scalar.copy(xT[:, bass.ds((n - 1) * CHUNK, CHUNK)], psz[:, :]).then_inc(x_written, 1)
                if mid:
                    gelus(n, 1, hid2)

            slots(act, slot)

        @block.vector
        def _(dve):
            dve.wait_ge(w_in, 16 * 7)
            nc.vector.tensor_scalar(s1_half[:, :], scales[:, 0, :], 0.5, None, ALU.mult).then_inc(scales_made, 1)
            for b in range(HB):
                nc.vector.tensor_tensor(w3[:, b, :], w3[:, b, :], s3[:, :], ALU.mult).then_inc(scales_made, 1)
            dve.wait_ge(scales_made, 1 + HB)
            nc.vector.tensor_tensor(s12_half[:, :], s1_half[:, :], scales[:, 1, :], ALU.mult).then_inc(scales_made, 2)
            dve.wait_ge(scales_made, 3 + HB)

            def slot(s):
                n = s.n
                up, mid, end = active(s)
                if end:
                    norm_stats(nc, dve, ln, y_sb, y_taken, n)
                if up:
                    for m in range(HB):
                        dve.wait_ge(tanh_done, HB * (n + 1) + m + 1)
                        nc.vector.scalar_tensor_tensor(gated[m % 2][:, :], tanh[m % 2][:, :], 1.0, ps1[m % 2][:, :],
                                                       ALU.add, ALU.mult).then_inc(gate_done, 1)
                        dve.wait_ge(up_done, 2 * HB * (n + 1) + 2 * m + 2)
                        if m == 0:
                            at_least(dve, hid_done, 2 * HB * n + HB)
                        dve.wait_ge(gate_done, HB * (n + 1) + m + 1)
                        nc.vector.scalar_tensor_tensor(hid0[:, m, :], gated[m % 2][:, :], s12_half[:, m:m + 1],
                                                       ps2[m % 2][:, :], ALU.mult, ALU.mult).then_inc(hid0_ready, 1)
                        if m == 1 and end:
                            norm_apply(nc, dve, ln, y_sb, n, stored if last else zt_done, 16 if last else 1)
                elif end:
                    norm_apply(nc, dve, ln, y_sb, n, stored if last else zt_done, 16 if last else 1)

            slots(dve, slot)

        @block.gpsimd
        def _(pool):
            def slot(s):
                if active(s)[2]:
                    norm_rstd(nc, pool, ln, s.n)

            slots(pool, slot)


def norm_stats(nc, dve, ln, y, y_ready, n, per=1):
    dve.wait_ge(y_ready, per * n)
    for t in range(ln.tiles):
        nc.vector.bn_stats(ln.stats[:, t, :], y[:, t, :]).then_inc(ln.bn_done, 1)
    at_least(dve, ln.rstd_done, n - 1)
    dve.wait_ge(ln.bn_done, ln.tiles * n)
    dve.sem_inc(ln.ln_step, 1)
    for t in range(ln.tiles):
        nc.vector.bn_aggr(ln.mean_var[:, t, :], ln.stats[:, t, :]).then_inc(ln.mv_done, 1)


def norm_rstd(nc, pool, ln, n):
    pool.wait_ge(ln.mv_done, ln.tiles * n)
    at_least(pool, ln.z_ready, ln.tiles * (n - 1))
    nc.gpsimd.tensor_tensor(ln.var_eps[:, :], ln.mean_var[:, :, 1], ln.consts["eps"][:, 0:ln.tiles],
                            ALU.add).then_inc(ln.eps_added, 1)
    pool.wait_ge(ln.eps_added, n)
    nc.gpsimd.tensor_tensor(ln.rstd[:, :], ln.var_eps[:, :], ln.consts["minus_half"][:, 0:ln.tiles],
                            ALU.pow).then_inc(ln.rstd_done, 1)


def norm_apply(nc, dve, ln, y, n, z_read, per):
    dve.wait_ge(ln.rstd_done, n)
    at_least(dve, z_read, per * (n - 1))
    for t in range(ln.tiles):
        nc.vector.tensor_scalar(ln.z[:, t, :], y[:, t, :], ln.mean_var[:, t, 0:1], ln.rstd[:, t:t + 1],
                                ALU.subtract, ALU.mult).then_inc(ln.z_ready, 1)


GATED = 341
GB = -(-GATED // P)
HALF = D // 2


def gated_ffn(nc, name, x1T, xT, out, consts, w, last):
    with ExitStack() as ctx:
        def sb(n, shape, dt=F32):
            return ctx.enter_context(nc.sbuf_tensor(f"{name}_{n}", shape, dt))

        def ps(n, shape, dt=F32):
            return ctx.enter_context(nc.psum_tensor(f"{name}_{n}", shape, dt))

        sems = phase_semaphores(nc, ctx)

        def sem(n):
            sems.append(nc.alloc_semaphore(f"{name}_{n}"))
            return sems[-1]

        ident = consts["ident"]
        w1 = sb("w1", [P, 2, GB, P])
        w2 = sb("w2", [P, GB, D])
        b1 = sb("b1", [P, 2, GB])
        gain_offset, b2 = sb("gain_offset", [P, 2]), sb("b2", [P, 1])
        b2_row, ones_row = sb("b2_row", [1, D]), sb("ones_row", [1, P])

        shifted = sb("shifted", [P, CT // 2, SEQ])
        x1_res, x_res = sb("x1_res", [P, CHUNK]), sb("x_res", [P, CHUNK])
        normed = [sb(f"normed{i}", [P, CHUNK]) for i in range(1)]
        gate = [sb(f"gate{i}", [P, CHUNK]) for i in range(2)]
        hid = sb("hid", [P, GB, CHUNK])
        y_sb = sb("y_sb", [P, CT, D])
        ln = Normaliser(name, sb, sem, consts, CT)
        if last:
            ln_out = Normaliser(name, lambda n, shape: sb("out_" + n, shape), lambda n: sem("out_" + n), consts, CT)

        psa = [ps(f"psa{i}", [P, CHUNK]) for i in range(2)]
        psg = [ps(f"psg{i}", [P, CHUNK]) for i in range(2)]
        pst, psz, pso = ps("pst", [P, CT, D]), ps("psz", [P, CHUNK]), ps("pso", [P, CT, D])

        w_in, shifted_in, res_in, stored = (sem(n) for n in ("w_in", "shifted_in", "res_in", "stored"))
        t_done, zt_done, up_done, out_done = (sem(n) for n in ("t_done", "zt_done", "up_done", "out_done"))
        ready, hid_ready = sem("ready"), sem("hid_ready")
        normed_ready, gate_done, out_taken = (sem(n) for n in ("normed_ready", "gate_done", "out_taken"))

        def active(s):
            if not s.known:
                return True, True, True
            return tuple(0 <= s.n + ahead < CHUNKS for ahead in (1, 0, -1))

        def slots(engine, body):
            for n in (-1, 0, 1):
                body(Slot(None, 1, n))
            with engine.Fori(0, CHUNKS - 3) as i:
                body(Slot(i, 1, 2))
            for n in (CHUNKS - 1, CHUNKS):
                body(Slot(None, 1, n))

        n_loads = 6
        res_loads = 2 if last else 1
        block = ctx.enter_context(nc.Block())

        @block.sync
        def _(sp):
            loads = [(w1[:, :, :, :], w["w1"].rearrange("p (e b n) -> p e b n", e=2, b=GB)),
                     (w2[:, :, :], w["w2"].rearrange("(b p) n -> p b n", p=P)), (b1[:, :, :], w["b1"]),
                     (gain_offset[:, :], w["gain_offset"]), (b2[:, :], w["b2"]), (b2_row[:, :], w["b2_row"])]
            for dst, src in loads:
                sp.dma_start(dst, src).then_inc(w_in, 16)
            sp.wait_ge(ready, 2)

            def slot(s):
                n = s.n
                norm, mid, end = active(s)

                def value(v):
                    return v if s.known else sp.snap(v)

                at_next = [value(n * CHUNK + CHUNK + SEQ * b) for b in range(CHUNK // SEQ)]
                at_before, at_out = value(n * CHUNK - CHUNK), value(n * CHUNK - CHUNK)
                t_read, out_read, z_made = value(n + 1), value(n - 1), value(CT * n)
                if norm:
                    at_least(sp, t_done, t_read)
                    for b in range(CHUNK // SEQ):
                        sp.dma_start(shifted[0:HALF, b, :], x1T[0:HALF, bass.ds(at_next[b], SEQ)]).then_inc(shifted_in, 16)
                        sp.dma_start(shifted[HALF:P, b, 1:SEQ], x1T[HALF:P, bass.ds(at_next[b], SEQ - 1)]).then_inc(shifted_in, 16)
                if end:
                    at_least(sp, out_done, out_read)
                    sp.dma_start(x1_res[:, :], x1T[:, bass.ds(at_before, CHUNK)]).then_inc(res_in, 16)
                    if last:
                        sp.dma_start(x_res[:, :], xT[:, bass.ds(at_before, CHUNK)]).then_inc(res_in, 16)
                        sp.wait_ge(ln_out.z_ready, z_made)
                        sp.dma_start(out[bass.ds(at_out, CHUNK), :].rearrange("(t p) d -> p t d", p=P),
                                     ln_out.z[:, :, :]).then_inc(stored, 16)

            slots(sp, slot)
            if last:
                sp.wait_ge(stored, 16 * CHUNKS)

        @block.tensor
        def _(pe):
            pe.wait_ge(w_in, 16 * n_loads)
            pe.wait_ge(ready, 2)

            def hidden(n, m):
                if m == 0:
                    pe.wait_ge(normed_ready, n + 1)
                at_least(pe, hid_ready, GB * n + m - 1)
                for bank, e in ((psg[m % 2], 1), (psa[m % 2], 0)):
                    mm = nc.tensor.matmul(bank[:, :], w1[:, e, m, :], normed[0][:, :], start=True, stop=True)
                mm.then_inc(up_done, 1)

            def slot(s):
                n = s.n
                norm, mid, end = active(s)
                if norm:
                    pe.wait_ge(shifted_in, 16 * 2 * (CHUNK // SEQ) * (n + 2))
                    at_least(pe, ln.z_ready, CT * (n + 1))
                    flat = shifted[:, :, :].rearrange("p b t -> p (b t)")
                    for t in range(CT):
                        mm = nc.tensor.transpose(pst[:, t, :], flat[:, P * t:P * t + P], ident[:, :])
                    mm.then_inc(t_done, 1)
                if end:
                    pe.wait_ge(hid_ready, GB * n)
                    at_least(pe, out_taken, n - 1)
                    pe.wait_ge(res_in, 16 * res_loads * n)
                    if last:
                        for t in range(CT):
                            ts = slice(P * t, P * t + P)
                            for k in range(GB):
                                nc.tensor.matmul(pso[:, t, :], hid[:, k, ts], w2[:, k, :], start=(k == 0), stop=False)
                            nc.tensor.matmul(pso[:, t, :], ones_row[:, :], b2_row[:, :], start=False, stop=False)
                            nc.tensor.matmul(pso[:, t, :], x1_res[:, ts], ident[:, :], start=False, stop=False)
                            mm = nc.tensor.matmul(pso[:, t, :], x_res[:, ts], ident[:, :], start=False, stop=True)
                    else:
                        flat = pso[:, :, :].rearrange("p t d -> p (t d)")
                        for k in range(GB):
                            nc.tensor.matmul(flat, w2[:, k, :], hid[:, k, :], start=(k == 0), stop=False)
                        mm = nc.tensor.matmul(flat, ident[:, :], x1_res[:, :], start=False, stop=True)
                    mm.then_inc(out_done, 1)
                if mid:
                    for m in range(GB):
                        hidden(n, m)
                if norm:
                    pe.wait_ge(ln.z_ready, CT * (n + 2))
                    at_least(pe, normed_ready, n + 1)
                    for t in range(CT):
                        mm = nc.tensor.transpose(psz[:, P * t:P * t + P], ln.z[:, t, :], ident[:, :])
                    mm.then_inc(zt_done, 1)

            slots(pe, slot)

        @block.scalar
        def _(act):
            act.wait_ge(w_in, 16 * n_loads)

            def slot(s):
                n = s.n
                norm, mid, end = active(s)
                if end:
                    act.wait_ge(out_done, n)
                    if last:
                        at_least(act, ln_out.z_ready, CT * (n - 1))
                        nc.scalar.copy(y_sb[:, :, :], pso[:, :, :]).then_inc(out_taken, 1)
                    else:
                        nc.scalar.activation(x1T[:, bass.ds((n - 1) * CHUNK, CHUNK)],
                                             pso[:, :, :].rearrange("p t d -> p (t d)"), ACT.Identity,
                                             bias=b2[:, :]).then_inc(out_taken, 1)
                if mid:
                    for m in range(GB):
                        act.wait_ge(up_done, GB * n + m + 1)
                        at_least(act, hid_ready, GB * n + m - 1)
                        nc.scalar.activation(gate[m % 2][:, :], psg[m % 2][:, :], ACT.Gelu,
                                             bias=b1[:, 1, m:m + 1]).then_inc(gate_done, 1)
                if norm:
                    act.wait_ge(zt_done, n + 2)
                    at_least(act, up_done, GB * (n + 1))
                    nc.scalar.activation(normed[0][:, :], psz[:, :], ACT.Identity, bias=gain_offset[:, 1:2],
                                         scale=gain_offset[:, 0:1]).then_inc(normed_ready, 1)

            slots(act, slot)

        @block.vector
        def _(dve):
            nc.vector.memset(shifted[:, :, 0:1], 0.0).then_inc(ready, 1)
            nc.vector.memset(ones_row[:, :], 1.0).then_inc(ready, 1)
            dve.wait_ge(w_in, 16 * n_loads)

            def slot(s):
                n = s.n
                norm, mid, end = active(s)
                if norm:
                    norm_stats(nc, dve, ln, pst, t_done, n + 2)
                if end and last:
                    norm_stats(nc, dve, ln_out, y_sb, out_taken, n)
                if norm:
                    norm_apply(nc, dve, ln, pst, n + 2, zt_done, 1)
                if mid:
                    for m in range(GB):
                        dve.wait_ge(gate_done, GB * n + m + 1)
                        if m == 0:
                            at_least(dve, out_done, n)
                        nc.vector.scalar_tensor_tensor(hid[:, m, :], psa[m % 2][:, :], b1[:, 0, m:m + 1],
                                                       gate[m % 2][:, :], ALU.add, ALU.mult).then_inc(hid_ready, 1)
                if end and last:
                    norm_apply(nc, dve, ln_out, y_sb, n, stored, 16)

            slots(dve, slot)

        @block.gpsimd
        def _(pool):
            def slot(s):
                norm, mid, end = active(s)
                if norm:
                    norm_rstd(nc, pool, ln, s.n + 2)
                if end and last:
                    norm_rstd(nc, pool, ln_out, s.n)

            slots(pool, slot)



LHEADS, LHD, WINDOW = 8, 64, 64
PAIRS = LHEADS // 2
INNER = LHEADS * LHD
SEEN0 = P + WINDOW
COLS = SEEN0 + P
QK_SCALE = 8.0
SQ_FLOOR = 1e-24


def local_attention(nc, name, src, dst, consts, w):
    with ExitStack() as ctx:
        def sb(n, shape, dt=F32):
            return ctx.enter_context(nc.sbuf_tensor(f"{name}_{n}", shape, dt))

        def ps(n, shape, dt=F32):
            return ctx.enter_context(nc.psum_tensor(f"{name}_{n}", shape, dt))

        sems = phase_semaphores(nc, ctx)

        def sem(n):
            sems.append(nc.alloc_semaphore(f"{name}_{n}"))
            return sems[-1]

        ident, ident_bf = consts["ident"], consts["ident_bf"]
        w_qkv = sb("w_qkv", [P, 3, INNER])
        wo = sb("wo", [P, PAIRS, D])
        rotary = sb("rotary", [P, 2, 2, 2, LHD])
        dim_scale = sb("dim_scale", [P, 2, LHD])
        masks = sb("masks", [P, 2 * SEEN0 + COLS])
        mask_q, mask_k = sb("mask_q", [P, 2 * SEEN0], BF16), sb("mask_k", [P, COLS], BF16)
        picks = sb("picks", [96, 4, P])
        minus_pick = sb("minus_pick", [96, 4, P], BF16)
        ones = sb("ones", [P, LHD])

        shifted = [sb(f"shifted{i}", [P, SEQ]) for i in range(2)]
        x_res = [sb(f"x_res{i}", [P, SEQ]) for i in range(2)]
        squares = [sb(f"squares{i}", [P, INNER]) for i in range(2)]
        terms = [sb(f"terms{i}", [P, 2, INNER]) for i in range(2)]
        length2, length2_held, rlength = (sb(n, [P, 4, LHEADS]) for n in ("length2", "length2_held", "rlength"))
        qk = [sb(f"qk{i}", [P, 4, INNER]) for i in range(2)]
        q_t = [sb(f"q_t{i}", [P, PAIRS, 2, SEQ]) for i in range(RING)]
        k_t = [sb(f"k_t{i}", [P, PAIRS, SEQ]) for i in range(RING)]
        v = [sb(f"v{i}", [P, 2, INNER]) for i in range(RING)]
        row_max = [sb(f"row_max{i}", [P, 2, LHEADS]) for i in range(2)]
        max_rest = sb("max_rest", [P, 2, 4])
        max_part = [sb(f"max_part{i}", [P, 2, 3, 4], BF16) for i in range(2)]
        max_rows = [sb(f"max_rows{i}", [96, SEQ], BF16) for i in range(2)]
        prob = [sb(f"prob{i}", [P, COLS]) for i in range(4)]
        pv_t = sb("pv_t", [P, 2, 8, 32])
        denom = sb("denom", [P, 8, 1])
        heads_t = sb("heads_t", [P, 8, 32])
        o_sb = sb("o_sb", [P, PAIRS, SEQ])

        qkv_ps = [ps(f"qkv_ps{i}", [P, INNER]) for i in range(2)]
        scores_q = [ps(f"scores_q{i}", [P, 2 * SEEN0]) for i in range(2)]
        scores_k = [ps(f"scores_k{i}", [P, COLS]) for i in range(2)]
        pv = ps("pv", [P, 2, SEQ])
        misc = ps("misc", [P, 2 * SEQ])
        misc_bf = misc[:, :].bitcast(BF16)

        w_in, ready, tables_made = sem("w_in"), sem("ready"), sem("tables_made")
        shifted_in = [sem(f"shifted_in{i}") for i in range(2)]
        x_res_in = [sem(f"x_res_in{i}") for i in range(2)]
        qkv_done, turned, sq_done, sk_done, pv_done, maxt_done, out_done = (
            sem(n) for n in ("qkv_done", "turned", "sq_done", "sk_done", "pv_done", "maxt_done", "out_done"))
        terms_done, length_done, scaled_qk, max_found, pv_turned, inverted, scaled, o_ready = (
            sem(n) for n in ("terms_done", "length_done", "scaled_qk", "max_found", "pv_turned", "inverted", "scaled", "o_ready"))
        squared, v_ready, qk_taken, maxt_taken, out_written, exp_done, q_half = (
            sem(n) for n in ("squared", "v_ready", "qk_taken", "maxt_taken", "out_written", "exp_done", "q_half"))
        added, held, rlength_done, max_step, max_split = (
            sem(n) for n in ("added", "held", "rlength_done", "max_step", "max_split"))

        def active(s):
            if not s.known:
                return (True,) * 5
            return tuple(0 <= s.n + ahead < BATCH for ahead in (3, 2, 1, 0, -1))

        def slots(engine, body):
            for n in range(-AHEAD, RING + 1):
                body(Slot(None, RING, n))
            with engine.Fori(0, (BATCH - 2 * RING) // RING) as i:
                for offset in range(RING + 1, 2 * RING + 1):
                    body(Slot(i, RING, offset))
            for n in range(BATCH - RING + 1, BATCH + 1):
                body(Slot(None, RING, n))

        n_loads = 6
        n_ready = 2 + RING + 2 + 1
        block = ctx.enter_context(nc.Block())

        @block.sync
        def _(sp):
            for to, of in ((w_qkv[:, :, :], w["w_qkv"]), (wo[:, :, :], w["wo"].rearrange("(b p) n -> p b n", p=P)),
                           (rotary[:, :, :, :, :], w["rotary"]), (masks[:, :], w["masks"]),
                           (picks[:, :, :], w["picks"]),
                           (dim_scale[:, :, :], w["dim_scale"].to_broadcast([P, 2, LHD]))):
                sp.dma_start(to, of).then_inc(w_in, 16)
            sp.wait_ge(ready, n_ready)

            def slot(s):
                n, j = s.n, s.offset % RING
                a, t, b1, b3, c = active(s)

                def value(x):
                    return x if s.known else sp.snap(x)

                at_next, at_now = value(n * SEQ + AHEAD * SEQ), value(n * SEQ)
                qkv_read, out_read = value(6 * n + 12), value(n - 1)
                if a:
                    buf = (j + AHEAD) % 2
                    at_least(sp, qkv_done, qkv_read)
                    sp.dma_start(shifted[buf][0:HALF, :], src[0:HALF, bass.ds(at_next, SEQ)]).then_inc(shifted_in[buf], 16)
                    sp.dma_start(shifted[buf][HALF:P, 1:SEQ],
                                 src[HALF:P, bass.ds(at_next, SEQ - 1)]).then_inc(shifted_in[buf], 16)
                if b3:
                    at_least(sp, out_done, out_read)
                    sp.dma_start(x_res[j % 2][:, :], src[:, bass.ds(at_now, SEQ)]).then_inc(x_res_in[j % 2], 16)

            slots(sp, slot)

        @block.tensor
        def _(pe):
            pe.wait_ge(w_in, 16 * n_loads)
            pe.wait_ge(ready, n_ready)
            pe.wait_ge(tables_made, 2 + 8 + 1)

            def misc_free(s, use):
                n = s.n
                a, t, b1, b3, c = active(s)
                order = [("max1", b3, maxt_taken, 2 * n + 2), ("turn0", t, qk_taken, 4 * (n + 2) + 1),
                         ("out", c, out_written, n), ("turn1", t, qk_taken, 4 * (n + 2) + 2),
                         ("max0", b1, maxt_taken, 2 * (n + 1) + 1), ("turn2", t, qk_taken, 4 * (n + 2) + 3),
                         ("turn3", t, qk_taken, 4 * (n + 2) + 4)]
                k = [o[0] for o in order].index(use)
                for o in reversed(order[:k]):
                    if o[1]:
                        return at_least(pe, o[2], o[3])
                before = active(Slot(s.i, RING, s.offset - 1))
                if before[1]:
                    at_least(pe, qk_taken, 4 * (n + 2))
                if before[2]:
                    at_least(pe, maxt_taken, 2 * n + 1)
                elif before[3]:
                    at_least(pe, maxt_taken, 2 * n)
                if before[4]:
                    at_least(pe, out_written, n - 1)

            def qkv(s, use):
                m, buf = s.n + 3, (s.offset + 3) % 2
                part, tile = (use % 2, use // 2) if use < 4 else (2, use - 4)
                if use == 0:
                    pe.wait_ge(shifted_in[buf], 32 * s.fills(3, 2))
                if use < 2:
                    at_least(pe, v_ready, 2 * m - 1 + use)
                else:
                    pe.wait_ge(squared, 4 * m + use - 1)
                    pe.wait_ge(terms_done, 8 * m + 2 * (use - 1))
                nc.tensor.matmul(qkv_ps[use % 2][:, :], shifted[buf][:, P * tile:P * tile + P], w_qkv[:, part, :],
                                 start=True, stop=True).then_inc(qkv_done, 1)

            def turn(s, use):
                m, which = s.n + 2, use // 2
                pe.wait_ge(scaled_qk, 4 * m + 2 * which + 2)
                misc_free(s, f"turn{use}")
                for p in range(2):
                    for tile in range(2):
                        pair = 2 * (use % 2) + p
                        mm = nc.tensor.transpose(misc[:, SEQ * p + P * tile:SEQ * p + P * tile + P],
                                                 qk[(s.offset + 2) % 2][:, 2 * tile + which, P * pair:P * pair + P],
                                                 ident[:, :])
                mm.then_inc(turned, 1)

            def turn_max(s, half, batch):
                misc_free(s, f"max{half}")
                pe.wait_ge(max_split, 2 * batch + half + 1)
                for qt in range(2):
                    mm = nc.tensor.transpose(misc_bf[0:12, P * qt:P * qt + P],
                                             max_part[half][:, qt, :, :].rearrange("p a h -> p (a h)"), ident_bf[:, :])
                mm.then_inc(maxt_done, 1)

            def weigh_v(n, j, pair):
                pe.wait_ge(exp_done, LHEADS * n + 2 * pair + 2)
                if pair == 0:
                    pe.wait_ge(v_ready, 2 * n + 2)
                at_least(pe, pv_turned, 4 * n + pair)
                for of_ones in range(2):
                    for kt, q0, q1, col, start, stop in ((0, 0, SEEN0, 0, True, False), (1, P, SEEN0, SEEN0, False, True),
                                                         (1, SEEN0, SEQ, 2 * P, True, True)):
                        for e in range(2):
                            h = 2 * pair + e
                            weights = ones[:, :] if of_ones else v[j][:, kt, LHD * h:LHD * h + LHD]
                            mm = nc.tensor.matmul(pv[LHD * e:LHD * e + LHD, of_ones, q0:q1], weights,
                                                  prob[h % 4][:, col:col + q1 - q0], start=start, stop=stop)
                mm.then_inc(pv_done, 1)

            def slot(s):
                n, j = s.n, s.offset % RING
                a, t, b1, b3, c = active(s)
                jb = (j + 1) % RING
                for h in range(LHEADS):
                    pair, e, u = h // 2, h % 2, h
                    if b1:
                        if h == 0:
                            pe.wait_ge(qk_taken, 4 * (n + 2))
                        at_least(pe, max_found, LHEADS * (n + 1) + h - 1)
                        bank = scores_q[h % 2]
                        nc.tensor.matmul(bank[:, :], ident_bf[:, :], mask_q[:, :], start=True, stop=False)
                        nc.tensor.matmul(bank[:, 0:P], q_t[jb][:, pair, e, 0:P], k_t[jb][:, pair, 0:P],
                                         start=False, stop=False)
                        nc.tensor.matmul(bank[:, SEEN0:2 * SEEN0], q_t[jb][:, pair, e, P:SEQ],
                                         k_t[jb][:, pair, P - WINDOW:SEQ], start=False, stop=True).then_inc(sq_done, 1)
                    if b3:
                        if h % 4 == 0:
                            pe.wait_ge(maxt_taken, 2 * n + 1 + h // 4)
                        at_least(pe, exp_done, LHEADS * n + h - 1)
                        bank, rows, pick = scores_k[h % 2], max_rows[h // 4], minus_pick[:, h % 4, :]
                        nc.tensor.matmul(bank[:, :], ident_bf[:, :], mask_k[:, :], start=True, stop=False)
                        nc.tensor.matmul(bank[:, 0:SEEN0], pick, rows[:, 0:SEEN0], start=False, stop=False)
                        nc.tensor.matmul(bank[:, SEEN0:COLS], pick, rows[:, P:SEQ], start=False, stop=False)
                        nc.tensor.matmul(bank[:, 0:SEEN0], k_t[j][:, pair, 0:P], q_t[j][:, pair, e, 0:SEEN0],
                                         start=False, stop=False)
                        nc.tensor.matmul(bank[:, SEEN0:COLS], k_t[j][:, pair, P:SEQ], q_t[j][:, pair, e, P:SEQ],
                                         start=False, stop=True).then_inc(sk_done, 1)
                    if u == 0:
                        if c:
                            weigh_v(n - 1, (j - 1) % RING, 3)
                        if b3:
                            turn_max(s, 1, n)
                    if u == 1:
                        if t:
                            turn(s, 0)
                        if a:
                            qkv(s, 0)
                    if u == 2:
                        if a:
                            qkv(s, 1)
                        if c:
                            misc_free(s, "out")
                            pe.wait_ge(o_ready, PAIRS * n)
                            pe.wait_ge(x_res_in[(j - 1) % 2], 16 * s.fills(-1, 2))
                            for p in range(PAIRS):
                                nc.tensor.matmul(misc[:, 0:SEQ], wo[:, p, :], o_sb[:, p, :], start=(p == 0), stop=False)
                            nc.tensor.matmul(misc[:, 0:SEQ], ident[:, :], x_res[(j - 1) % 2][:, :],
                                             start=False, stop=True).then_inc(out_done, 1)
                    if u == 3:
                        if t:
                            turn(s, 1)
                        if b3:
                            weigh_v(n, j, 0)
                        if a:
                            qkv(s, 2)
                    if u == 4:
                        if b1:
                            turn_max(s, 0, n + 1)
                        if a:
                            qkv(s, 3)
                    if u == 5:
                        if t:
                            turn(s, 2)
                        if b3:
                            weigh_v(n, j, 1)
                        if a:
                            qkv(s, 4)
                    if u == 6:
                        if t:
                            turn(s, 3)
                        if a:
                            qkv(s, 5)
                    if u == 7 and b3:
                        weigh_v(n, j, 2)

            slots(pe, slot)

        @block.vector
        def _(dve):
            for x in shifted:
                nc.vector.memset(x[:, 0:1], 0.0).then_inc(ready, 1)
            for q in q_t:
                nc.vector.memset(q[:, :, :, :], 0.0).then_inc(ready, 1)
            for m in max_rows:
                nc.vector.memset(m[:, :], 0.0).then_inc(ready, 1)
            nc.vector.memset(ones[:, :], 1.0).then_inc(ready, 1)
            dve.wait_ge(w_in, 16 * n_loads)
            nc.vector.tensor_copy(mask_q[:, :], masks[:, 0:2 * SEEN0]).then_inc(tables_made, 1)
            nc.vector.tensor_copy(mask_k[:, :], masks[:, 2 * SEEN0:]).then_inc(tables_made, 1)
            for which in range(2):
                for tile in range(2):
                    for f in range(2):
                        nc.vector.tensor_tensor(rotary[:, which, tile, f, :], rotary[:, which, tile, f, :],
                                                dim_scale[:, which, :], ALU.mult).then_inc(tables_made, 1)
            nc.vector.tensor_copy(minus_pick[:, :, :], picks[:, :, :]).then_inc(tables_made, 1)
            dve.wait_ge(tables_made, 2 + 8 + 1)

            def take_qk(s, use):
                m = s.n + 3
                which, tile = use % 2, use // 2
                dve.wait_ge(squared, 4 * m + use + 1)
                at_least(dve, added, 8 * m + 2 * use - 2)
                heads = qkv_ps[use % 2][:, :].rearrange("p (h d) -> p h d", d=LHD)
                for f in range(2):
                    factor = rotary[:, which, tile, f:f + 1, :].to_broadcast([P, LHEADS, LHD])
                    nc.vector.tensor_tensor(terms[use % 2][:, f, :].rearrange("p (h d) -> p h d", d=LHD), heads, factor,
                                            ALU.mult).then_inc(terms_done, 1)
                nc.vector.tensor_reduce(length2[:, use, :], squares[use % 2][:, :].rearrange("p (h d) -> p h d", d=LHD),
                                        AX.X, ALU.add).then_inc(length_done, 1)
                if use == 3:
                    at_least(dve, rlength_done, m)
                    dve.wait_ge(length_done, 4 * (m + 1))
                    nc.vector.tensor_scalar(length2_held[:, :, :], length2[:, :, :], SQ_FLOOR, None,
                                            ALU.max).then_inc(held, 1)

            def to_unit(s, which):
                dve.wait_ge(rlength_done, s.n + 3)
                for tile in range(2):
                    i = 2 * tile + which
                    x = qk[(s.offset + 2) % 2][:, i, :].rearrange("p (h d) -> p h d", d=LHD)
                    r = rlength[:, i, :].rearrange("p (h d) -> p h d", d=1).to_broadcast([P, LHEADS, LHD])
                    nc.vector.tensor_tensor(x, x, r, ALU.mult).then_inc(scaled_qk, 1)

            def normalise_pair(m, pair):
                at_least(dve, scaled, 4 * m + pair)
                dve.wait_ge(pv_done, 4 * m + pair + 1)
                nc.vector.transpose(pv_t[:, :, :, :].rearrange("p g c x -> p (g c x)"),
                                    pv[:, :, :].rearrange("p g q -> p (g q)")).then_inc(pv_turned, 1)
                dve.wait_ge(pv_turned, 4 * m + pair + 1)
                nc.vector.reciprocal(denom[:, :, :], pv_t[:, 1, :, 0:1]).then_inc(inverted, 1)
                at_least(dve, o_ready, 4 * m + pair)
                dve.wait_ge(inverted, 4 * m + pair + 1)
                nc.vector.tensor_tensor(heads_t[:, :, :], pv_t[:, 0, :, :], denom[:, :, :].to_broadcast([P, 8, 32]),
                                        ALU.mult).then_inc(scaled, 1)
                if pair == 0:
                    at_least(dve, out_done, m)
                dve.wait_ge(scaled, 4 * m + pair + 1)
                nc.vector.transpose(o_sb[:, pair, :], heads_t[:, :, :].rearrange("p c x -> p (c x)")).then_inc(o_ready, 1)

            def slot(s):
                n, j = s.n, s.offset % RING
                a, t, b1, b3, c = active(s)
                for h in range(LHEADS):
                    if b1:
                        if h == 0:
                            at_least(dve, max_split, 2 * n)
                        dve.wait_ge(sq_done, LHEADS * (n + 1) + h + 1)
                        nc.vector.tensor_reduce(row_max[(j + 1) % 2][:, :, h],
                                                scores_q[h % 2][:, :].rearrange("p (t k) -> p t k", t=2),
                                                AX.X, ALU.max).then_inc(max_found, 1)
                    if h == 0 and t:
                        to_unit(s, 0)
                    if h == 1 and c:
                        normalise_pair(n - 1, 3)
                    if h == 1 and a:
                        take_qk(s, 0)
                    if h == 2 and t:
                        to_unit(s, 1)
                    if h == 2 and a:
                        take_qk(s, 1)
                    if h == 3 and a:
                        take_qk(s, 2)
                    if h == 4 and b3:
                        normalise_pair(n, 0)
                    if h == 4 and a:
                        take_qk(s, 3)
                    if h == 6 and b3:
                        normalise_pair(n, 1)
                    if h == 7 and b3:
                        normalise_pair(n, 2)

            slots(dve, slot)

        @block.scalar
        def _(act):
            act.wait_ge(ready, n_ready)

            def square(s, use):
                m = s.n + 3
                act.wait_ge(qkv_done, 6 * m + use + 1)
                at_least(act, length_done, 4 * m + use - 1)
                nc.scalar.activation(squares[use % 2][:, :], qkv_ps[use % 2][:, :], ACT.Square).then_inc(squared, 1)

            def take_v(s, tile):
                m = s.n + 3
                act.wait_ge(qkv_done, 6 * m + 5 + tile)
                at_least(act, pv_done, PAIRS * s.n)
                nc.scalar.copy(v[(s.offset + 3) % RING][:, tile, :], qkv_ps[tile][:, :]).then_inc(v_ready, 1)

            def take_turned(s, use):
                m, jt, pairs = s.n + 2, (s.offset + 2) % RING, slice(2 * (use % 2), 2 * (use % 2) + 2)
                act.wait_ge(turned, 4 * m + use + 1)
                at_least(act, sk_done, LHEADS * (s.n - 1))
                bank = misc[:, :].rearrange("p (a q) -> p a q", a=2)
                if use < 2:
                    nc.scalar.copy(q_t[jt][0:HALF, pairs, 0, :], bank[0:HALF, :, :]).then_inc(q_half, 1)
                    nc.scalar.copy(q_t[jt][HALF:P, pairs, 1, :], bank[HALF:P, :, :]).then_inc(qk_taken, 1)
                else:
                    nc.scalar.copy(k_t[jt][:, pairs, :], bank[:, :, :]).then_inc(qk_taken, 1)

            def take_max(batch, half, scored):
                act.wait_ge(maxt_done, 2 * batch + half + 1)
                at_least(act, sk_done, scored)
                nc.scalar.copy(max_rows[half][0:12, :], misc_bf[0:12, 0:SEQ]).then_inc(maxt_taken, 1)

            def slot(s):
                n, j = s.n, s.offset % RING
                a, t, b1, b3, c = active(s)
                for h in range(LHEADS):
                    if b3:
                        act.wait_ge(sk_done, LHEADS * n + h + 1)
                        at_least(act, pv_done, PAIRS * n + h // 2 - 1)
                        nc.scalar.activation(prob[h % 4][:, :], scores_k[h % 2][:, :], ACT.Exp,
                                             scale=QK_SCALE).then_inc(exp_done, 1)
                    if h == 0 and b3:
                        take_max(n, 1, LHEADS * n)
                    if h == 1:
                        if t:
                            take_turned(s, 0)
                        if a:
                            square(s, 0)
                    if h == 2:
                        if a:
                            square(s, 1)
                        if c:
                            act.wait_ge(out_done, n)
                            nc.scalar.copy(dst[:, bass.ds((n - 1) * SEQ, SEQ)], misc[:, 0:SEQ]).then_inc(out_written, 1)
                    if h == 3:
                        if t:
                            take_turned(s, 1)
                        if a:
                            square(s, 2)
                    if h == 4:
                        if b1:
                            take_max(n + 1, 0, LHEADS * n + 4)
                        if a:
                            square(s, 3)
                    if h == 5:
                        if t:
                            take_turned(s, 2)
                        if a:
                            take_v(s, 0)
                    if h == 6:
                        if t:
                            take_turned(s, 3)
                        if a:
                            take_v(s, 1)

            slots(act, slot)

        @block.gpsimd
        def _(pool):
            pool.wait_ge(ready, n_ready)
            zeros = consts["zeros"][:, 0:8].rearrange("p (a b) -> p a b", a=2)

            def split_max(batch, j, half):
                hs = slice(4 * half, 4 * half + 4)
                m, part = row_max[j % 2], max_part[half]
                pool.wait_ge(max_found, LHEADS * batch + 4 * half + 4)
                at_least(pool, maxt_done, 2 * (batch - 1) + half + 1)
                steps = 3 * (2 * batch + half)
                nc.gpsimd.tensor_tensor(part[:, :, 0, :], m[:, :, hs], zeros, ALU.add).then_inc(max_step, 1)
                pool.wait_ge(max_step, steps + 1)
                nc.gpsimd.tensor_tensor(max_rest[:, :, :], m[:, :, hs], part[:, :, 0, :], ALU.subtract).then_inc(max_step, 1)
                pool.wait_ge(max_step, steps + 2)
                nc.gpsimd.tensor_tensor(part[:, :, 1, :], max_rest[:, :, :], zeros, ALU.add).then_inc(max_step, 1)
                pool.wait_ge(max_step, steps + 3)
                nc.gpsimd.tensor_tensor(part[:, :, 2, :], max_rest[:, :, :], part[:, :, 1, :],
                                        ALU.subtract).then_inc(max_split, 1)

            def add_terms(s, use):
                m = s.n + 3
                pool.wait_ge(terms_done, 8 * m + 2 * use + 2)
                if use == 0:
                    at_least(pool, turned, 4 * (m - 1))
                halves = "p (h e d) -> p h e d"
                own = terms[use % 2][:, 0, :].rearrange(halves, e=2, d=LHD // 2)
                other = terms[use % 2][:, 1, :].rearrange(halves, e=2, d=LHD // 2)
                to = qk[(s.offset + 3) % 2][:, use, :].rearrange(halves, e=2, d=LHD // 2)
                for e in range(2):
                    nc.gpsimd.tensor_tensor(to[:, :, e, :], own[:, :, e, :], other[:, :, 1 - e, :],
                                            ALU.add).then_inc(added, 1)

            def slot(s):
                n, j = s.n, s.offset % RING
                a, t, b1, b3, c = active(s)
                if b3:
                    split_max(n, j, 1)
                if a:
                    for use in range(3):
                        add_terms(s, use)
                if b1:
                    split_max(n + 1, j + 1, 0)
                if a:
                    add_terms(s, 3)
                    m = n + 3
                    flat = "p a h -> p (a h)"
                    at_least(pool, scaled_qk, 4 * m)
                    pool.wait_ge(held, m + 1)
                    nc.gpsimd.tensor_tensor(rlength[:, :, :].rearrange(flat), length2_held[:, :, :].rearrange(flat),
                                            consts["minus_half"][:, :], ALU.pow).then_inc(rlength_done, 1)

            slots(pool, slot)


def build(nc, stages, x, out, d):
    with ExitStack() as ctx:
        def sb(n, shape, dt=F32):
            return ctx.enter_context(nc.sbuf_tensor(n, shape, dt))

        xT = sb("xT", [P, TOKENS])
        consts = {"ident": sb("ident", [P, P]), "ident_bf": sb("ident_bf", [P, P], BF16),
                  "eps": sb("eps", [P, 4]), "minus_half": sb("minus_half", [P, 4 * LHEADS]), "zeros": sb("zeros", [P, 2 * HEADS])}
        loaded = ctx.enter_context(nc.semaphore("loaded"))
        filled = ctx.enter_context(nc.semaphore("filled"))
        with nc.Block() as block:
            @block.sync
            def _(sp):
                sp.dma_start(xT[:, :], x).then_inc(loaded, 16)
                sp.dma_start(consts["ident"][:, :], d["ident"]).then_inc(loaded, 16)
                sp.wait_ge(loaded, 32)

            @block.vector
            def _(dve):
                dve.wait_ge(loaded, 32)
                nc.vector.memset(consts["eps"][:, :], LN_EPS).then_inc(filled, 1)
                nc.vector.memset(consts["minus_half"][:, :], -0.5).then_inc(filled, 1)
                nc.vector.tensor_copy(consts["ident_bf"][:, :], consts["ident"][:, :]).then_inc(filled, 1)
                nc.vector.memset(consts["zeros"][:, :], 0.0).then_inc(filled, 1)
                dve.wait_ge(filled, 4)

        x1T = sb("x1T", [P, TOKENS]) if "local0" in stages else None
        for k, stage in enumerate(stages):
            last = k == len(stages) - 1
            if stage in ("attn0", "attn1"):
                attention(nc, stage, xT, out, consts, d[stage], stage == "attn0", last)
            elif stage == "ffn0":
                ffn(nc, stage, xT, out, consts, d[stage], last)
            elif stage in ("local0", "local1"):
                local_attention(nc, stage, xT if stage == "local0" else x1T, x1T, consts, d[stage])
            elif stage in ("gated0", "gated1"):
                gated_ffn(nc, stage, x1T, xT, out, consts, d[stage], last)


STAGES = ("attn0", "ffn0", "attn1", "local0", "gated0", "local1", "gated1")


def laid_out(inputs):
    f = {k: np.asarray(v) for k, v in inputs.items()}
    c = np.ascontiguousarray

    def by_dim(w):
        return c(w.reshape(w.shape[0], HEADS, HD).transpose(0, 2, 1).reshape(w.shape[0], D))

    def by_group(w):
        return c(w.reshape(4, 4, HD, D).transpose(1, 0, 2, 3).reshape(D, D))

    inv_freq = (np.float32(1.0) / np.float32(10000.0) ** (np.arange(0, HD, 2, dtype=np.float32) / np.float32(HD))).astype(np.float32)
    angle = np.arange(SEQ, dtype=np.float32)[:, None] * inv_freq[None, :]
    cos = np.repeat(np.repeat(np.cos(angle), 2, axis=1).T, HEADS, axis=0)
    sin = np.repeat(np.repeat(np.sin(angle), 2, axis=1).T, HEADS, axis=0)
    w0 = f["L0_attn_w_qkv"]
    w1 = f["L1_attn_qkv_w"].T.reshape(D, HEADS, 3, HD)
    b1 = f["L1_attn_qkv_b"].reshape(1, HEADS, 3, HD)
    pick = lambda w, i: c(w[:, :, i, :].reshape(w.shape[0], D))
    shapes = {}

    half_idx = np.arange(0, LHD, 2, dtype=np.float32)
    t = np.arange(SEQ, dtype=np.float32)
    freqs = t[:, None] * (np.float32(1.0) / np.float32(10000.0) ** (half_idx / np.float32(LHD)))[None, :]
    freqs = np.concatenate([freqs, freqs], axis=-1)
    base = ((half_idx + np.float32(0.4 * LHD)) / np.float32(1.4 * LHD)).astype(np.float32)
    scale = base[None, :] ** ((t - SEQ // 2) / np.float32(WINDOW // 2))[:, None]
    scale = np.concatenate([scale, scale], axis=-1)
    sign = np.where(np.arange(LHD) < LHD // 2, 1.0, -1.0).astype(np.float32)
    other = (np.arange(LHD) + LHD // 2) % LHD
    factors = []
    for decay in (scale, 1 / scale):
        own, turned = np.cos(freqs) * decay, (np.sin(freqs) * decay)[:, other] * sign
        factors.append(np.stack([own, turned], axis=1).reshape(2, P, 2, LHD).transpose(1, 0, 2, 3))
    rotary = c(np.stack(factors, axis=1).astype(np.float32))

    def mask(query, key):
        return np.where((key <= query) & (query <= key + WINDOW), 0.0, -1e30).astype(np.float32)

    i, far = np.arange(P)[:, None], 10 * SEQ
    col = np.arange(SEEN0)[None, :]
    masks = c(np.concatenate([mask(i, np.where(col < P, col, far)), mask(P + i, P - WINDOW + col),
                              mask(col, i), mask(P + np.arange(P)[None, :], P + i)], axis=1))
    picks = np.zeros((96, 4, P), np.float32)
    for h in range(4):
        picks[[h, 4 + h, 8 + h], h] = -1.0
    for l in range(2):
        shapes[f"local{l}.w_qkv"] = c(f["L1_ffn_wqkv"][l].reshape(D, 3, INNER))
        shapes[f"local{l}.wo"] = c(f["L1_ffn_wo"][l])
        shapes[f"local{l}.dim_scale"] = c(np.stack([f["L1_ffn_q_scale"][l], f["L1_ffn_k_scale"][l]])[None])
        shapes[f"local{l}.rotary"], shapes[f"local{l}.masks"], shapes[f"local{l}.picks"] = rotary, masks, picks
        pad = np.zeros((D, GB * P - GATED), np.float32)
        w_in, w_out, b_in = f["L1_ffn_w1"][l], f["L1_ffn_w2"][l], f["L1_ffn_b1"][l][None]
        shapes[f"gated{l}.w1"] = c(np.concatenate([w_in[:, :GATED], pad, w_in[:, GATED:], pad], axis=1))
        shapes[f"gated{l}.w2"] = c(np.concatenate([w_out, pad.T], axis=0))
        shapes[f"gated{l}.b1"] = c(np.concatenate([b_in[:, :GATED], pad[:1], b_in[:, GATED:], pad[:1]], axis=1)
                                   .reshape(2, GB, P).transpose(2, 0, 1))
        shapes[f"gated{l}.gain_offset"] = c(np.stack([f["L1_ffn_ln_g"][l], f["L1_ffn_ln_b"][l]], axis=1))
        shapes[f"gated{l}.b2"] = c(f["L1_ffn_b2"][l].reshape(D, 1))
        shapes[f"gated{l}.b2_row"] = c(f["L1_ffn_b2"][l].reshape(1, D))
    return shapes | {
        "ffn0.w1": c(f["L0_ffn_w1_w"].T), "ffn0.w2": c(f["L0_ffn_w2_w"].T),
        "ffn0.h1": c(f["L0_ffn_h1_w"].T), "ffn0.h2": c(f["L0_ffn_h2_w"].T), "ffn0.w3": c(f["L0_ffn_w3_w"].T),
        "ffn0.s3": f["L0_ffn_w3_s"].reshape(1, D),
        "ffn0.scales": c(np.stack([f[f"L0_ffn_{k}_s"].reshape(HB, P) for k in ("w1", "w2", "h1", "h2")]).transpose(2, 0, 1)),
        "x": c(f["L0_attn_x"].reshape(TOKENS, D).T),
        "ident": np.eye(P, dtype=np.float32),
        "attn0.wq": by_dim(w0[:, 0:D]), "attn0.wk": by_dim(w0[:, D:2 * D]), "attn0.wv": c(w0[:, 2 * D:]),
        "attn0.wo": by_group(f["L0_attn_w_proj"]),
        "attn0.cos_sin": c(np.stack([cos, sin], axis=1).astype(np.float32)),
        "attn1.wq": by_dim(pick(w1, 0)), "attn1.wk": by_dim(pick(w1, 1)), "attn1.wv": pick(w1, 2),
        "attn1.wo": by_group(c(f["L1_attn_fc_w"].T)),
        "attn1.bq": by_dim(pick(b1, 0)).reshape(D, 1), "attn1.bk": by_dim(pick(b1, 1)).reshape(D, 1),
        "attn1.bv": pick(b1, 2), "attn1.bo": f["L1_attn_fc_b"].reshape(1, D),
        "attn1.mask": c(np.tile(f["L1_attn_head_mask"], HD).reshape(D, 1)),
        "attn1.mask_v": c(np.repeat(f["L1_attn_head_mask"], HD).reshape(1, D)),
    }


def kernel(**inputs):
    import concourse.bacc as bacc
    from concourse.bass_utils import run_bass_kernel_spmd

    nc = bacc.Bacc("TRN2", target_bir_lowering=False, num_devices=1)
    arrays = {"in_" + n.replace(".", "_"): a for n, a in laid_out(inputs).items()}
    views = {}
    for name, a in laid_out(inputs).items():
        ap = nc.dram_tensor("in_" + name.replace(".", "_"), a.shape, mybir.dt.from_np(a.dtype), kind="ExternalInput").ap()
        group, _, key = name.rpartition(".")
        if group:
            views.setdefault(group, {})[key] = ap
        else:
            views[key] = ap
    out = nc.dram_tensor("out", (TOKENS, D), F32, kind="ExternalOutput").ap()
    build(nc, STAGES, views["x"], out, views)
    result = run_bass_kernel_spmd(nc, [arrays], core_ids=[0])
    return result.results[0]["out"].reshape(BATCH, SEQ, D)
```

```python
import concourse.bass as bass
from concourse import mybir
from contextlib import ExitStack
import numpy as np

F32 = mybir.dt.float32
F32R = mybir.dt.float32r
BF16 = mybir.dt.bfloat16
ALU = mybir.AluOpType
ACT = mybir.ActivationFunctionType
AX = mybir.AxisListType

P = 128
BATCH, SEQ, D = 32, 256, 128
TOKENS = BATCH * SEQ
LN_EPS = 1e-5


def phase_semaphores(nc, ctx):
    sems = []

    def clear():
        nc.clear_and_free_semaphores(sems)
        nc.all_engine_barrier()

    ctx.callback(clear)
    return sems


class Slot:

    def __init__(self, i, step, offset):
        self.i, self.step, self.offset = i, step, offset
        self.known = i is None
        self.n = offset if i is None else i * step + offset

    def fills(self, ahead, ring):
        times = (self.offset + ahead) // ring + 1
        return times if self.known else self.i * (self.step // ring) + times


def at_least(engine, sem, value):
    if isinstance(value, int) and value <= 0:
        return
    engine.wait_ge(sem, value)


PRODUCTS = ((0, 0), (0, 1), (1, 0))


def split_matmul(nc, out, lhs, rhs, start, stop):
    for i, (a, b) in enumerate(PRODUCTS):
        mm = nc.tensor.matmul(out, lhs(a), rhs(b), start=start and i == 0, stop=stop and i == len(PRODUCTS) - 1)
    return mm


def write_rest(nc, lo, whole, hi):
    return nc.vector.tensor_tensor(lo, whole, hi.bitcast(F32), ALU.subtract)


HEADS, HD = 16, 8
UNITS = HEADS // 2
Q_PARTS = [0, 0, 0, 1, 1, 2]
K_PARTS = [0, 1, 2, 0, 1, 0]
STACKED = HD * len(Q_PARTS)
MAX_ROW = 96
ROWS_MAX, ROWS_PROB = MAX_ROW, MAX_ROW + 3
AHEAD = 3
RING = 4
LOOPS = BATCH // RING - 3
STACK_DMAS = len(Q_PARTS) + len(K_PARTS)


def attention(nc, name, src, xT, out, consts, w, rotary, last):
    with ExitStack() as ctx:
        def sb(n, shape, dt=F32):
            return ctx.enter_context(nc.sbuf_tensor(f"{name}_{n}", shape, dt))

        def ps(n, shape, dt=F32):
            return ctx.enter_context(nc.psum_tensor(f"{name}_{n}", shape, dt))

        sems = phase_semaphores(nc, ctx)

        def sem(n):
            sems.append(nc.alloc_semaphore(f"{name}_{n}"))
            return sems[-1]

        ident, ident_bf = consts["ident"], consts["ident_bf"]

        wq, wk, wv, wo = (sb(n, [P, D]) for n in ("wq", "wk", "wv", "wo"))
        if rotary:
            wq_rot, wk_rot = sb("wq_rot", [P, D]), sb("wk_rot", [P, D])
            cos_sin = sb("cos_sin", [P, 2, SEQ])
        else:
            bias_mask = sb("bias_mask", [P, 3])
            v_bias, v_mask = sb("v_bias", [P, D]), sb("v_mask", [P, D])
            wo_bias, ones_row = sb("wo_bias", [1, D]), sb("ones_row", [1, P])

        x_proj = [sb(f"x_proj{i}", [P, SEQ]) for i in range(2)]
        x_res = [sb(f"x_res{i}", [P, SEQ]) for i in range(2)]
        qk_terms = sb("qk_terms", [P, 2, 2, SEQ])
        qk = sb("qk", [P, 2, SEQ])
        qk_rest = sb("qk_rest", [P, 2, SEQ])
        qk_part = sb("qk_part", [P, 3, 2, SEQ], BF16)
        q_stack = [sb(f"q_stack{i}", [P, HEADS, SEQ], BF16) for i in range(RING)]
        k_stack = [sb(f"k_stack{i}", [P, HEADS, SEQ], BF16) for i in range(RING)]
        v_ones = [sb(f"v_ones{i}", [P, 2, HEADS, 32]) for i in range(RING)]
        row_max = [sb(f"row_max{i}", [P, 2, HEADS]) for i in range(2)]
        max_rest = sb("max_rest", [P, 2, HEADS // 2])
        max_part = [sb(f"max_part{i}", [P, 2, 3, HEADS // 2], BF16) for i in range(2)]
        max_rows = [sb(f"max_rows{i}", [24, SEQ], BF16) for i in range(2)]
        prob = [sb(f"prob{i}", [P, 2, 2, SEQ]) for i in range(4)]
        pv_t = sb("pv_t", [P, 2, 8, 32])
        denom = sb("denom", [P, 2, 8, 1])
        heads_t = sb("heads_t", [P, 8, 32])
        o_sb = sb("o_sb", [P, SEQ])
        y_sb = sb("y_sb", [P, 2, D])
        stats, mean_var = sb("stats", [P, 2, 6]), sb("mean_var", [P, 2, 2])
        var_eps, rstd = sb("var_eps", [P, 2]), sb("rstd", [P, 2])
        z_sb = sb("z_sb", [P, 2, D])

        scores_q = [ps(f"scores_q{i}", [P, 2, SEQ]) for i in range(2)]
        scores_k = [ps(f"scores_k{i}", [P, 2, 2, SEQ]) for i in range(2)]
        pv = ps("pv", [P, 2, SEQ])
        misc = ps("misc", [P, 2 * SEQ])
        misc_bf = misc[:, :].bitcast(BF16)

        w_in, consts_made, stacks_clear, weights_made, minus_rows = (
            sem(n) for n in ("w_in", "consts_made", "stacks_clear", "weights_made", "minus_rows"))
        x_proj_in = [sem(f"x_proj_in{i}") for i in range(2)]
        x_res_in = [sem(f"x_res_in{i}") for i in range(2)]
        stack_in = [sem(f"stack_in{i}") for i in range(RING)]
        max_in = [sem(f"max_in{i}") for i in range(2)]
        stored = [sem(f"stored{i}") for i in range(2)]
        qk_done, v_done, sq_done, sk_done, pv_done, maxt_done, y_done, zt_done = (
            sem(n) for n in ("qk_done", "v_done", "sq_done", "sk_done", "pv_done", "maxt_done", "y_done", "zt_done"))
        qk_taken, max_found, pv_turned, inverted, scaled, o_ready, bn_done, mv_done, z_ready = (
            sem(n) for n in ("qk_taken", "max_found", "pv_turned", "inverted", "scaled", "o_ready", "bn_done", "mv_done", "z_ready"))
        ln_step = sem("ln_step")
        exp_done, part1, part2, v_ready, maxt_taken, y_taken, x_written = (
            sem(n) for n in ("exp_done", "part1", "part2", "v_ready", "maxt_taken", "y_taken", "x_written"))
        added, rest_done, part3, max_step, max_split, eps_added, rstd_done = (
            sem(n) for n in ("added", "rest_done", "part3", "max_step", "max_split", "eps_added", "rstd_done"))

        def active(s):
            if not s.known:
                return True, True, True, True
            return tuple(0 <= s.n + ahead < BATCH for ahead in (AHEAD, 1, 0, -1))

        def slots(engine, body):
            for n in range(-AHEAD, RING + 1):
                body(Slot(None, RING, n))
            with engine.Fori(0, LOOPS) as i:
                for offset in range(RING + 1, 2 * RING + 1):
                    body(Slot(i, RING, offset))
            for n in range(RING * LOOPS + RING + 1, BATCH + 1):
                body(Slot(None, RING, n))

        n_weights = 5 if rotary else 10
        n_made = RING + 4
        block = ctx.enter_context(nc.Block())

        @block.sync
        def _(sp):
            for to, of in ((wq, w["wq"]), (wk, w["wk"]), (wv, w["wv"]), (wo, w["wo"])):
                sp.dma_start(to[:, :], of).then_inc(w_in, 16)
            if rotary:
                sp.dma_start(cos_sin[:, :, :], w["cos_sin"]).then_inc(w_in, 16)
            else:
                for c, b in enumerate(("bq", "bk", "mask")):
                    sp.dma_start(bias_mask[:, c:c + 1], w[b]).then_inc(w_in, 16)
                sp.dma_start(v_bias[:, :], w["bv"].to_broadcast([P, D])).then_inc(w_in, 16)
                sp.dma_start(v_mask[:, :], w["mask_v"].to_broadcast([P, D])).then_inc(w_in, 16)
                sp.dma_start(wo_bias[:, :], w["bo"]).then_inc(w_in, 16)

            def slot(s):
                n, j = s.n, s.offset % RING
                a, b1, b3, c = active(s)
                def value(v):
                    return v if s.known else sp.snap(v)

                x_ahead, x_now, x_before = value(n * SEQ + (AHEAD + 1) * SEQ), value(n * SEQ), value(n * SEQ - SEQ)
                v_read, z_made = value(n + AHEAD), value(2 * n)
                max_taken_n, max_taken_next = value(2 * n + 2), value(2 * n + 3)
                parts_made = value(n + AHEAD + 1)
                if s.known and n == -AHEAD:
                    load_x(0, 0)
                if not s.known or n + AHEAD + 1 < BATCH:
                    at_least(sp, v_done, v_read)
                    load_x((j + AHEAD + 1) % 2, x_ahead)
                if b3:
                    if s.known:
                        at_least(sp, y_done, n - 1)
                    sp.dma_start(x_res[j % 2][:, :], src[:, bass.ds(x_now, SEQ)]).then_inc(x_res_in[j % 2], 16)
                    sp.wait_ge(maxt_taken, max_taken_n)
                    sp.dma_start(q_stack[j][MAX_ROW:MAX_ROW + 3, 8:16, :], max_rows[1][:, :]).then_inc(max_in[1], 16)
                if a:
                    sp.wait_ge(part1, parts_made)
                    if s.known and n == -AHEAD:
                        sp.wait_ge(stacks_clear, 2 * RING)
                    stack_part(j, 0)
                if b1:
                    sp.wait_ge(maxt_taken, max_taken_next)
                    sp.dma_start(q_stack[(j + 1) % RING][MAX_ROW:MAX_ROW + 3, 0:8, :],
                                 max_rows[0][:, :]).then_inc(max_in[0], 16)
                if a:
                    sp.wait_ge(part2, parts_made)
                    stack_part(j, 1)
                    sp.wait_ge(part3, parts_made)
                    stack_part(j, 2)
                if c and last:
                    sp.wait_ge(z_ready, z_made)
                    sp.dma_start(out[bass.ds(x_before, SEQ), :].rearrange("(t p) d -> p t d", p=P),
                                 z_sb[:, :, :]).then_inc(stored[0], 16)

            def load_x(buf, at):
                sp.dma_start(x_proj[buf][:, :], src[:, bass.ds(at, SEQ)]).then_inc(x_proj_in[buf], 16)

            def stack_part(j, part):
                ja = (j + AHEAD) % RING
                for which, stack, order in ((0, q_stack[ja], Q_PARTS), (1, k_stack[ja], K_PARTS)):
                    for row, p in enumerate(order):
                        if p == part:
                            sp.dma_start(stack[HD * row:HD * (row + 1), :, :],
                                         qk_part[:, part, which, :]).then_inc(stack_in[ja], 16)

            slots(sp, slot)
            if last:
                sp.wait_ge(stored[0], 16 * BATCH)

        @block.tensor
        def _(pe):
            pe.wait_ge(w_in, 16 * n_weights)
            pe.wait_ge(weights_made, n_made)

            def misc_free(s, a, b1, b3, c, use):
                n = s.n
                order = [("q", a, qk_taken, 2 * (n + AHEAD) + 1), ("maxt1", b3, maxt_taken, 2 * n + 2),
                         ("k", a, qk_taken, 2 * (n + AHEAD) + 2), ("y", c, y_taken, n),
                         ("maxt0", b1, maxt_taken, 2 * (n + 1) + 1), ("v", a, v_ready, n + AHEAD + 1)]
                if not last:
                    order.append(("zt", c, x_written, n))
                k = [o[0] for o in order].index(use)
                for o in reversed(order[:k]):
                    if o[1]:
                        return at_least(pe, o[2], o[3])
                at_least(pe, maxt_taken, 2 * n + 1 if b3 else 0)
                a0, _, b30, c0 = active(Slot(s.i, RING, s.offset - 1))
                if a0:
                    at_least(pe, v_ready, n + AHEAD)
                if c0:
                    at_least(pe, y_taken, n - 1)
                    if not last:
                        at_least(pe, x_written, n - 1)
                elif b30:
                    at_least(pe, maxt_taken, 2 * n)

            def weigh_v(n, j, g):
                pe.wait_ge(exp_done, UNITS * n + 2 * g + 2)
                if g == 0:
                    at_least(pe, v_ready, n + 1)
                if g % 2 == 0:
                    at_least(pe, pv_turned, 2 * n + g // 2)
                for kt in range(2):
                    for r in range(4):
                        h = 4 * g + r
                        mm = nc.tensor.matmul(pv[32 * r:32 * r + 32, g % 2, :], v_ones[j][:, kt, h, :],
                                              prob[(2 * g + r // 2) % 4][:, r % 2, kt, :],
                                              start=(kt == 0), stop=(kt == 1))
                mm.then_inc(pv_done, 1)

            def project(x, first, rot):
                mm = nc.tensor.matmul(misc[:, 0:SEQ], first[:, :], x, start=True, stop=True)
                if rot is not None:
                    mm = nc.tensor.matmul(misc[:, SEQ:2 * SEQ], rot[:, :], x, start=True, stop=True)
                mm.then_inc(qk_done, 1)

            def slot(s):
                n, j = s.n, s.offset % RING
                a, b1, b3, c = active(s)
                ja, jb = (j + AHEAD) % RING, (j + 1) % RING
                for u in range(UNITS):
                    if b1:
                        if u == 0:
                            at_least(pe, stack_in[jb], 16 * STACK_DMAS * s.fills(1, RING))
                        for qt in range(2):
                            at_least(pe, max_found, 2 * UNITS * (n + 1) + 2 * u + qt - 1)
                            for e in range(2):
                                h = 2 * u + e
                                mm = nc.tensor.matmul(scores_q[qt][:, e, :],
                                                      q_stack[jb][0:ROWS_MAX, h, P * qt:P * qt + P],
                                                      k_stack[jb][0:ROWS_MAX, h, :], start=True, stop=True)
                            mm.then_inc(sq_done, 1)
                    if u == 0 and a:
                        pe.wait_ge(x_proj_in[ja % 2], 16 * s.fills(AHEAD, 2))
                        misc_free(s, a, b1, b3, c, "q")
                        project(x_proj[ja % 2][:, :], wq, wq_rot if rotary else None)
                    if b3:
                        if u == 0 and s.known and n < RING:
                            pe.wait_ge(minus_rows, n + 1)
                        if u % 4 == 0:
                            pe.wait_ge(max_in[u // 4], 16 * (n + 1))
                        at_least(pe, exp_done, UNITS * n + u - 1)
                        for e in range(2):
                            for kt in range(2):
                                h = 2 * u + e
                                mm = nc.tensor.matmul(scores_k[u % 2][:, e, kt, :],
                                                      k_stack[j][0:ROWS_PROB, h, P * kt:P * kt + P],
                                                      q_stack[j][0:ROWS_PROB, h, :], start=True, stop=True)
                        mm.then_inc(sk_done, 1)
                    if u == 1 and b3:
                        turn_max(s, a, b1, b3, c, 1, n)
                    if u == 1 and c:
                        weigh_v(n - 1, (j - 1) % RING, 3)
                    if u in (3, 5, 7) and b3:
                        if u == 5 and b1:
                            turn_max(s, a, b1, b3, c, 0, n + 1)
                        weigh_v(n, j, u // 2 - 1)
                    if u == 2 and a:
                        misc_free(s, a, b1, b3, c, "k")
                        project(x_proj[ja % 2][:, :], wk, wk_rot if rotary else None)
                    if u == 4 and c:
                        misc_free(s, a, b1, b3, c, "y")
                        pe.wait_ge(o_ready, n)
                        jr = (j - 1) % 2
                        pe.wait_ge(x_res_in[jr], 16 * s.fills(-1, 2))
                        for t in range(2):
                            ts, y = slice(P * t, P * t + P), misc[:, D * t:D * t + D]
                            nc.tensor.matmul(y, o_sb[:, ts], wo[:, :], start=True, stop=False)
                            if not rotary:
                                nc.tensor.matmul(y, ones_row[:, :], wo_bias[:, :], start=False, stop=False)
                            mm = nc.tensor.matmul(y, x_res[jr][:, ts], ident[:, :], start=False, stop=True)
                        mm.then_inc(y_done, 1)
                    if u == 6 and a:
                        misc_free(s, a, b1, b3, c, "v")
                        for kt in range(2):
                            mm = nc.tensor.matmul(misc[:, D * kt:D * kt + D], x_proj[ja % 2][:, P * kt:P * kt + P],
                                                  wv[:, :], start=True, stop=True)
                        mm.then_inc(v_done, 1)
                    if u == 5 and b1 and not b3:
                        turn_max(s, a, b1, b3, c, 0, n + 1)
                    if u == 7 and c and not last:
                        misc_free(s, a, b1, b3, c, "zt")
                        pe.wait_ge(z_ready, 2 * n)
                        for t in range(2):
                            mm = nc.tensor.transpose(misc[:, P * t:P * t + P], z_sb[:, t, :], ident[:, :])
                        mm.then_inc(zt_done, 1)

            def turn_max(s, a, b1, b3, c, half, batch):
                misc_free(s, a, b1, b3, c, f"maxt{half}")
                pe.wait_ge(max_split, 2 * batch + half + 1)
                for qt in range(2):
                    mm = nc.tensor.transpose(misc_bf[0:24, P * qt:P * qt + P],
                                             max_part[half][:, qt, :, :].rearrange("p a h -> p (a h)"), ident_bf[:, :])
                mm.then_inc(maxt_done, 1)

            slots(pe, slot)

        @block.vector
        def _(dve):
            def made(ins, value):
                ins.then_inc(consts_made, 1)
                dve.wait_ge(consts_made, value)

            for v in v_ones:
                nc.vector.memset(v[:, :, :, :], 0.0).then_inc(consts_made, 1)
            nc.vector.memset(heads_t[:, :, :], 0.0).then_inc(consts_made, 1)
            nc.vector.memset(stats[:, :, :], 0.0).then_inc(consts_made, 1)
            dve.wait_ge(consts_made, RING + 2)
            for v in v_ones:
                nc.vector.memset(v[:, :, :, HD:HD + 1], 1.0).then_inc(weights_made, 1)
            dve.wait_ge(w_in, 16 * n_weights)
            if rotary:
                for w_plain, w_rot in ((wq, wq_rot), (wk, wk_rot)):
                    plain = w_plain[:, :].rearrange("p (i e h) -> p i e h", e=2, h=HEADS)
                    rot = w_rot[:, :].rearrange("p (i e h) -> p i e h", e=2, h=HEADS)
                    nc.vector.tensor_scalar(rot[:, :, 0, :], plain[:, :, 1, :], -1.0, None, ALU.mult).then_inc(weights_made, 1)
                    nc.vector.tensor_copy(rot[:, :, 1, :], plain[:, :, 0, :]).then_inc(weights_made, 1)
            else:
                nc.vector.tensor_scalar(bias_mask[:, 0:2], bias_mask[:, 0:2], bias_mask[:, 2:3], None, ALU.mult).then_inc(weights_made, 1)
                nc.vector.tensor_tensor(wv[:, :], wv[:, :], v_mask[:, :], ALU.mult).then_inc(weights_made, 1)
                nc.vector.tensor_tensor(v_bias[:, :], v_bias[:, :], v_mask[:, :], ALU.mult).then_inc(weights_made, 1)
                nc.vector.memset(ones_row[:, :], 1.0).then_inc(weights_made, 1)
            dve.wait_ge(weights_made, n_made)

            def normalise_heads(m, half):
                at_least(dve, scaled, 2 * m + half)
                dve.wait_ge(pv_done, 4 * m + 2 * half + 2)
                nc.vector.transpose(pv_t[:, :, :, :].rearrange("p g c x -> p (g c x)"),
                                    pv[:, :, :].rearrange("p g q -> p (g q)")).then_inc(pv_turned, 1)
                dve.wait_ge(pv_turned, 2 * m + half + 1)
                nc.vector.reciprocal(denom[:, :, :, :], pv_t[:, :, :, HD:HD + 1]).then_inc(inverted, 1)
                dve.wait_ge(inverted, 2 * m + half + 1)
                dst = heads_t[:, :, :].rearrange("p c (g d) -> p g c d", d=HD)
                nc.vector.tensor_tensor(dst[:, 2 * half:2 * half + 2, :, :], pv_t[:, :, :, 0:HD],
                                        denom[:, :, :, :].to_broadcast([P, 2, 8, HD]), ALU.mult).then_inc(scaled, 1)
                if half == 1:
                    dve.wait_ge(scaled, 2 * m + 2)
                    at_least(dve, y_done, m)
                    nc.vector.transpose(o_sb[:, :], heads_t[:, :, :].rearrange("p c x -> p (c x)")).then_inc(o_ready, 1)

            def take_qk(n, which):
                dve.wait_ge(qk_done, 2 * (n + AHEAD) + 1 + which)
                at_least(dve, added, n + AHEAD)
                nc.vector.tensor_tensor(qk_terms[:, which, :, :], misc[:, :].rearrange("p (e t) -> p e t", e=2),
                                        cos_sin[:, :, :], ALU.mult).then_inc(qk_taken, 1)

            def slot(s):
                n, j = s.n, s.offset % RING
                a, b1, b3, c = active(s)
                jb = (j + 1) % RING
                for u in range(UNITS):
                    if b1:
                        for qt in range(2):
                            if u == 0 and qt == 0:
                                at_least(dve, max_split, 2 * n)
                            dve.wait_ge(sq_done, 2 * UNITS * (n + 1) + 2 * u + qt + 1)
                            nc.vector.tensor_reduce(row_max[jb % 2][:, qt, 2 * u:2 * u + 2], scores_q[qt][:, :, :],
                                                    AX.X, ALU.max).then_inc(max_found, 1)
                    if u == 0 and a and rotary:
                        take_qk(n, 0)
                    if u == 2 and a and rotary:
                        take_qk(n, 1)
                    if u == 2 and c:
                        normalise_heads(n - 1, 1)
                    if u == 6 and b3:
                        normalise_heads(n, 0)
                    if u == 5 and c:
                        dve.wait_ge(y_taken, n)
                        for t in range(2):
                            nc.vector.bn_stats(stats[:, t, :], y_sb[:, t, :]).then_inc(bn_done, 1)
                        dve.wait_ge(bn_done, 2 * n)
                        at_least(dve, rstd_done, n - 1)
                        dve.sem_inc(ln_step, 1)
                        for t in range(2):
                            nc.vector.bn_aggr(mean_var[:, t, :], stats[:, t, :]).then_inc(mv_done, 1)
                    if u == 6 and a and not rotary:
                        ja = (j + AHEAD) % RING
                        dve.wait_ge(v_done, n + AHEAD + 1)
                        at_least(dve, pv_done, 4 * n)
                        nc.vector.tensor_tensor(v_ones[ja][:, :, :, 0:HD],
                                                misc[:, 0:2 * D].rearrange("p (k h d) -> p k h d", k=2, d=HD),
                                                v_bias[:, :].rearrange("p (k h d) -> p k h d", k=1, d=HD)
                                                .to_broadcast([P, 2, HEADS, HD]), ALU.add).then_inc(v_ready, 1)
                    if u == 6 and c:
                        dve.wait_ge(rstd_done, n)
                        if last:
                            at_least(dve, stored[0], 16 * (n - 1))
                        else:
                            at_least(dve, zt_done, n - 1)
                        for t in range(2):
                            nc.vector.tensor_scalar(z_sb[:, t, :], y_sb[:, t, :], mean_var[:, t, 0:1],
                                                    rstd[:, t:t + 1], ALU.subtract, ALU.mult).then_inc(z_ready, 1)
                if s.known and n + AHEAD < RING:
                    nc.vector.memset(k_stack[n + AHEAD][MAX_ROW:MAX_ROW + 3, :, :], -1.0).then_inc(minus_rows, 1)

            slots(dve, slot)

        @block.scalar
        def _(act):
            act.wait_ge(weights_made, n_made)

            def slot(s):
                n, j = s.n, s.offset % RING
                a, b1, b3, c = active(s)
                for u in range(UNITS):
                    if u == 0 and a and not rotary:
                        take_qk(n, 0)
                    if b3:
                        act.wait_ge(sk_done, UNITS * n + u + 1)
                        at_least(act, pv_done, 4 * n + u // 2 - 1)
                        nc.scalar.activation(prob[u % 4][:, :, :, :], scores_k[u % 2][:, :, :, :], ACT.Exp,
                                             scale=float(HD) ** -0.5).then_inc(exp_done, 1)
                    if u == 1 and b3:
                        take_max(n, 1)
                    if u == 2 and a and not rotary:
                        take_qk(n, 1)
                    if u == 4 and c:
                        act.wait_ge(y_done, n)
                        at_least(act, z_ready, 2 * (n - 1))
                        nc.scalar.copy(y_sb[:, :, :], misc[:, 0:2 * D].rearrange("p (t d) -> p t d", t=2)).then_inc(y_taken, 1)
                    if u == 3 and a:
                        act.wait_ge(added if rotary else qk_taken, (n + AHEAD + 1) * (1 if rotary else 2))
                        if not s.known or n + AHEAD > 0:
                            act.wait_ge(stack_in[(j + AHEAD - 1) % RING], 16 * STACK_DMAS * s.fills(AHEAD - 1, RING))
                        nc.scalar.copy(qk_part[:, 0, :, :], qk[:, :, :]).then_inc(part1, 1)
                    if u == 6 and a and rotary:
                        ja = (j + AHEAD) % RING
                        act.wait_ge(v_done, n + AHEAD + 1)
                        at_least(act, pv_done, 4 * n)
                        nc.scalar.copy(v_ones[ja][:, :, :, 0:HD],
                                       misc[:, 0:2 * D].rearrange("p (k h d) -> p k h d", k=2, d=HD)).then_inc(v_ready, 1)
                    if u == 5 and b1:
                        take_max(n + 1, 0)
                    if u == 5 and a:
                        act.wait_ge(rest_done, n + AHEAD + 1)
                        nc.scalar.copy(qk_part[:, 1, :, :], qk_rest[:, :, :]).then_inc(part2, 1)
                    if u == 7 and c and not last:
                        act.wait_ge(zt_done, n)
                        nc.scalar.copy(xT[:, bass.ds((n - 1) * SEQ, SEQ)], misc[:, 0:SEQ]).then_inc(x_written, 1)

            def take_qk(n, which):
                act.wait_ge(qk_done, 2 * (n + AHEAD) + 1 + which)
                at_least(act, rest_done, n + AHEAD)
                nc.scalar.activation(qk[:, which, :], misc[:, 0:SEQ], ACT.Identity, bias=bias_mask[:, which:which + 1],
                                     scale=bias_mask[:, 2:3]).then_inc(qk_taken, 1)

            def take_max(batch, half):
                act.wait_ge(maxt_done, 2 * batch + half + 1)
                at_least(act, max_in[half], 16 * batch)
                nc.scalar.copy(max_rows[half][:, :], misc_bf[0:24, 0:SEQ]).then_inc(maxt_taken, 1)

            slots(act, slot)

        @block.gpsimd
        def _(pool):
            for stack in (q_stack[0], k_stack[0], *q_stack[1:], *k_stack[1:]):
                nc.gpsimd.memset(stack[0:MAX_ROW, :, :].rearrange("p h t -> p (h t)").bitcast(F32), 0.0).then_inc(stacks_clear, 1)
            pool.wait_ge(w_in, 16 * n_weights)
            pool.wait_ge(weights_made, n_made)
            zeros = consts["zeros"][:, 0:HEADS].rearrange("p (a b) -> p a b", a=2)

            def split_max(batch, j, half):
                hs = slice(8 * half, 8 * half + 8)
                m, part = row_max[j % 2], max_part[half]
                pool.wait_ge(max_found, 2 * UNITS * batch + 8 * half + 8)
                at_least(pool, maxt_done, 2 * (batch - 1) + half + 1)
                steps = 3 * (2 * batch + half)
                nc.gpsimd.tensor_tensor(part[:, :, 0, :], m[:, :, hs], zeros, ALU.add).then_inc(max_step, 1)
                pool.wait_ge(max_step, steps + 1)
                nc.gpsimd.tensor_tensor(max_rest[:, :, :], m[:, :, hs], part[:, :, 0, :], ALU.subtract).then_inc(max_step, 1)
                pool.wait_ge(max_step, steps + 2)
                nc.gpsimd.tensor_tensor(part[:, :, 1, :], max_rest[:, :, :], zeros, ALU.add).then_inc(max_step, 1)
                pool.wait_ge(max_step, steps + 3)
                nc.gpsimd.tensor_tensor(part[:, :, 2, :], max_rest[:, :, :], part[:, :, 1, :],
                                        ALU.subtract).then_inc(max_split, 1)

            def slot(s):
                n, j = s.n, s.offset % RING
                a, b1, b3, c = active(s)
                if b3:
                    split_max(n, j, 1)
                if a:
                    if rotary:
                        pool.wait_ge(qk_taken, 2 * (n + AHEAD) + 2)
                        at_least(pool, part1, n + AHEAD)
                        nc.gpsimd.tensor_tensor(qk[:, :, :], qk_terms[:, :, 0, :], qk_terms[:, :, 1, :],
                                                ALU.add).then_inc(added, 1)
                        pool.wait_ge(added, n + AHEAD + 1)
                    pool.wait_ge(part1, n + AHEAD + 1)
                    at_least(pool, part2, n + AHEAD)
                    nc.gpsimd.tensor_tensor(qk_rest[:, :, :], qk[:, :, :], qk_part[:, 0, :, :],
                                            ALU.subtract).then_inc(rest_done, 1)
                if b1:
                    split_max(n + 1, j + 1, 0)
                if c:
                    pool.wait_ge(mv_done, 2 * n)
                    at_least(pool, z_ready, 2 * (n - 1))
                    nc.gpsimd.tensor_tensor(var_eps[:, :], mean_var[:, :, 1], consts["eps"][:, 0:2], ALU.add).then_inc(eps_added, 1)
                    pool.wait_ge(eps_added, n)
                    nc.gpsimd.tensor_tensor(rstd[:, :], var_eps[:, :], consts["minus_half"][:, 0:2], ALU.pow).then_inc(rstd_done, 1)
                if a:
                    pool.wait_ge(part2, n + AHEAD + 1)
                    nc.gpsimd.tensor_tensor(qk_part[:, 2, :, :], qk_rest[:, :, :], qk_part[:, 1, :, :],
                                            ALU.subtract).then_inc(part3, 1)

            slots(pool, slot)



CHUNK = 512
CHUNKS = TOKENS // CHUNK
CT = CHUNK // P
HID = 512
HB = HID // P


class Normaliser:

    def __init__(self, name, sb, sem, consts, tiles):
        self.tiles, self.consts = tiles, consts
        self.stats, self.mean_var = sb("stats", [P, tiles, 6]), sb("mean_var", [P, tiles, 2])
        self.var_eps, self.rstd = sb("var_eps", [P, tiles]), sb("rstd", [P, tiles])
        self.z = sb("z", [P, tiles, D])
        self.bn_done, self.mv_done, self.ln_step, self.eps_added, self.rstd_done, self.z_ready = (
            sem(n) for n in ("bn_done", "mv_done", "ln_step", "eps_added", "rstd_done", "z_ready"))


def ffn(nc, name, xT, out, consts, w, last):
    with ExitStack() as ctx:
        def sb(n, shape, dt=F32):
            return ctx.enter_context(nc.sbuf_tensor(f"{name}_{n}", shape, dt))

        def ps(n, shape, dt=F32):
            return ctx.enter_context(nc.psum_tensor(f"{name}_{n}", shape, dt))

        sems = phase_semaphores(nc, ctx)

        def sem(n):
            sems.append(nc.alloc_semaphore(f"{name}_{n}"))
            return sems[-1]

        ident = consts["ident"]
        w1, w2 = sb("w1", [P, HID]), sb("w2", [P, HID])
        h1, h2 = sb("h1", [P, HB, HID]), sb("h2", [P, HB, HID])
        w3, s3 = sb("w3", [P, HB, D]), sb("s3", [P, D])
        scales = sb("scales", [P, 4, HB])
        s1_half, s12_half = sb("s1_half", [P, HB]), sb("s12_half", [P, HB])

        w1_parts, w2_parts = sb("w1_parts", [P, 2, HID], F32R), sb("w2_parts", [P, 2, HID], F32R)
        h1_parts, h2_parts = sb("h1_parts", [P, 2, HB, HID], F32R), sb("h2_parts", [P, 2, HB, HID], F32R)

        x_up = sb("x_up", [P, CHUNK])
        x_parts = sb("x_parts", [P, 2, CHUNK], F32R)
        x_res = sb("x_res", [P, CHUNK])
        tanh = [sb(f"tanh{i}", [P, CHUNK]) for i in range(2)]
        gated = [sb(f"gated{i}", [P, CHUNK]) for i in range(2)]
        whole = [sb(f"whole{i}", [P, CHUNK]) for i in range(4)]
        hid0, hid1 = (sb(f"hid{i}", [P, 2, HB, CHUNK], F32R) for i in range(2))
        hid2 = sb("hid2", [P, HB, CHUNK])
        y_sb = sb("y_sb", [P, CT, D])
        ln = Normaliser(name, sb, sem, consts, CT)

        ps1 = [ps(f"ps1_{i}", [P, CHUNK]) for i in range(2)]
        ps2 = [ps(f"ps2_{i}", [P, CHUNK]) for i in range(2)]
        psh = [ps(f"psh_{i}", [P, CHUNK]) for i in range(2)]
        psy, psz = ps("psy", [P, CT, D]), ps("psz", [P, CHUNK])

        h_in = sem("h_in")
        w_in, x_up_in, x_res_in, stored = (sem(n) for n in ("w_in", "x_up_in", "x_res_in", "stored"))
        up_done, hid_done, y_done, zt_done = (sem(n) for n in ("up_done", "hid_done", "y_done", "zt_done"))
        scales_made, gate_done, hid0_whole, hid0_hi, hid0_ready = (
            sem(n) for n in ("scales_made", "gate_done", "hid0_whole", "hid0_hi", "hid0_ready"))
        weights_hi, weights_split, x_hi, x_split, gelu_whole, rest_done = (
            sem(n) for n in ("weights_hi", "weights_split", "x_hi", "x_split", "gelu_whole", "rest_done"))
        tanh_done, gelu_done, y_taken, x_written = (sem(n) for n in ("tanh_done", "gelu_done", "y_taken", "x_written"))

        def active(s):
            if not s.known:
                return True, True, True
            return tuple(0 <= s.n + ahead < CHUNKS for ahead in (1, 0, -1))

        def slots(engine, body):
            for n in (-1, 0, 1):
                body(Slot(None, 1, n))
            with engine.Fori(0, CHUNKS - 3) as i:
                body(Slot(i, 1, 2))
            for n in (CHUNKS - 1, CHUNKS):
                body(Slot(None, 1, n))

        weights = [(w1[:, :], w1_parts), (w2[:, :], w2_parts), (h1[:, :, :], h1_parts), (h2[:, :, :], h2_parts)]
        block = ctx.enter_context(nc.Block())

        @block.sync
        def _(sp):
            loads = [(w1[:, :], w["w1"]), (w2[:, :], w["w2"]), (w3[:, :, :], w["w3"].rearrange("(b p) n -> p b n", p=P)),
                     (scales[:, :, :], w["scales"]), (s3[:, :], w["s3"].to_broadcast([P, D]))]
            for dst, src in loads:
                sp.dma_start(dst, src).then_inc(w_in, 16)
            for dst, src in ((h1, w["h1"]), (h2, w["h2"])):
                sp.dma_start(dst[:, :, :], src.rearrange("(b p) n -> p b n", p=P)).then_inc(h_in, 16)

            def slot(s):
                n = s.n
                up, mid, end = active(s)

                def value(v):
                    return v if s.known else sp.snap(v)

                at_up, at_res, at_out = value(n * CHUNK + CHUNK), value(n * CHUNK - CHUNK), value(n * CHUNK - CHUNK)
                up_read, y_read, z_made = value(n + 1), value(n - 1), value(CT * n)
                if up:
                    at_least(sp, x_split, up_read)
                    sp.dma_start(x_up[:, :], xT[:, bass.ds(at_up, CHUNK)]).then_inc(x_up_in, 16)
                if end:
                    at_least(sp, y_done, y_read)
                    sp.dma_start(x_res[:, :], xT[:, bass.ds(at_res, CHUNK)]).then_inc(x_res_in, 16)
                    if last:
                        sp.wait_ge(ln.z_ready, z_made)
                        sp.dma_start(out[bass.ds(at_out, CHUNK), :].rearrange("(t p) d -> p t d", p=P),
                                     ln.z[:, :, :]).then_inc(stored, 16)

            slots(sp, slot)
            if last:
                sp.wait_ge(stored, 16 * CHUNKS)

        @block.tensor
        def _(pe):
            pe.wait_ge(weights_split, 2)

            def layer(n, weights, source, first):
                for m in range(HB):
                    at_least(pe, gelu_done, first + m - 1)
                    for k in range(HB):
                        mm = split_matmul(nc, psh[m % 2][:, :], lambda a: weights[:, a, k, P * m:P * m + P],
                                          lambda b: source[:, b, k, :], k == 0, k == HB - 1)
                    mm.then_inc(hid_done, 1)

            def slot(s):
                n = s.n
                up, mid, end = active(s)
                if s.known and n == 0:
                    pe.wait_ge(weights_split, len(weights))
                if mid:
                    pe.wait_ge(hid0_ready, HB * (n + 1))
                    layer(n, h1_parts, hid0, 2 * HB * n)
                if end:
                    pe.wait_ge(gelu_done, 2 * HB * n)
                    at_least(pe, y_taken, n - 1)
                    pe.wait_ge(x_res_in, 16 * n)
                    for t in range(CT):
                        for k in range(HB):
                            nc.tensor.matmul(psy[:, t, :], hid2[:, k, P * t:P * t + P], w3[:, k, :],
                                             start=(k == 0), stop=False)
                        mm = nc.tensor.matmul(psy[:, t, :], x_res[:, P * t:P * t + P], ident[:, :], start=False, stop=True)
                    mm.then_inc(y_done, 1)
                if up:
                    pe.wait_ge(x_split, n + 2)
                    for m in range(HB):
                        at_least(pe, hid0_whole, HB * (n + 1) + m - 1)
                        for bank, parts in ((ps1[m % 2], w1_parts), (ps2[m % 2], w2_parts)):
                            split_matmul(nc, bank[:, :], lambda a: parts[:, a, P * m:P * m + P],
                                         lambda b: x_parts[:, b, :], True, True).then_inc(up_done, 1)
                if end and not last:
                    pe.wait_ge(ln.z_ready, CT * n)
                    at_least(pe, x_written, n - 1)
                    for t in range(CT):
                        mm = nc.tensor.transpose(psz[:, P * t:P * t + P], ln.z[:, t, :], ident[:, :])
                    mm.then_inc(zt_done, 1)
                if mid:
                    pe.wait_ge(rest_done, HB * (n + 1))
                    layer(n, h2_parts, hid1, 2 * HB * n + HB)

            slots(pe, slot)

        @block.scalar
        def _(act):
            act.wait_ge(w_in, 16 * 5)
            act.wait_ge(scales_made, 3 + HB)

            def round_weights(some):
                for weight, parts in some:
                    nc.scalar.copy(parts[:, 0], weight).then_inc(weights_hi, 1)

            round_weights(weights[:2])

            def gelus(n, which):
                for m in range(HB):
                    act.wait_ge(hid_done, 2 * HB * n + HB * which + m + 1)
                    if m == 0 and which == 1:
                        at_least(act, y_done, n)
                    if m == 0 and which == 0:
                        at_least(act, hid_done, 2 * HB * n)
                    bank, scale = psh[m % 2][:, :], scales[:, 2 + which, m:m + 1]
                    if which == 0:
                        at_least(act, rest_done, HB * n + m - 1)
                        nc.scalar.activation(whole[m % 2][:, :], bank, ACT.Gelu, scale=scale).then_inc(gelu_whole, 1)
                        nc.scalar.activation(hid1[:, 0, m, :], bank, ACT.Gelu, scale=scale).then_inc(gelu_done, 1)
                    else:
                        nc.scalar.activation(hid2[:, m, :], bank, ACT.Gelu, scale=scale).then_inc(gelu_done, 1)

            def round_hid0(n, m):
                act.wait_ge(hid0_whole, HB * (n + 1) + m + 1)
                if m == 0:
                    at_least(act, hid_done, 2 * HB * n + HB)
                nc.scalar.copy(hid0[:, 0, m, :], whole[2 + m % 2][:, :]).then_inc(hid0_hi, 1)

            def slot(s):
                n = s.n
                up, mid, end = active(s)
                if s.known and n == 0:
                    act.wait_ge(h_in, 32)
                    round_weights(weights[2:])
                if up:
                    act.wait_ge(x_up_in, 16 * (n + 2))
                    at_least(act, up_done, 2 * HB * (n + 1))
                    nc.scalar.copy(x_parts[:, 0, :], x_up[:, :]).then_inc(x_hi, 1)
                if mid:
                    gelus(n, 0)
                if end:
                    act.wait_ge(y_done, n)
                    at_least(act, ln.z_ready, CT * (n - 1))
                    nc.scalar.copy(y_sb[:, :, :], psy[:, :, :]).then_inc(y_taken, 1)
                if up:
                    for m in range(HB):
                        act.wait_ge(up_done, 2 * HB * (n + 1) + 2 * m + 1)
                        at_least(act, gate_done, HB * (n + 1) + m - 1)
                        nc.scalar.activation(tanh[m % 2][:, :], ps1[m % 2][:, :], ACT.Tanh,
                                             scale=s1_half[:, m:m + 1]).then_inc(tanh_done, 1)
                        if m > 0:
                            round_hid0(n, m - 1)
                    round_hid0(n, HB - 1)
                if end and not last:
                    act.wait_ge(zt_done, n)
                    nc.scalar.copy(xT[:, bass.ds((n - 1) * CHUNK, CHUNK)], psz[:, :]).then_inc(x_written, 1)
                if mid:
                    gelus(n, 1)

            slots(act, slot)

        @block.vector
        def _(dve):
            dve.wait_ge(w_in, 16 * 5)
            nc.vector.tensor_scalar(s1_half[:, :], scales[:, 0, :], 0.5, None, ALU.mult).then_inc(scales_made, 1)
            for b in range(HB):
                nc.vector.tensor_tensor(w3[:, b, :], w3[:, b, :], s3[:, :], ALU.mult).then_inc(scales_made, 1)
            dve.wait_ge(scales_made, 1 + HB)
            nc.vector.tensor_tensor(s12_half[:, :], s1_half[:, :], scales[:, 1, :], ALU.mult).then_inc(scales_made, 2)
            dve.wait_ge(scales_made, 3 + HB)

            def rest_of_weights(first, end):
                for i in range(first, end):
                    dve.wait_ge(weights_hi, i + 1)
                    write_rest(nc, weights[i][1][:, 1], weights[i][0], weights[i][1][:, 0]).then_inc(weights_split, 1)

            rest_of_weights(0, 2)

            def rests_of_hid1(n):
                for m in range(HB):
                    dve.wait_ge(gelu_done, 2 * HB * n + m + 1)
                    write_rest(nc, hid1[:, 1, m, :], whole[m % 2][:, :], hid1[:, 0, m, :]).then_inc(rest_done, 1)

            def rest_of_hid0(n, m):
                dve.wait_ge(hid0_hi, HB * (n + 1) + m + 1)
                write_rest(nc, hid0[:, 1, m, :], whole[2 + m % 2][:, :], hid0[:, 0, m, :]).then_inc(hid0_ready, 1)

            def slot(s):
                n = s.n
                up, mid, end = active(s)
                if s.known and n == 0:
                    dve.wait_ge(h_in, 32)
                    rest_of_weights(2, 4)
                if up:
                    dve.wait_ge(x_hi, n + 2)
                    write_rest(nc, x_parts[:, 1, :], x_up[:, :], x_parts[:, 0, :]).then_inc(x_split, 1)
                if mid:
                    rests_of_hid1(n)
                if end:
                    norm_stats(nc, dve, ln, y_sb, y_taken, n)
                if up:
                    for m in range(HB):
                        dve.wait_ge(tanh_done, HB * (n + 1) + m + 1)
                        nc.vector.scalar_tensor_tensor(gated[m % 2][:, :], tanh[m % 2][:, :], 1.0, ps1[m % 2][:, :],
                                                       ALU.add, ALU.mult).then_inc(gate_done, 1)
                        dve.wait_ge(up_done, 2 * HB * (n + 1) + 2 * m + 2)
                        dve.wait_ge(gate_done, HB * (n + 1) + m + 1)
                        nc.vector.scalar_tensor_tensor(whole[2 + m % 2][:, :], gated[m % 2][:, :], s12_half[:, m:m + 1],
                                                       ps2[m % 2][:, :], ALU.mult, ALU.mult).then_inc(hid0_whole, 1)
                        if m > 0:
                            rest_of_hid0(n, m - 1)
                        if m == 1 and end:
                            norm_apply(nc, dve, ln, y_sb, n, stored if last else zt_done, 16 if last else 1)
                    rest_of_hid0(n, HB - 1)
                elif end:
                    norm_apply(nc, dve, ln, y_sb, n, stored if last else zt_done, 16 if last else 1)

            slots(dve, slot)

        @block.gpsimd
        def _(pool):
            def slot(s):
                if active(s)[2]:
                    norm_rstd(nc, pool, ln, s.n)

            slots(pool, slot)


def norm_stats(nc, dve, ln, y, y_ready, n, per=1):
    dve.wait_ge(y_ready, per * n)
    for t in range(ln.tiles):
        nc.vector.bn_stats(ln.stats[:, t, :], y[:, t, :]).then_inc(ln.bn_done, 1)
    at_least(dve, ln.rstd_done, n - 1)
    dve.wait_ge(ln.bn_done, ln.tiles * n)
    dve.sem_inc(ln.ln_step, 1)
    for t in range(ln.tiles):
        nc.vector.bn_aggr(ln.mean_var[:, t, :], ln.stats[:, t, :]).then_inc(ln.mv_done, 1)


def norm_rstd(nc, pool, ln, n):
    pool.wait_ge(ln.mv_done, ln.tiles * n)
    at_least(pool, ln.z_ready, ln.tiles * (n - 1))
    nc.gpsimd.tensor_tensor(ln.var_eps[:, :], ln.mean_var[:, :, 1], ln.consts["eps"][:, 0:ln.tiles],
                            ALU.add).then_inc(ln.eps_added, 1)
    pool.wait_ge(ln.eps_added, n)
    nc.gpsimd.tensor_tensor(ln.rstd[:, :], ln.var_eps[:, :], ln.consts["minus_half"][:, 0:ln.tiles],
                            ALU.pow).then_inc(ln.rstd_done, 1)


def norm_apply(nc, dve, ln, y, n, z_read, per):
    dve.wait_ge(ln.rstd_done, n)
    at_least(dve, z_read, per * (n - 1))
    for t in range(ln.tiles):
        nc.vector.tensor_scalar(ln.z[:, t, :], y[:, t, :], ln.mean_var[:, t, 0:1], ln.rstd[:, t:t + 1],
                                ALU.subtract, ALU.mult).then_inc(ln.z_ready, 1)


GATED = 341
GB = -(-GATED // P)
HALF = D // 2


def gated_ffn(nc, name, x1T, xT, out, consts, w, last):
    with ExitStack() as ctx:
        def sb(n, shape, dt=F32):
            return ctx.enter_context(nc.sbuf_tensor(f"{name}_{n}", shape, dt))

        def ps(n, shape, dt=F32):
            return ctx.enter_context(nc.psum_tensor(f"{name}_{n}", shape, dt))

        sems = phase_semaphores(nc, ctx)

        def sem(n):
            sems.append(nc.alloc_semaphore(f"{name}_{n}"))
            return sems[-1]

        ident = consts["ident"]
        w1 = sb("w1", [P, 2, GB, P])
        w2 = sb("w2", [P, GB, D])
        b1 = sb("b1", [P, 2, GB])
        gain_offset, b2 = sb("gain_offset", [P, 2]), sb("b2", [P, 1])
        w1_parts, w2_parts = sb("w1_parts", [P, 2, 2, GB, P], F32R), sb("w2_parts", [P, 2, GB, D], F32R)

        shifted = sb("shifted", [P, CT // 2, SEQ])
        x1_res, x_res = sb("x1_res", [P, CHUNK]), sb("x_res", [P, CHUNK])
        normed = sb("normed", [P, CHUNK])
        normed_parts = [sb(f"normed_parts{i}", [P, 2, CHUNK], F32R) for i in range(2)]
        gate = [sb(f"gate{i}", [P, CHUNK]) for i in range(2)]
        whole = [sb(f"whole{i}", [P, CHUNK]) for i in range(GB)]
        hid_parts = sb("hid_parts", [P, 2, GB, CHUNK], F32R)
        ln = Normaliser(name, sb, sem, consts, CT)
        if last:
            both_res, sum_sb = sb("both_res", [P, CHUNK]), sb("sum_sb", [P, CHUNK])
            psy = ps("psy", [P, CT, D])
            ln_out = Normaliser(name, lambda n, shape: sb("out_" + n, shape), lambda n: sem("out_" + n), consts, CT)

        psa = [ps(f"psa{i}", [P, CHUNK]) for i in range(2)]
        psg = [ps(f"psg{i}", [P, CHUNK]) for i in range(2)]
        pst, psz, pso = ps("pst", [P, CT, D]), ps("psz", [P, CHUNK]), ps("pso", [P, CHUNK])

        w_in, shifted_in, res_in, stored = (sem(n) for n in ("w_in", "shifted_in", "res_in", "stored"))
        t_done, zt_done, up_done, out_done = (sem(n) for n in ("t_done", "zt_done", "up_done", "out_done"))
        ready, hid_ready = sem("ready"), sem("hid_ready")
        normed_ready, gate_done, out_taken = (sem(n) for n in ("normed_ready", "gate_done", "out_taken"))
        weights_hi, weights_split, normed_whole, normed_split, hid_whole, hid_hi, both_added, turned_out = (
            sem(n) for n in ("weights_hi", "weights_split", "normed_whole", "normed_split", "hid_whole", "hid_hi",
                             "both_added", "turned_out"))

        def active(s):
            if not s.known:
                return True, True, True, True
            return tuple(0 <= s.n + ahead < CHUNKS for ahead in (2, 1, 0, -1))

        def slots(engine, body):
            for n in range(-2, 2):
                body(Slot(None, 2, n))
            with engine.Fori(0, CHUNKS // 2 - 2) as i:
                for offset in (2, 3):
                    body(Slot(i, 2, offset))
            for n in range(CHUNKS - 2, CHUNKS + 1):
                body(Slot(None, 2, n))

        def of_buffer_before(n, m):
            return GB * n + (m - 1 if m >= 2 else 0)

        n_loads = 5
        res_loads = 2 if last else 1
        block = ctx.enter_context(nc.Block())

        @block.sync
        def _(sp):
            loads = [(w1[:, :, :, :], w["w1"].rearrange("p (e b n) -> p e b n", e=2, b=GB)),
                     (w2[:, :, :], w["w2"].rearrange("(b p) n -> p b n", p=P)), (b1[:, :, :], w["b1"]),
                     (gain_offset[:, :], w["gain_offset"]), (b2[:, :], w["b2"])]
            for dst, src in loads:
                sp.dma_start(dst, src).then_inc(w_in, 16)
            sp.wait_ge(ready, 1)

            def slot(s):
                n = s.n
                norm, turn, mid, end = active(s)

                def value(v):
                    return v if s.known else sp.snap(v)

                at_next = [value(n * CHUNK + 2 * CHUNK + SEQ * b) for b in range(CHUNK // SEQ)]
                at_before, at_out = value(n * CHUNK - CHUNK), value(n * CHUNK - 2 * CHUNK)
                t_read, out_read, z_made = value(n + 2), value(n - 1), value(CT * n - CT)
                if norm:
                    at_least(sp, t_done, t_read)
                    for b in range(CHUNK // SEQ):
                        sp.dma_start(shifted[0:HALF, b, :], x1T[0:HALF, bass.ds(at_next[b], SEQ)]).then_inc(shifted_in, 16)
                        sp.dma_start(shifted[HALF:P, b, 1:SEQ], x1T[HALF:P, bass.ds(at_next[b], SEQ - 1)]).then_inc(shifted_in, 16)
                if end:
                    at_least(sp, both_added if last else out_taken, out_read)
                    sp.dma_start(x1_res[:, :], x1T[:, bass.ds(at_before, CHUNK)]).then_inc(res_in, 16)
                    if last:
                        sp.dma_start(x_res[:, :], xT[:, bass.ds(at_before, CHUNK)]).then_inc(res_in, 16)
                if last and (not s.known or n >= 2):
                    sp.wait_ge(ln_out.z_ready, z_made)
                    store(at_out)

            def store(at):
                sp.dma_start(out[bass.ds(at, CHUNK), :].rearrange("(t p) d -> p t d", p=P),
                             ln_out.z[:, :, :]).then_inc(stored, 16)

            slots(sp, slot)
            if last:
                sp.wait_ge(ln_out.z_ready, CT * CHUNKS)
                store(TOKENS - CHUNK)
                sp.wait_ge(stored, 16 * CHUNKS)

        @block.tensor
        def _(pe):
            pe.wait_ge(weights_split, 2)
            pe.wait_ge(ready, 1)

            def hidden(n, m, parts):
                if m == 0:
                    pe.wait_ge(normed_split, n + 1)
                at_least(pe, hid_whole, of_buffer_before(n, m))
                for bank, e in ((psg[m % 2], 1), (psa[m % 2], 0)):
                    mm = split_matmul(nc, bank[:, :], lambda a: w1_parts[:, a, e, m, :],
                                      lambda b: parts[:, b, :], True, True)
                mm.then_inc(up_done, 1)

            def slot(s):
                n = s.n
                norm, turn, mid, end = active(s)
                if turn:
                    pe.wait_ge(ln.z_ready, CT * (n + 2))
                    at_least(pe, normed_ready, n + 1)
                    for t in range(CT):
                        mm = nc.tensor.transpose(psz[:, P * t:P * t + P], ln.z[:, t, :], ident[:, :])
                    mm.then_inc(zt_done, 1)
                if norm:
                    pe.wait_ge(shifted_in, 16 * 2 * (CHUNK // SEQ) * (n + 3))
                    at_least(pe, ln.z_ready, CT * (n + 2))
                    flat = shifted[:, :, :].rearrange("p b t -> p (b t)")
                    for t in range(CT):
                        mm = nc.tensor.transpose(pst[:, t, :], flat[:, P * t:P * t + P], ident[:, :])
                    mm.then_inc(t_done, 1)
                if mid:
                    hidden(n, 0, normed_parts[s.offset % 2])
                if end:
                    pe.wait_ge(hid_ready, GB * n)
                    at_least(pe, out_taken, n - 1)
                    for k in range(GB):
                        mm = split_matmul(nc, pso[:, :], lambda a: w2_parts[:, a, k, :], lambda b: hid_parts[:, b, k, :],
                                          k == 0, k == GB - 1)
                    mm.then_inc(out_done, 1)
                if mid:
                    hidden(n, 1, normed_parts[s.offset % 2])
                if end and last:
                    pe.wait_ge(out_taken, n)
                    at_least(pe, ln_out.z_ready, CT * (n - 1))
                    for t in range(CT):
                        mm = nc.tensor.transpose(psy[:, t, :], sum_sb[:, P * t:P * t + P], ident[:, :])
                    mm.then_inc(turned_out, 1)
                if mid:
                    hidden(n, 2, normed_parts[s.offset % 2])

            slots(pe, slot)

        @block.scalar
        def _(act):
            act.wait_ge(w_in, 16 * n_loads)
            nc.scalar.copy(w1_parts[:, 0], w1[:, :, :, :]).then_inc(weights_hi, 1)
            nc.scalar.copy(w2_parts[:, 0], w2[:, :, :]).then_inc(weights_hi, 1)

            def round_hid(n, m):
                act.wait_ge(hid_whole, GB * n + m + 1)
                if m == 0:
                    at_least(act, out_done, n)
                nc.scalar.copy(hid_parts[:, 0, m, :], whole[m][:, :]).then_inc(hid_hi, 1)

            def slot(s):
                n = s.n
                norm, turn, mid, end = active(s)
                if turn:
                    act.wait_ge(zt_done, n + 2)
                    at_least(act, normed_split, n + 1)
                    nc.scalar.activation(normed[:, :], psz[:, :], ACT.Identity, bias=gain_offset[:, 1:2],
                                         scale=gain_offset[:, 0:1]).then_inc(normed_whole, 1)
                    at_least(act, up_done, GB * n)
                    nc.scalar.activation(normed_parts[(s.offset + 1) % 2][:, 0, :], psz[:, :], ACT.Identity, bias=gain_offset[:, 1:2],
                                         scale=gain_offset[:, 0:1]).then_inc(normed_ready, 1)
                if mid:
                    for m in range(GB):
                        act.wait_ge(up_done, GB * n + m + 1)
                        at_least(act, hid_whole, of_buffer_before(n, m))
                        nc.scalar.activation(gate[m % 2][:, :], psg[m % 2][:, :], ACT.Gelu,
                                             bias=b1[:, 1, m:m + 1]).then_inc(gate_done, 1)
                        if m > 0:
                            round_hid(n, m - 1)
                    round_hid(n, GB - 1)

            slots(act, slot)

        @block.vector
        def _(dve):
            nc.vector.memset(shifted[:, :, 0:1], 0.0).then_inc(ready, 1)
            dve.wait_ge(w_in, 16 * n_loads)
            for i, (weight, parts) in enumerate(((w1[:, :, :, :], w1_parts), (w2[:, :, :], w2_parts))):
                dve.wait_ge(weights_hi, i + 1)
                write_rest(nc, parts[:, 1], weight, parts[:, 0]).then_inc(weights_split, 1)

            def slot(s):
                n = s.n
                norm, turn, mid, end = active(s)
                if norm:
                    norm_stats(nc, dve, ln, pst, t_done, n + 3)
                if turn:
                    dve.wait_ge(normed_ready, n + 2)
                    parts = normed_parts[(s.offset + 1) % 2]
                    write_rest(nc, parts[:, 1, :], normed[:, :], parts[:, 0, :]).then_inc(normed_split, 1)
                if mid:
                    gated_hidden(n, 0)
                if end:
                    dve.wait_ge(out_done, n)
                    if last:
                        dve.wait_ge(both_added, n)
                        at_least(dve, turned_out, n - 1)
                        to, res = sum_sb[:, :], both_res
                    else:
                        dve.wait_ge(res_in, 16 * n)
                        to, res = x1T[:, bass.ds((n - 1) * CHUNK, CHUNK)], x1_res
                    nc.vector.scalar_tensor_tensor(to, pso[:, :], b2[:, :], res[:, :], ALU.add, ALU.add).then_inc(out_taken, 1)
                if norm:
                    norm_apply(nc, dve, ln, pst, n + 3, zt_done, 1)
                if mid:
                    gated_hidden(n, 1)
                if end and last:
                    norm_stats(nc, dve, ln_out, psy, turned_out, n)
                if mid:
                    gated_hidden(n, 2)
                if end and last:
                    norm_apply(nc, dve, ln_out, psy, n, stored, 16)

            def gated_hidden(n, m):
                dve.wait_ge(gate_done, GB * n + m + 1)
                at_least(dve, hid_ready, GB * (n - 1) + m + 1)
                nc.vector.scalar_tensor_tensor(whole[m][:, :], psa[m % 2][:, :], b1[:, 0, m:m + 1],
                                               gate[m % 2][:, :], ALU.add, ALU.mult).then_inc(hid_whole, 1)

            slots(dve, slot)

        @block.gpsimd
        def _(pool):
            def slot(s):
                norm, turn, mid, end = active(s)
                if end and last:
                    pool.wait_ge(res_in, 16 * res_loads * s.n)
                    at_least(pool, out_taken, s.n - 1)
                    nc.gpsimd.tensor_tensor(both_res[:, :], x1_res[:, :], x_res[:, :], ALU.add).then_inc(both_added, 1)
                if norm:
                    norm_rstd(nc, pool, ln, s.n + 3)
                if mid:
                    hidden_rest(s.n, 0)
                    hidden_rest(s.n, 1)
                if end and last:
                    norm_rstd(nc, pool, ln_out, s.n)
                if mid:
                    hidden_rest(s.n, 2)

            def hidden_rest(n, m):
                pool.wait_ge(hid_hi, GB * n + m + 1)
                nc.gpsimd.tensor_tensor(hid_parts[:, 1, m, :], whole[m][:, :],
                                        hid_parts[:, 0, m, :].bitcast(F32), ALU.subtract).then_inc(hid_ready, 1)

            slots(pool, slot)



LHEADS, LHD, WINDOW = 8, 64, 64
PAIRS = LHEADS // 2
INNER = LHEADS * LHD
SEEN0 = P + WINDOW
COLS = SEEN0 + P
QK_SCALE = 8.0
SQ_FLOOR = 1e-24


def local_attention(nc, name, src, dst, consts, w):
    with ExitStack() as ctx:
        def sb(n, shape, dt=F32):
            return ctx.enter_context(nc.sbuf_tensor(f"{name}_{n}", shape, dt))

        def ps(n, shape, dt=F32):
            return ctx.enter_context(nc.psum_tensor(f"{name}_{n}", shape, dt))

        sems = phase_semaphores(nc, ctx)

        def sem(n):
            sems.append(nc.alloc_semaphore(f"{name}_{n}"))
            return sems[-1]

        ident, ident_bf = consts["ident"], consts["ident_bf"]
        w_qkv, w_qkv_parts = sb("w_qkv", [P, 3, INNER]), sb("w_qkv_parts", [P, 2, 3, INNER], F32R)
        wo = sb("wo", [P, PAIRS, D])
        rotary = sb("rotary", [P, 2, 2, 2, LHD])
        dim_scale = sb("dim_scale", [P, 2, LHD])
        masks = sb("masks", [P, 2 * SEEN0 + COLS])
        mask_q, mask_k = sb("mask_q", [P, 2 * SEEN0], BF16), sb("mask_k", [P, COLS], BF16)
        picks = sb("picks", [96, 4, P])
        minus_pick = sb("minus_pick", [96, 4, P], BF16)
        ones = sb("ones", [P, LHD])

        shifted = [sb(f"shifted{i}", [P, SEQ]) for i in range(2)]
        shifted_parts = sb("shifted_parts", [P, 2, SEQ], F32R)
        x_res = [sb(f"x_res{i}", [P, SEQ]) for i in range(2)]
        squares = [sb(f"squares{i}", [P, INNER]) for i in range(2)]
        terms = [sb(f"terms{i}", [P, 2, INNER]) for i in range(2)]
        length2, length2_held, rlength = (sb(n, [P, 4, LHEADS]) for n in ("length2", "length2_held", "rlength"))
        qk = [sb(f"qk{i}", [P, 4, INNER]) for i in range(2)]
        q_t = [sb(f"q_t{i}", [P, PAIRS, 2, SEQ]) for i in range(RING)]
        k_t = [sb(f"k_t{i}", [P, PAIRS, SEQ]) for i in range(RING)]
        v = [sb(f"v{i}", [P, 2, INNER]) for i in range(RING)]
        row_max = [sb(f"row_max{i}", [P, 2, LHEADS]) for i in range(2)]
        max_rest = sb("max_rest", [P, 2, 4])
        max_part = [sb(f"max_part{i}", [P, 2, 3, 4], BF16) for i in range(2)]
        max_rows = [sb(f"max_rows{i}", [96, SEQ], BF16) for i in range(2)]
        prob = [sb(f"prob{i}", [P, COLS]) for i in range(4)]
        pv_t = sb("pv_t", [P, 2, 8, 32])
        denom = sb("denom", [P, 8, 1])
        heads_t = sb("heads_t", [P, 8, 32])
        o_sb = sb("o_sb", [P, PAIRS, SEQ])

        qkv_ps = [ps(f"qkv_ps{i}", [P, INNER]) for i in range(2)]
        scores_q = [ps(f"scores_q{i}", [P, 2 * SEEN0]) for i in range(2)]
        scores_k = [ps(f"scores_k{i}", [P, COLS]) for i in range(2)]
        pv = ps("pv", [P, 2, SEQ])
        misc = ps("misc", [P, 2 * SEQ])
        misc_bf = misc[:, :].bitcast(BF16)

        w_in, ready, tables_made = sem("w_in"), sem("ready"), sem("tables_made")
        shifted_in = [sem(f"shifted_in{i}") for i in range(2)]
        x_res_in = [sem(f"x_res_in{i}") for i in range(2)]
        weights_hi, weights_split, shifted_hi, shifted_split = (
            sem(n) for n in ("weights_hi", "weights_split", "shifted_hi", "shifted_split"))
        qkv_done, turned, sq_done, sk_done, pv_done, maxt_done, out_done = (
            sem(n) for n in ("qkv_done", "turned", "sq_done", "sk_done", "pv_done", "maxt_done", "out_done"))
        terms_done, length_done, scaled_qk, max_found, pv_turned, inverted, scaled, o_ready = (
            sem(n) for n in ("terms_done", "length_done", "scaled_qk", "max_found", "pv_turned", "inverted", "scaled", "o_ready"))
        squared, v_ready, qk_taken, maxt_taken, out_written, exp_done, q_half = (
            sem(n) for n in ("squared", "v_ready", "qk_taken", "maxt_taken", "out_written", "exp_done", "q_half"))
        added, held, rlength_done, max_step, max_split = (
            sem(n) for n in ("added", "held", "rlength_done", "max_step", "max_split"))

        def active(s):
            if not s.known:
                return (True,) * 5
            return tuple(0 <= s.n + ahead < BATCH for ahead in (3, 2, 1, 0, -1))

        def slots(engine, body):
            for n in range(-AHEAD, RING + 1):
                body(Slot(None, RING, n))
            with engine.Fori(0, (BATCH - 2 * RING) // RING) as i:
                for offset in range(RING + 1, 2 * RING + 1):
                    body(Slot(i, RING, offset))
            for n in range(BATCH - RING + 1, BATCH + 1):
                body(Slot(None, RING, n))

        n_loads, n_tables = 6, 2 + 8 + 1
        n_ready = 2 + RING + 2 + 1
        block = ctx.enter_context(nc.Block())

        @block.sync
        def _(sp):
            for to, of in ((w_qkv[:, :, :], w["w_qkv"]), (wo[:, :, :], w["wo"].rearrange("(b p) n -> p b n", p=P)),
                           (rotary[:, :, :, :, :], w["rotary"]), (masks[:, :], w["masks"]),
                           (picks[:, :, :], w["picks"]),
                           (dim_scale[:, :, :], w["dim_scale"].to_broadcast([P, 2, LHD]))):
                sp.dma_start(to, of).then_inc(w_in, 16)
            sp.wait_ge(ready, n_ready)

            def slot(s):
                n, j = s.n, s.offset % RING
                a, t, b1, b3, c = active(s)

                def value(x):
                    return x if s.known else sp.snap(x)

                at_next, at_now = value(n * SEQ + AHEAD * SEQ), value(n * SEQ)
                split, out_read = value(n + 2), value(n - 1)
                if a:
                    buf = (j + AHEAD) % 2
                    at_least(sp, shifted_split, split)
                    sp.dma_start(shifted[buf][0:HALF, :], src[0:HALF, bass.ds(at_next, SEQ)]).then_inc(shifted_in[buf], 16)
                    sp.dma_start(shifted[buf][HALF:P, 1:SEQ],
                                 src[HALF:P, bass.ds(at_next, SEQ - 1)]).then_inc(shifted_in[buf], 16)
                if b3:
                    at_least(sp, out_written, out_read)
                    sp.dma_start(x_res[j % 2][:, :], src[:, bass.ds(at_now, SEQ)]).then_inc(x_res_in[j % 2], 16)

            slots(sp, slot)

        @block.tensor
        def _(pe):
            pe.wait_ge(w_in, 16 * n_loads)
            pe.wait_ge(weights_split, 1)

            def misc_free(s, use):
                n = s.n
                a, t, b1, b3, c = active(s)
                order = [("turn0", t, qk_taken, 4 * (n + 2) + 1), ("out", c, out_written, n),
                         ("max1", b3, maxt_taken, 2 * n + 2), ("turn1", t, qk_taken, 4 * (n + 2) + 2),
                         ("max0", b1, maxt_taken, 2 * (n + 1) + 1), ("turn2", t, qk_taken, 4 * (n + 2) + 3),
                         ("turn3", t, qk_taken, 4 * (n + 2) + 4)]
                k = [o[0] for o in order].index(use)
                for o in reversed(order[:k]):
                    if o[1]:
                        return at_least(pe, o[2], o[3])
                before = active(Slot(s.i, RING, s.offset - 1))
                if before[1]:
                    at_least(pe, qk_taken, 4 * (n + 2))
                if before[2]:
                    at_least(pe, maxt_taken, 2 * n + 1)
                elif before[3]:
                    at_least(pe, maxt_taken, 2 * n)
                if before[4]:
                    at_least(pe, out_written, n - 1)

            def qkv(s, use):
                m = s.n + 3
                part, tile = (use % 2, use // 2) if use < 4 else (2, use - 4)
                if use == 0:
                    pe.wait_ge(shifted_split, m + 1)
                if use < 2:
                    at_least(pe, v_ready, 2 * m - 1 + use)
                else:
                    pe.wait_ge(squared, 4 * m + use - 1)
                    pe.wait_ge(terms_done, 8 * m + 2 * (use - 1))
                split_matmul(nc, qkv_ps[use % 2][:, :], lambda a: shifted_parts[:, a, P * tile:P * tile + P],
                             lambda b: w_qkv_parts[:, b, part, :], True, True).then_inc(qkv_done, 1)

            def turn(s, use):
                m, which = s.n + 2, use // 2
                pe.wait_ge(scaled_qk, 4 * m + 2 * which + 2)
                misc_free(s, f"turn{use}")
                for p in range(2):
                    for tile in range(2):
                        pair = 2 * (use % 2) + p
                        mm = nc.tensor.transpose(misc[:, SEQ * p + P * tile:SEQ * p + P * tile + P],
                                                 qk[(s.offset + 2) % 2][:, 2 * tile + which, P * pair:P * pair + P],
                                                 ident[:, :])
                mm.then_inc(turned, 1)

            def turn_max(s, half, batch):
                misc_free(s, f"max{half}")
                pe.wait_ge(max_split, 2 * batch + half + 1)
                for qt in range(2):
                    mm = nc.tensor.transpose(misc_bf[0:12, P * qt:P * qt + P],
                                             max_part[half][:, qt, :, :].rearrange("p a h -> p (a h)"), ident_bf[:, :])
                mm.then_inc(maxt_done, 1)

            def weigh_v(n, j, pair):
                pe.wait_ge(exp_done, LHEADS * n + 2 * pair + 2)
                if pair == 0:
                    pe.wait_ge(v_ready, 2 * n + 2)
                at_least(pe, pv_turned, 4 * n + pair)
                for of_ones in range(2):
                    for kt, q0, q1, col, start, stop in ((0, 0, SEEN0, P, True, False), (1, P, SEEN0, 0, False, True),
                                                         (1, SEEN0, SEQ, WINDOW, True, True)):
                        for e in range(2):
                            h = 2 * pair + e
                            weights = ones[:, :] if of_ones else v[j][:, kt, LHD * h:LHD * h + LHD]
                            mm = nc.tensor.matmul(pv[LHD * e:LHD * e + LHD, of_ones, q0:q1], weights,
                                                  prob[h % 4][:, col:col + q1 - q0], start=start, stop=stop)
                mm.then_inc(pv_done, 1)

            def slot(s):
                n, j = s.n, s.offset % RING
                a, t, b1, b3, c = active(s)
                jb = (j + 1) % RING
                if s.known and n == -1:
                    pe.wait_ge(tables_made, n_tables)
                    pe.wait_ge(ready, n_ready)
                for h in range(LHEADS):
                    pair, e, u = h // 2, h % 2, h
                    if b1:
                        if h == 0:
                            pe.wait_ge(qk_taken, 4 * (n + 2))
                        at_least(pe, max_found, LHEADS * (n + 1) + h - 1)
                        bank = scores_q[h % 2]
                        nc.tensor.matmul(bank[:, :], ident_bf[:, :], mask_q[:, :], start=True, stop=False)
                        nc.tensor.matmul(bank[:, 0:P], q_t[jb][:, pair, e, 0:P], k_t[jb][:, pair, 0:P],
                                         start=False, stop=False)
                        nc.tensor.matmul(bank[:, SEEN0:2 * SEEN0], q_t[jb][:, pair, e, P:SEQ],
                                         k_t[jb][:, pair, P - WINDOW:SEQ], start=False, stop=True).then_inc(sq_done, 1)
                    if b3:
                        if h % 4 == 0:
                            pe.wait_ge(maxt_taken, 2 * n + 1 + h // 4)
                        at_least(pe, exp_done, LHEADS * n + h - 1)
                        bank, rows, pick = scores_k[h % 2], max_rows[h // 4], minus_pick[:, h % 4, :]
                        nc.tensor.matmul(bank[:, :], ident_bf[:, :], mask_k[:, :], start=True, stop=False)
                        nc.tensor.matmul(bank[:, P:COLS], pick, rows[:, 0:SEEN0], start=False, stop=False)
                        nc.tensor.matmul(bank[:, 0:P], pick, rows[:, P:SEQ], start=False, stop=False)
                        nc.tensor.matmul(bank[:, P:COLS], k_t[j][:, pair, 0:P], q_t[j][:, pair, e, 0:SEEN0],
                                         start=False, stop=False)
                        nc.tensor.matmul(bank[:, 0:P], k_t[j][:, pair, P:SEQ], q_t[j][:, pair, e, P:SEQ],
                                         start=False, stop=True).then_inc(sk_done, 1)
                    if u == 0:
                        if c:
                            weigh_v(n - 1, (j - 1) % RING, 3)
                    if u == 1:
                        if t:
                            turn(s, 0)
                        if a:
                            qkv(s, 0)
                    if u == 2:
                        if a:
                            qkv(s, 1)
                        if c:
                            misc_free(s, "out")
                            pe.wait_ge(o_ready, PAIRS * n)
                            for p in range(PAIRS):
                                mm = nc.tensor.matmul(misc[:, 0:SEQ], wo[:, p, :], o_sb[:, p, :],
                                                      start=(p == 0), stop=(p == PAIRS - 1))
                            mm.then_inc(out_done, 1)
                    if u == 3:
                        if b3:
                            turn_max(s, 1, n)
                        if t:
                            turn(s, 1)
                        if b3:
                            weigh_v(n, j, 0)
                        if a:
                            qkv(s, 2)
                    if u == 4:
                        if b1:
                            turn_max(s, 0, n + 1)
                        if a:
                            qkv(s, 3)
                    if u == 5:
                        if t:
                            turn(s, 2)
                        if b3:
                            weigh_v(n, j, 1)
                        if a:
                            qkv(s, 4)
                    if u == 6:
                        if t:
                            turn(s, 3)
                        if a:
                            qkv(s, 5)
                    if u == 7 and b3:
                        weigh_v(n, j, 2)

            slots(pe, slot)

        @block.vector
        def _(dve):
            for x in shifted:
                nc.vector.memset(x[:, 0:1], 0.0).then_inc(ready, 1)
            for m in max_rows:
                nc.vector.memset(m[:, :], 0.0).then_inc(ready, 1)
            nc.vector.memset(ones[:, :], 1.0).then_inc(ready, 1)
            dve.wait_ge(w_in, 16 * n_loads)
            dve.wait_ge(weights_hi, 1)
            write_rest(nc, w_qkv_parts[:, 1], w_qkv[:, :, :], w_qkv_parts[:, 0]).then_inc(weights_split, 1)
            nc.vector.tensor_copy(mask_q[:, :], masks[:, 0:2 * SEEN0]).then_inc(tables_made, 1)
            nc.vector.tensor_copy(mask_k[:, :], masks[:, 2 * SEEN0:]).then_inc(tables_made, 1)
            for which in range(2):
                for tile in range(2):
                    for f in range(2):
                        nc.vector.tensor_tensor(rotary[:, which, tile, f, :], rotary[:, which, tile, f, :],
                                                dim_scale[:, which, :], ALU.mult).then_inc(tables_made, 1)
            nc.vector.tensor_copy(minus_pick[:, :, :], picks[:, :, :]).then_inc(tables_made, 1)
            dve.wait_ge(tables_made, n_tables)

            def take_qk(s, use):
                m = s.n + 3
                which, tile = use % 2, use // 2
                dve.wait_ge(squared, 4 * m + use + 1)
                at_least(dve, added, 8 * m + 2 * use - 2)
                heads = qkv_ps[use % 2][:, :].rearrange("p (h d) -> p h d", d=LHD)
                for f in range(2):
                    factor = rotary[:, which, tile, f:f + 1, :].to_broadcast([P, LHEADS, LHD])
                    nc.vector.tensor_tensor(terms[use % 2][:, f, :].rearrange("p (h d) -> p h d", d=LHD), heads, factor,
                                            ALU.mult).then_inc(terms_done, 1)
                nc.vector.tensor_reduce(length2[:, use, :], squares[use % 2][:, :].rearrange("p (h d) -> p h d", d=LHD),
                                        AX.X, ALU.add).then_inc(length_done, 1)
                if use == 3:
                    at_least(dve, rlength_done, m)
                    dve.wait_ge(length_done, 4 * (m + 1))
                    nc.vector.tensor_scalar(length2_held[:, :, :], length2[:, :, :], SQ_FLOOR, None,
                                            ALU.max).then_inc(held, 1)

            def to_unit(s, which):
                dve.wait_ge(rlength_done, s.n + 3)
                for tile in range(2):
                    i = 2 * tile + which
                    x = qk[(s.offset + 2) % 2][:, i, :].rearrange("p (h d) -> p h d", d=LHD)
                    r = rlength[:, i, :].rearrange("p (h d) -> p h d", d=1).to_broadcast([P, LHEADS, LHD])
                    nc.vector.tensor_tensor(x, x, r, ALU.mult).then_inc(scaled_qk, 1)

            def normalise_pair(m, pair):
                at_least(dve, scaled, 4 * m + pair)
                dve.wait_ge(pv_done, 4 * m + pair + 1)
                nc.vector.transpose(pv_t[:, :, :, :].rearrange("p g c x -> p (g c x)"),
                                    pv[:, :, :].rearrange("p g q -> p (g q)")).then_inc(pv_turned, 1)
                dve.wait_ge(pv_turned, 4 * m + pair + 1)
                nc.vector.reciprocal(denom[:, :, :], pv_t[:, 1, :, 0:1]).then_inc(inverted, 1)
                at_least(dve, o_ready, 4 * m + pair)
                dve.wait_ge(inverted, 4 * m + pair + 1)
                nc.vector.tensor_tensor(heads_t[:, :, :], pv_t[:, 0, :, :], denom[:, :, :].to_broadcast([P, 8, 32]),
                                        ALU.mult).then_inc(scaled, 1)
                if pair == 0:
                    at_least(dve, out_done, m)
                dve.wait_ge(scaled, 4 * m + pair + 1)
                nc.vector.transpose(o_sb[:, pair, :], heads_t[:, :, :].rearrange("p c x -> p (c x)")).then_inc(o_ready, 1)

            def slot(s):
                n, j = s.n, s.offset % RING
                a, t, b1, b3, c = active(s)
                for h in range(LHEADS):
                    if b1:
                        if h == 0:
                            at_least(dve, max_split, 2 * n)
                        dve.wait_ge(sq_done, LHEADS * (n + 1) + h + 1)
                        nc.vector.tensor_reduce(row_max[(j + 1) % 2][:, :, h],
                                                scores_q[h % 2][:, :].rearrange("p (t k) -> p t k", t=2),
                                                AX.X, ALU.max).then_inc(max_found, 1)
                    if h == 0 and a:
                        dve.wait_ge(shifted_hi, n + 4)
                        write_rest(nc, shifted_parts[:, 1, :], shifted[(j + 3) % 2][:, :],
                                   shifted_parts[:, 0, :]).then_inc(shifted_split, 1)
                    if h == 0 and t:
                        to_unit(s, 0)
                    if h == 1 and c:
                        normalise_pair(n - 1, 3)
                    if h == 1 and a:
                        take_qk(s, 0)
                    if h == 2 and t:
                        to_unit(s, 1)
                    if h == 2 and c:
                        dve.wait_ge(out_done, n)
                        dve.wait_ge(x_res_in[(j - 1) % 2], 16 * s.fills(-1, 2))
                        nc.vector.tensor_tensor(dst[:, bass.ds((n - 1) * SEQ, SEQ)], misc[:, 0:SEQ], x_res[(j - 1) % 2][:, :],
                                                ALU.add).then_inc(out_written, 1)
                    if h == 2 and a:
                        take_qk(s, 1)
                    if h == 3 and a:
                        take_qk(s, 2)
                    if h == 4 and b3:
                        normalise_pair(n, 0)
                    if h == 4 and a:
                        take_qk(s, 3)
                    if h == 6 and b3:
                        normalise_pair(n, 1)
                    if h == 7 and b3:
                        normalise_pair(n, 2)

            slots(dve, slot)

        @block.scalar
        def _(act):
            act.wait_ge(w_in, 16 * n_loads)
            nc.scalar.copy(w_qkv_parts[:, 0], w_qkv[:, :, :]).then_inc(weights_hi, 1)
            act.wait_ge(ready, n_ready)

            def square(s, use):
                m = s.n + 3
                act.wait_ge(qkv_done, 6 * m + use + 1)
                at_least(act, length_done, 4 * m + use - 1)
                nc.scalar.activation(squares[use % 2][:, :], qkv_ps[use % 2][:, :], ACT.Square).then_inc(squared, 1)

            def take_v(s, tile):
                m = s.n + 3
                act.wait_ge(qkv_done, 6 * m + 5 + tile)
                at_least(act, pv_done, PAIRS * s.n)
                nc.scalar.copy(v[(s.offset + 3) % RING][:, tile, :], qkv_ps[tile][:, :]).then_inc(v_ready, 1)

            def take_turned(s, use):
                m, jt, pairs = s.n + 2, (s.offset + 2) % RING, slice(2 * (use % 2), 2 * (use % 2) + 2)
                act.wait_ge(turned, 4 * m + use + 1)
                at_least(act, sk_done, LHEADS * (s.n - 1))
                bank = misc[:, :].rearrange("p (a q) -> p a q", a=2)
                if use < 2:
                    nc.scalar.copy(q_t[jt][0:HALF, pairs, 0, :], bank[0:HALF, :, :]).then_inc(q_half, 1)
                    nc.scalar.copy(q_t[jt][HALF:P, pairs, 1, :], bank[HALF:P, :, :]).then_inc(qk_taken, 1)
                else:
                    nc.scalar.copy(k_t[jt][:, pairs, :], bank[:, :, :]).then_inc(qk_taken, 1)

            def take_max(batch, half, scored):
                act.wait_ge(maxt_done, 2 * batch + half + 1)
                at_least(act, sk_done, scored)
                nc.scalar.copy(max_rows[half][0:12, :], misc_bf[0:12, 0:SEQ]).then_inc(maxt_taken, 1)

            def slot(s):
                n, j = s.n, s.offset % RING
                a, t, b1, b3, c = active(s)
                for h in range(LHEADS):
                    if h == 0 and a:
                        act.wait_ge(shifted_in[(j + 3) % 2], 32 * s.fills(3, 2))
                        at_least(act, qkv_done, 6 * (n + 3))
                        nc.scalar.copy(shifted_parts[:, 0, :], shifted[(j + 3) % 2][:, :]).then_inc(shifted_hi, 1)
                    if b3:
                        act.wait_ge(sk_done, LHEADS * n + h + 1)
                        at_least(act, pv_done, PAIRS * n + h // 2 - 1)
                        nc.scalar.activation(prob[h % 4][:, :], scores_k[h % 2][:, :], ACT.Exp,
                                             scale=QK_SCALE).then_inc(exp_done, 1)
                    if h == 1:
                        if t:
                            take_turned(s, 0)
                        if a:
                            square(s, 0)
                    if h == 2:
                        if a:
                            square(s, 1)
                    if h == 3:
                        if b3:
                            take_max(n, 1, LHEADS * n)
                        if t:
                            take_turned(s, 1)
                        if a:
                            square(s, 2)
                    if h == 4:
                        if b1:
                            take_max(n + 1, 0, LHEADS * n + 4)
                        if a:
                            square(s, 3)
                    if h == 5:
                        if t:
                            take_turned(s, 2)
                        if a:
                            take_v(s, 0)
                    if h == 6:
                        if t:
                            take_turned(s, 3)
                        if a:
                            take_v(s, 1)

            slots(act, slot)

        @block.gpsimd
        def _(pool):
            for q in q_t:
                nc.gpsimd.memset(q[:, :, :, :], 0.0).then_inc(ready, 1)
            zeros = consts["zeros"][:, 0:8].rearrange("p (a b) -> p a b", a=2)

            def split_max(batch, j, half):
                hs = slice(4 * half, 4 * half + 4)
                m, part = row_max[j % 2], max_part[half]
                pool.wait_ge(max_found, LHEADS * batch + 4 * half + 4)
                at_least(pool, maxt_done, 2 * (batch - 1) + half + 1)
                steps = 3 * (2 * batch + half)
                nc.gpsimd.tensor_tensor(part[:, :, 0, :], m[:, :, hs], zeros, ALU.add).then_inc(max_step, 1)
                pool.wait_ge(max_step, steps + 1)
                nc.gpsimd.tensor_tensor(max_rest[:, :, :], m[:, :, hs], part[:, :, 0, :], ALU.subtract).then_inc(max_step, 1)
                pool.wait_ge(max_step, steps + 2)
                nc.gpsimd.tensor_tensor(part[:, :, 1, :], max_rest[:, :, :], zeros, ALU.add).then_inc(max_step, 1)
                pool.wait_ge(max_step, steps + 3)
                nc.gpsimd.tensor_tensor(part[:, :, 2, :], max_rest[:, :, :], part[:, :, 1, :],
                                        ALU.subtract).then_inc(max_split, 1)

            def add_terms(s, use):
                m = s.n + 3
                pool.wait_ge(terms_done, 8 * m + 2 * use + 2)
                if use == 0:
                    at_least(pool, turned, 4 * (m - 1))
                halves = "p (h e d) -> p h e d"
                own = terms[use % 2][:, 0, :].rearrange(halves, e=2, d=LHD // 2)
                other = terms[use % 2][:, 1, :].rearrange(halves, e=2, d=LHD // 2)
                to = qk[(s.offset + 3) % 2][:, use, :].rearrange(halves, e=2, d=LHD // 2)
                for e in range(2):
                    nc.gpsimd.tensor_tensor(to[:, :, e, :], own[:, :, e, :], other[:, :, 1 - e, :],
                                            ALU.add).then_inc(added, 1)

            def slot(s):
                n, j = s.n, s.offset % RING
                a, t, b1, b3, c = active(s)
                if b3:
                    split_max(n, j, 1)
                if a:
                    for use in range(2):
                        add_terms(s, use)
                if b1:
                    split_max(n + 1, j + 1, 0)
                if a:
                    for use in (2, 3):
                        add_terms(s, use)
                    m = n + 3
                    flat = "p a h -> p (a h)"
                    at_least(pool, scaled_qk, 4 * m)
                    pool.wait_ge(held, m + 1)
                    nc.gpsimd.tensor_tensor(rlength[:, :, :].rearrange(flat), length2_held[:, :, :].rearrange(flat),
                                            consts["minus_half"][:, :], ALU.pow).then_inc(rlength_done, 1)

            slots(pool, slot)


def build(nc, stages, x, out, d):
    with ExitStack() as ctx:
        def sb(n, shape, dt=F32):
            return ctx.enter_context(nc.sbuf_tensor(n, shape, dt))

        xT = sb("xT", [P, TOKENS])
        consts = {"ident": sb("ident", [P, P]), "ident_bf": sb("ident_bf", [P, P], BF16),
                  "eps": sb("eps", [P, 4]), "minus_half": sb("minus_half", [P, 4 * LHEADS]), "zeros": sb("zeros", [P, 2 * HEADS])}
        loaded = ctx.enter_context(nc.semaphore("loaded"))
        filled = ctx.enter_context(nc.semaphore("filled"))
        with nc.Block() as block:
            @block.sync
            def _(sp):
                sp.dma_start(consts["ident"][:, :], d["ident"]).then_inc(loaded, 16)
                sp.wait_ge(loaded, 16)

            @block.vector
            def _(dve):
                dve.wait_ge(loaded, 16)
                nc.vector.memset(consts["eps"][:, :], LN_EPS).then_inc(filled, 1)
                nc.vector.memset(consts["minus_half"][:, :], -0.5).then_inc(filled, 1)
                nc.vector.tensor_copy(consts["ident_bf"][:, :], consts["ident"][:, :]).then_inc(filled, 1)
                nc.vector.memset(consts["zeros"][:, :], 0.0).then_inc(filled, 1)
                dve.wait_ge(filled, 4)

        x1T = None
        for k, stage in enumerate(stages):
            last = k == len(stages) - 1
            if stage in ("attn0", "attn1"):
                attention(nc, stage, x if k == 0 else xT, xT, out, consts, d[stage], stage == "attn0", last)
            elif stage == "ffn0":
                ffn(nc, stage, xT, out, consts, d[stage], last)
            elif stage in ("local0", "local1"):
                if x1T is None:
                    x1T = sb("x1T", [P, TOKENS])
                local_attention(nc, stage, xT if stage == "local0" else x1T, x1T, consts, d[stage])
            elif stage in ("gated0", "gated1"):
                gated_ffn(nc, stage, x1T, xT, out, consts, d[stage], last)


STAGES = ("attn0", "ffn0", "attn1", "local0", "gated0", "local1", "gated1")


def laid_out(inputs):
    f = {k: np.asarray(v) for k, v in inputs.items()}
    c = np.ascontiguousarray

    def by_dim(w):
        return c(w.reshape(w.shape[0], HEADS, HD).transpose(0, 2, 1).reshape(w.shape[0], D))

    def by_group(w):
        return c(w.reshape(4, 4, HD, D).transpose(1, 0, 2, 3).reshape(D, D))

    inv_freq = (np.float32(1.0) / np.float32(10000.0) ** (np.arange(0, HD, 2, dtype=np.float32) / np.float32(HD))).astype(np.float32)
    angle = np.arange(SEQ, dtype=np.float32)[:, None] * inv_freq[None, :]
    cos = np.repeat(np.repeat(np.cos(angle), 2, axis=1).T, HEADS, axis=0)
    sin = np.repeat(np.repeat(np.sin(angle), 2, axis=1).T, HEADS, axis=0)
    w0 = f["L0_attn_w_qkv"]
    w1 = f["L1_attn_qkv_w"].T.reshape(D, HEADS, 3, HD)
    b1 = f["L1_attn_qkv_b"].reshape(1, HEADS, 3, HD)
    pick = lambda w, i: c(w[:, :, i, :].reshape(w.shape[0], D))
    shapes = {}

    half_idx = np.arange(0, LHD, 2, dtype=np.float32)
    t = np.arange(SEQ, dtype=np.float32)
    freqs = t[:, None] * (np.float32(1.0) / np.float32(10000.0) ** (half_idx / np.float32(LHD)))[None, :]
    freqs = np.concatenate([freqs, freqs], axis=-1)
    base = ((half_idx + np.float32(0.4 * LHD)) / np.float32(1.4 * LHD)).astype(np.float32)
    scale = base[None, :] ** ((t - SEQ // 2) / np.float32(WINDOW // 2))[:, None]
    scale = np.concatenate([scale, scale], axis=-1)
    sign = np.where(np.arange(LHD) < LHD // 2, 1.0, -1.0).astype(np.float32)
    other = (np.arange(LHD) + LHD // 2) % LHD
    factors = []
    for decay in (scale, 1 / scale):
        own, turned = np.cos(freqs) * decay, (np.sin(freqs) * decay)[:, other] * sign
        factors.append(np.stack([own, turned], axis=1).reshape(2, P, 2, LHD).transpose(1, 0, 2, 3))
    rotary = c(np.stack(factors, axis=1).astype(np.float32))

    def mask(query, key):
        return np.where((key <= query) & (query <= key + WINDOW), 0.0, -1e30).astype(np.float32)

    i, far = np.arange(P)[:, None], 10 * SEQ
    col = np.arange(SEEN0)[None, :]
    masks = c(np.concatenate([mask(i, np.where(col < P, col, far)), mask(P + i, P - WINDOW + col),
                              mask(P + np.arange(P)[None, :], P + i), mask(col, i)], axis=1))
    picks = np.zeros((96, 4, P), np.float32)
    for h in range(4):
        picks[[h, 4 + h, 8 + h], h] = -1.0
    for l in range(2):
        shapes[f"local{l}.w_qkv"] = c(f["L1_ffn_wqkv"][l].reshape(D, 3, INNER))
        shapes[f"local{l}.wo"] = c(f["L1_ffn_wo"][l])
        shapes[f"local{l}.dim_scale"] = c(np.stack([f["L1_ffn_q_scale"][l], f["L1_ffn_k_scale"][l]])[None])
        shapes[f"local{l}.rotary"], shapes[f"local{l}.masks"], shapes[f"local{l}.picks"] = rotary, masks, picks
        pad = np.zeros((D, GB * P - GATED), np.float32)
        w_in, w_out, b_in = f["L1_ffn_w1"][l], f["L1_ffn_w2"][l], f["L1_ffn_b1"][l][None]
        shapes[f"gated{l}.w1"] = c(np.concatenate([w_in[:, :GATED], pad, w_in[:, GATED:], pad], axis=1))
        shapes[f"gated{l}.w2"] = c(np.concatenate([w_out, pad.T], axis=0))
        shapes[f"gated{l}.b1"] = c(np.concatenate([b_in[:, :GATED], pad[:1], b_in[:, GATED:], pad[:1]], axis=1)
                                   .reshape(2, GB, P).transpose(2, 0, 1))
        shapes[f"gated{l}.gain_offset"] = c(np.stack([f["L1_ffn_ln_g"][l], f["L1_ffn_ln_b"][l]], axis=1))
        shapes[f"gated{l}.b2"] = c(f["L1_ffn_b2"][l].reshape(D, 1))
    return shapes | {
        "ffn0.w1": c(f["L0_ffn_w1_w"].T), "ffn0.w2": c(f["L0_ffn_w2_w"].T),
        "ffn0.h1": c(f["L0_ffn_h1_w"].T), "ffn0.h2": c(f["L0_ffn_h2_w"].T), "ffn0.w3": c(f["L0_ffn_w3_w"].T),
        "ffn0.s3": f["L0_ffn_w3_s"].reshape(1, D),
        "ffn0.scales": c(np.stack([f[f"L0_ffn_{k}_s"].reshape(HB, P) for k in ("w1", "w2", "h1", "h2")]).transpose(2, 0, 1)),
        "x": c(f["L0_attn_x"].reshape(TOKENS, D).T),
        "ident": np.eye(P, dtype=np.float32),
        "attn0.wq": by_dim(w0[:, 0:D]), "attn0.wk": by_dim(w0[:, D:2 * D]), "attn0.wv": c(w0[:, 2 * D:]),
        "attn0.wo": by_group(f["L0_attn_w_proj"]),
        "attn0.cos_sin": c(np.stack([cos, sin], axis=1).astype(np.float32)),
        "attn1.wq": by_dim(pick(w1, 0)), "attn1.wk": by_dim(pick(w1, 1)), "attn1.wv": pick(w1, 2),
        "attn1.wo": by_group(c(f["L1_attn_fc_w"].T)),
        "attn1.bq": by_dim(pick(b1, 0)).reshape(D, 1), "attn1.bk": by_dim(pick(b1, 1)).reshape(D, 1),
        "attn1.bv": pick(b1, 2), "attn1.bo": f["L1_attn_fc_b"].reshape(1, D),
        "attn1.mask": c(np.tile(f["L1_attn_head_mask"], HD).reshape(D, 1)),
        "attn1.mask_v": c(np.repeat(f["L1_attn_head_mask"], HD).reshape(1, D)),
    }


def kernel(**inputs):
    import concourse.bacc as bacc
    from concourse.bass_utils import run_bass_kernel_spmd

    nc = bacc.Bacc("TRN2", target_bir_lowering=False, num_devices=1)
    arrays = {"in_" + n.replace(".", "_"): a for n, a in laid_out(inputs).items()}
    views = {}
    for name, a in laid_out(inputs).items():
        ap = nc.dram_tensor("in_" + name.replace(".", "_"), a.shape, mybir.dt.from_np(a.dtype), kind="ExternalInput").ap()
        group, _, key = name.rpartition(".")
        if group:
            views.setdefault(group, {})[key] = ap
        else:
            views[key] = ap
    out = nc.dram_tensor("out", (TOKENS, D), F32, kind="ExternalOutput").ap()
    build(nc, STAGES, views["x"], out, views)
    result = run_bass_kernel_spmd(nc, [arrays], core_ids=[0])
    return result.results[0]["out"].reshape(BATCH, SEQ, D)
```
